# Optimizing a Trainium2 kernel written in Bass

```python
import numpy as np
import jax
import jax.numpy as jnp

def _softmax(x, axis=-1):
    return jax.nn.softmax(x, axis=axis)

def _gelu(x):
    return jax.nn.gelu(x, approximate=True)

def _silu(x):
    return jax.nn.silu(x)

def _sigmoid(x):
    return jax.nn.sigmoid(x)

def _layernorm(x, axis=-1, eps=1e-05):
    m = jnp.mean(x, axis=axis, keepdims=True)
    v = jnp.var(x, axis=axis, keepdims=True)
    return (x - m) / jnp.sqrt(v + eps)

def _scatter_add(tgt, idx, src, axis=0):
    return tgt.at[idx].add(src)

def _segment_sum(src, seg, n):
    return jax.ops.segment_sum(src, seg, n)
kernel_name = 'mk_seq_postln_d4_jaxref_r8_f5fa50'

def setup_inputs(seed: int=0):
    np.random.seed(seed)
    _w = jnp.asarray

    def _L0_attn_setup():
        import jax, jax.numpy as jnp
        import numpy as np
        B, N, D = (8, 256, 128)
        key = jax.random.key(seed)
        k1, k2, k3, k4 = jax.random.split(key, 4)
        data = jax.random.normal(k1, (B, N, D), dtype=jnp.float32)
        W1 = jax.random.normal(k2, (1, D), dtype=jnp.float32) * 0.02
        b1 = jnp.zeros((D,), dtype=jnp.float32)
        W2 = jax.random.normal(k3, (2 * D, D), dtype=jnp.float32) * 0.02
        return {'data': data, 'W1': W1, 'b1': b1, 'W2': W2}
    _L0_attn_in = _L0_attn_setup()

    def _L0_ffn_setup():
        import jax, jax.numpy as jnp
        import numpy as np

        def _binarize(w):
            alpha = jax.lax.stop_gradient(jnp.mean(jnp.abs(w), axis=1, keepdims=True))
            bw = alpha * jnp.sign(w)
            return w + jax.lax.stop_gradient(bw - w)
        key = jax.random.key(seed)
        k1, k2, k3, k4, k5 = jax.random.split(key, 5)
        D, H = (128, 512)
        x = jax.random.normal(k1, (64, 196, D), dtype=jnp.float32)
        w1 = jax.random.normal(k2, (H, D), dtype=jnp.float32) * 0.02
        b1 = jax.random.normal(k3, (H,), dtype=jnp.float32) * 0.02
        w2 = jax.random.normal(k4, (D, H), dtype=jnp.float32) * 0.02
        b2 = jax.random.normal(k5, (D,), dtype=jnp.float32) * 0.02
        return {'x': x, 'w1': w1, 'b1': b1, 'w2': w2, 'b2': b2}
    _L0_ffn_in = _L0_ffn_setup()

    def _L1_attn_setup():
        import jax, jax.numpy as jnp
        import numpy as np
        B, S, D = (4, 256, 128)
        H, C = (16, 64)
        HID = H * C
        key = jax.random.key(seed)
        ks = jax.random.split(key, 9)
        scale = 0.02
        return {'x': jax.random.normal(ks[0], (B, S, D), dtype=jnp.float32), 'Wq': jax.random.normal(ks[1], (D, HID), dtype=jnp.float32) * scale, 'bq': jnp.zeros((HID,), dtype=jnp.float32), 'Wk': jax.random.normal(ks[2], (D, HID), dtype=jnp.float32) * scale, 'bk': jnp.zeros((HID,), dtype=jnp.float32), 'Wv': jax.random.normal(ks[3], (D, HID), dtype=jnp.float32) * scale, 'bv': jnp.zeros((HID,), dtype=jnp.float32), 'Wo': jax.random.normal(ks[4], (HID, D), dtype=jnp.float32) * scale, 'bo': jnp.zeros((D,), dtype=jnp.float32)}
    _L1_attn_in = _L1_attn_setup()

    def _L1_ffn_setup():
        import jax, jax.numpy as jnp
        import numpy as np
        EPS = 1e-06
        LN_EPS = 1e-05

        def _absmean_core(W):
            gamma = jnp.mean(jnp.abs(W)) + EPS
            Ws = W / gamma
            Wq = jnp.sign(Ws) * jnp.minimum(jnp.round(jnp.abs(Ws)), 1.0)
            return (Wq, gamma)

        @jax.custom_vjp
        def absmean(W):
            return _absmean_core(W)[0]

        def _absmean_fwd(W):
            Wq, gamma = _absmean_core(W)
            return (Wq, gamma)

        def _absmean_bwd(gamma, g):
            return (g / gamma,)
        absmean.defvjp(_absmean_fwd, _absmean_bwd)

        def layernorm(x, w, b, eps=LN_EPS):
            mu = jnp.mean(x, axis=-1, keepdims=True)
            var = jnp.mean((x - mu) ** 2, axis=-1, keepdims=True)
            return (x - mu) * jax.lax.rsqrt(var + eps) * w + b
        key = jax.random.key(seed)
        k1, k2, k3 = jax.random.split(key, 3)
        d, h = (128, 512)
        B, T = (8, 256)
        return {'x': jax.random.normal(k1, (B, T, d), jnp.float32), 'W_fc': jax.random.normal(k2, (h, d), jnp.float32), 'ln_w': jnp.ones((h,), jnp.float32), 'ln_b': jnp.zeros((h,), jnp.float32), 'W_proj': jax.random.normal(k3, (d, h), jnp.float32)}
    _L1_ffn_in = _L1_ffn_setup()

    def _L2_attn_setup():
        import jax, jax.numpy as jnp
        import numpy as np
        B, N, E, H = (2, 256, 128, 16)
        D = E // H
        EPS = 1e-05
        SCALE = D ** (-0.5)
        STD = 0.02
        key = jax.random.key(seed)
        ks = jax.random.split(key, 10)
        rn = lambda k, shape: jax.random.normal(k, shape, dtype=jnp.float32)
        x = rn(ks[0], (B, N, E))
        Wq = rn(ks[1], (E, E)) * STD
        Wk = rn(ks[2], (E, E)) * STD
        Wv = rn(ks[3], (E, E)) * STD
        Wo = rn(ks[4], (E, E)) * STD
        Wf1 = rn(ks[5], (E, D)) * STD
        Wf2 = rn(ks[6], (D, E)) * STD
        Wg1 = rn(ks[7], (E, D)) * STD
        Wg2 = rn(ks[8], (D, E)) * STD
        norm_weight = jnp.ones((E,), dtype=jnp.float32)
        return dict(x=x, Wq=Wq, Wk=Wk, Wv=Wv, Wo=Wo, Wf1=Wf1, Wf2=Wf2, Wg1=Wg1, Wg2=Wg2, norm_weight=norm_weight)
    _L2_attn_in = _L2_attn_setup()

    def _L2_ffn_setup():
        import jax, jax.numpy as jnp
        import numpy as np
        B, S, D, F, E = (4, 256, 128, 512, 4)
        key = jax.random.key(seed)
        ks = jax.random.split(key, 8)
        sd = 1.0 / np.sqrt(D)
        sf = 1.0 / np.sqrt(F)
        return {'x': jax.random.normal(ks[0], (B, S, D), dtype=jnp.float32), 'W1': jax.random.uniform(ks[1], (E, D, F), jnp.float32, -sd, sd), 'b1': jax.random.uniform(ks[2], (E, F), jnp.float32, -sd, sd), 'W2': jax.random.uniform(ks[3], (E, F, D), jnp.float32, -sf, sf), 'b2': jax.random.uniform(ks[4], (E, D), jnp.float32, -sf, sf), 'Wu': jax.random.uniform(ks[5], (D, 1), jnp.float32, -sd, sd), 'bu': jax.random.uniform(ks[6], (1,), jnp.float32, -sd, sd)}
    _L2_ffn_in = _L2_ffn_setup()

    def _L3_attn_setup():
        import jax, jax.numpy as jnp
        import numpy as np
        D_MODEL = 128
        D_STATE = 64
        N_HEADS = 16
        CHUNK = 64

        def segsum(x):
            T = x.shape[-1]
            xx = jnp.broadcast_to(x[..., None], x.shape + (T,))
            lower = jnp.tril(jnp.ones((T, T), dtype=bool), -1)
            xs = jnp.cumsum(jnp.where(lower, xx, 0.0), axis=-2)
            keep = jnp.tril(jnp.ones((T, T), dtype=bool), 0)
            return jnp.where(keep, xs, -jnp.inf)

        def ssd_minimal(X, A, B, C, block_len):
            b, L, h, p = X.shape
            n = B.shape[-1]
            c = L // block_len
            l = block_len
            X = X.reshape(b, c, l, h, p)
            A = A.reshape(b, c, l, h).transpose(0, 3, 1, 2)
            B = B.reshape(b, c, l, h, n)
            C = C.reshape(b, c, l, h, n)
            A_cumsum = jnp.cumsum(A, axis=-1)
            Lmat = jnp.exp(segsum(A))
            Y_diag = jnp.einsum('bclhn,bcshn,bhcls,bcshp->bclhp', C, B, Lmat, X)
            decay_states = jnp.exp(A_cumsum[:, :, :, -1:] - A_cumsum)
            states = jnp.einsum('bclhn,bhcl,bclhp->bchpn', B, decay_states, X)
            init = jnp.zeros_like(states[:, :1])
            states = jnp.concatenate([init, states], axis=1)
            A_last = A_cumsum[:, :, :, -1]
            decay_chunk = jnp.exp(segsum(jnp.pad(A_last, ((0, 0), (0, 0), (1, 0)))))
            new_states = jnp.einsum('bhzc,bchpn->bzhpn', decay_chunk, states)
            states, final_state = (new_states[:, :-1], new_states[:, -1])
            state_decay_out = jnp.exp(A_cumsum)
            Y_off = jnp.einsum('bclhn,bchpn,bhcl->bclhp', C, states, state_decay_out)
            Y = (Y_diag + Y_off).reshape(b, L, h, p)
            return (Y, final_state)

        def mamba2_forward(x, W_in, W_dt, b_dt, W_B, W_C, W_out, A_log):
            b, L, d = x.shape
            h, n = (N_HEADS, D_STATE)
            p = d // h
            xz = x @ W_in.T
            x_in, z = (xz[..., :d], xz[..., d:])
            dt = jax.nn.softplus(x @ W_dt.T + b_dt)
            A = -jnp.exp(A_log)[None, None, :] * dt
            B = (x @ W_B.T).reshape(b, L, h, n)
            C = (x @ W_C.T).reshape(b, L, h, n)
            X = x_in.reshape(b, L, h, p) * dt[..., None]
            Y, new_state = ssd_minimal(X, A, B, C, CHUNK)
            y = Y.reshape(b, L, d) * jax.nn.silu(z)
            y = y @ W_out.T
            return (y, new_state)

        def _reference_tuple_inner(x, W_in, W_dt, b_dt, W_B, W_C, W_out, A_log):
            return mamba2_forward(x, W_in, W_dt, b_dt, W_B, W_C, W_out, A_log)
        key = jax.random.key(seed)
        ks = jax.random.split(key, 7)
        d, h, n = (D_MODEL, N_HEADS, D_STATE)
        x = jax.random.normal(ks[0], (2, 512, d), dtype=jnp.float32)
        lim_in = 0.5 * np.sqrt(6.0 / (d + 2 * d))
        W_in = jax.random.uniform(ks[1], (2 * d, d), minval=-lim_in, maxval=lim_in, dtype=jnp.float32)
        lim_out = 0.5 * np.sqrt(6.0 / (d + d))
        W_out = jax.random.uniform(ks[2], (d, d), minval=-lim_out, maxval=lim_out, dtype=jnp.float32)
        lim = 1.0 / np.sqrt(d)
        W_dt = jax.random.uniform(ks[3], (h, d), minval=-lim, maxval=lim, dtype=jnp.float32)
        b_dt = jnp.zeros((h,), dtype=jnp.float32)
        W_B = jax.random.uniform(ks[4], (h * n, d), minval=-lim, maxval=lim, dtype=jnp.float32)
        W_C = jax.random.uniform(ks[5], (h * n, d), minval=-lim, maxval=lim, dtype=jnp.float32)
        A_log = jnp.log(jnp.linspace(1.0, 16.0, h)).astype(jnp.float32)
        return {'x': x, 'W_in': W_in, 'W_dt': W_dt, 'b_dt': b_dt, 'W_B': W_B, 'W_C': W_C, 'W_out': W_out, 'A_log': A_log}
    _L3_attn_in = _L3_attn_setup()

    def _L3_ffn_setup():
        import jax, jax.numpy as jnp
        import numpy as np
        D_MODEL = 128
        D1, D2 = (32, 32)
        F1, F2 = (64, 64)
        E = 64
        TOP_K = 2

        def kmoe(x_flat, W_router, A, B, scale, bias, d_in1, d_in2, d_out1, d_out2, top_k):
            logits = x_flat @ W_router.T
            vals, idx = jax.lax.top_k(logits, top_k)
            probs = jax.nn.softmax(vals, axis=-1)
            xs = x_flat.reshape(-1, d_in1, d_in2)
            Ag = A[idx]
            Bg = B[idx]
            Y = jnp.einsum('nkoi,nij,nkpj->nkop', Ag, xs, Bg)
            out = jnp.einsum('nkop,nk->nop', Y, probs).reshape(-1, d_out1 * d_out2)
            return out * scale + bias
        key = jax.random.key(seed)
        ks = jax.random.split(key, 12)
        s = 0.02
        return {'x': jax.random.normal(ks[0], (4, 256, D_MODEL), dtype=jnp.float32), 'W_up': jax.random.normal(ks[1], (E, D1 * D2), dtype=jnp.float32) * s, 'A_up': jax.random.normal(ks[2], (E, F1, D1), dtype=jnp.float32) * s, 'B_up': jax.random.normal(ks[3], (E, F2, D2), dtype=jnp.float32) * s, 'scale_up': jnp.ones((1,), dtype=jnp.float32), 'bias_up': jnp.zeros((F1 * F2,), dtype=jnp.float32), 'W_down': jax.random.normal(ks[4], (E, F1 * F2), dtype=jnp.float32) * s, 'A_down': jax.random.normal(ks[5], (E, D1, F1), dtype=jnp.float32) * s, 'B_down': jax.random.normal(ks[6], (E, D2, F2), dtype=jnp.float32) * s, 'scale_down': jnp.ones((1,), dtype=jnp.float32), 'bias_down': jnp.zeros((D1 * D2,), dtype=jnp.float32)}
    _L3_ffn_in = _L3_ffn_setup()
    _d = {'L0_attn_data': _L0_attn_in['data'], 'L0_attn_W1': _L0_attn_in['W1'], 'L0_attn_b1': _L0_attn_in['b1'], 'L0_attn_W2': _L0_attn_in['W2'], 'L0_ffn_w1': _L0_ffn_in['w1'], 'L0_ffn_b1': _L0_ffn_in['b1'], 'L0_ffn_w2': _L0_ffn_in['w2'], 'L0_ffn_b2': _L0_ffn_in['b2'], 'L1_attn_Wq': _L1_attn_in['Wq'], 'L1_attn_bq': _L1_attn_in['bq'], 'L1_attn_Wk': _L1_attn_in['Wk'], 'L1_attn_bk': _L1_attn_in['bk'], 'L1_attn_Wv': _L1_attn_in['Wv'], 'L1_attn_bv': _L1_attn_in['bv'], 'L1_attn_Wo': _L1_attn_in['Wo'], 'L1_attn_bo': _L1_attn_in['bo'], 'L1_ffn_W_fc': _L1_ffn_in['W_fc'], 'L1_ffn_ln_w': _L1_ffn_in['ln_w'], 'L1_ffn_ln_b': _L1_ffn_in['ln_b'], 'L1_ffn_W_proj': _L1_ffn_in['W_proj'], 'L2_attn_Wq': _L2_attn_in['Wq'], 'L2_attn_Wk': _L2_attn_in['Wk'], 'L2_attn_Wv': _L2_attn_in['Wv'], 'L2_attn_Wo': _L2_attn_in['Wo'], 'L2_attn_Wf1': _L2_attn_in['Wf1'], 'L2_attn_Wf2': _L2_attn_in['Wf2'], 'L2_attn_Wg1': _L2_attn_in['Wg1'], 'L2_attn_Wg2': _L2_attn_in['Wg2'], 'L2_attn_norm_weight': _L2_attn_in['norm_weight'], 'L2_ffn_W1': _L2_ffn_in['W1'], 'L2_ffn_b1': _L2_ffn_in['b1'], 'L2_ffn_W2': _L2_ffn_in['W2'], 'L2_ffn_b2': _L2_ffn_in['b2'], 'L2_ffn_Wu': _L2_ffn_in['Wu'], 'L2_ffn_bu': _L2_ffn_in['bu'], 'L3_attn_W_in': _L3_attn_in['W_in'], 'L3_attn_W_dt': _L3_attn_in['W_dt'], 'L3_attn_b_dt': _L3_attn_in['b_dt'], 'L3_attn_W_B': _L3_attn_in['W_B'], 'L3_attn_W_C': _L3_attn_in['W_C'], 'L3_attn_W_out': _L3_attn_in['W_out'], 'L3_attn_A_log': _L3_attn_in['A_log'], 'L3_ffn_W_up': _L3_ffn_in['W_up'], 'L3_ffn_A_up': _L3_ffn_in['A_up'], 'L3_ffn_B_up': _L3_ffn_in['B_up'], 'L3_ffn_scale_up': _L3_ffn_in['scale_up'], 'L3_ffn_bias_up': _L3_ffn_in['bias_up'], 'L3_ffn_W_down': _L3_ffn_in['W_down'], 'L3_ffn_A_down': _L3_ffn_in['A_down'], 'L3_ffn_B_down': _L3_ffn_in['B_down'], 'L3_ffn_scale_down': _L3_ffn_in['scale_down'], 'L3_ffn_bias_down': _L3_ffn_in['bias_down']}
    _x0 = _d['L0_attn_data']
    _d['L0_attn_data'] = jax.random.normal(jax.random.fold_in(jax.random.key(seed), 1), (4, 1024, 128), dtype=_x0.dtype)
    del _x0
    return _d

def reference(L0_attn_data, L0_attn_W1, L0_attn_b1, L0_attn_W2, L0_ffn_w1, L0_ffn_b1, L0_ffn_w2, L0_ffn_b2, L1_attn_Wq, L1_attn_bq, L1_attn_Wk, L1_attn_bk, L1_attn_Wv, L1_attn_bv, L1_attn_Wo, L1_attn_bo, L1_ffn_W_fc, L1_ffn_ln_w, L1_ffn_ln_b, L1_ffn_W_proj, L2_attn_Wq, L2_attn_Wk, L2_attn_Wv, L2_attn_Wo, L2_attn_Wf1, L2_attn_Wf2, L2_attn_Wg1, L2_attn_Wg2, L2_attn_norm_weight, L2_ffn_W1, L2_ffn_b1, L2_ffn_W2, L2_ffn_b2, L2_ffn_Wu, L2_ffn_bu, L3_attn_W_in, L3_attn_W_dt, L3_attn_b_dt, L3_attn_W_B, L3_attn_W_C, L3_attn_W_out, L3_attn_A_log, L3_ffn_W_up, L3_ffn_A_up, L3_ffn_B_up, L3_ffn_scale_up, L3_ffn_bias_up, L3_ffn_W_down, L3_ffn_A_down, L3_ffn_B_down, L3_ffn_scale_down, L3_ffn_bias_down):

    def _L0_attn_ref(data, W1, b1, W2):
        import jax, jax.numpy as jnp
        import numpy as np
        B, N, D = (8, 256, 128)
        sq = jnp.sum(data * data, axis=-1, keepdims=True)
        normed = data * jax.lax.rsqrt(jnp.maximum(sq, 1e-12))
        sim = jnp.einsum('bnd,bmd->bnm', normed, normed)
        counter = jnp.sum(jax.nn.relu(sim), axis=-1, keepdims=True)
        counter = jax.nn.softplus(counter @ W1 + b1)
        out = jnp.concatenate([data, counter], axis=-1) @ W2
        return out

    def _L0_ffn_ref(x, w1, b1, w2, b2):
        import jax, jax.numpy as jnp
        import numpy as np

        def _binarize(w):
            alpha = jax.lax.stop_gradient(jnp.mean(jnp.abs(w), axis=1, keepdims=True))
            bw = alpha * jnp.sign(w)
            return w + jax.lax.stop_gradient(bw - w)
        bw1 = _binarize(w1)
        h = jnp.einsum('bsd,hd->bsh', x, bw1) + b1
        h = jax.nn.gelu(h, approximate=False)
        bw2 = _binarize(w2)
        out = jnp.einsum('bsh,dh->bsd', h, bw2) + b2
        return out

    def _L1_attn_ref(x, Wq, bq, Wk, bk, Wv, bv, Wo, bo):
        import jax, jax.numpy as jnp
        import numpy as np
        B, S, D = (4, 256, 128)
        H, C = (16, 64)
        HID = H * C
        b, s, _ = x.shape
        inv_sqrt_c = jnp.asarray(1.0 / C ** 0.5, dtype=x.dtype)
        Q = (x @ Wq + bq).reshape(b, s, H, C) * inv_sqrt_c
        K = (x @ Wk + bk).reshape(b, s, H, C)
        V = (x @ Wv + bv).reshape(b, s, H, C)
        scores = jnp.einsum('bshq,bshk->bshqk', Q, K)
        mask = jnp.triu(jnp.ones((C, C), dtype=bool), 1)
        scores = jnp.where(mask, jnp.asarray(-jnp.inf, scores.dtype), scores)
        w = jax.nn.softmax(scores, axis=-1)
        attn = jnp.einsum('bshqk,bshk->bshq', w, V)
        attn = attn.reshape(b, s, HID)
        return attn @ Wo + bo

    def _L1_ffn_ref(x, W_fc, ln_w, ln_b, W_proj):
        import jax, jax.numpy as jnp
        import numpy as np
        EPS = 1e-06
        LN_EPS = 1e-05

        def _absmean_core(W):
            gamma = jnp.mean(jnp.abs(W)) + EPS
            Ws = W / gamma
            Wq = jnp.sign(Ws) * jnp.minimum(jnp.round(jnp.abs(Ws)), 1.0)
            return (Wq, gamma)

        @jax.custom_vjp
        def absmean(W):
            return _absmean_core(W)[0]

        def _absmean_fwd(W):
            Wq, gamma = _absmean_core(W)
            return (Wq, gamma)

        def _absmean_bwd(gamma, g):
            return (g / gamma,)
        absmean.defvjp(_absmean_fwd, _absmean_bwd)

        def layernorm(x, w, b, eps=LN_EPS):
            mu = jnp.mean(x, axis=-1, keepdims=True)
            var = jnp.mean((x - mu) ** 2, axis=-1, keepdims=True)
            return (x - mu) * jax.lax.rsqrt(var + eps) * w + b
        h = jnp.einsum('btd,hd->bth', x, absmean(W_fc))
        h = jax.nn.gelu(h, approximate=False)
        h = layernorm(h, ln_w, ln_b)
        return jnp.einsum('bth,dh->btd', h, absmean(W_proj))

    def _L2_attn_ref(x, Wq, Wk, Wv, Wo, Wf1, Wf2, Wg1, Wg2, norm_weight):
        import jax, jax.numpy as jnp
        import numpy as np
        B, N, E, H = (2, 256, 128, 16)
        D = E // H
        EPS = 1e-05
        SCALE = D ** (-0.5)
        STD = 0.02
        b, n, e = x.shape
        q = jax.nn.silu(x @ Wq).reshape(b, n, H, D)
        k = jax.nn.silu(x @ Wk).reshape(b, n, H, D)
        v = (x @ Wv).reshape(b, n, H, D)
        f = jax.nn.sigmoid(x @ Wf1 @ Wf2).reshape(b, n, H, D)

        def step(S, qkvf):
            qt, kt, vt, ft = qkvf
            S = ft[..., :, None] * S + kt[..., :, None] * vt[..., None, :]
            ot = jnp.einsum('bhk,bhkv->bhv', qt, S)
            return (S, ot)
        S0 = jnp.zeros((b, H, D, D), x.dtype)
        xs = (jnp.moveaxis(q, 1, 0) * SCALE, jnp.moveaxis(k, 1, 0), jnp.moveaxis(v, 1, 0), jnp.moveaxis(f, 1, 0))
        _, o = jax.lax.scan(step, S0, xs)
        o = jnp.moveaxis(o, 0, 1).reshape(b, n, e)
        g = jax.nn.sigmoid(x @ Wg1 @ Wg2)
        og = (o * g).reshape(b, n, H, D)
        og = og * jax.lax.rsqrt(jnp.mean(og * og, axis=-1, keepdims=True) + EPS)
        o = og.reshape(b, n, e) * norm_weight
        return o @ Wo

    def _L2_ffn_ref(x, W1, b1, W2, b2, Wu, bu):
        import jax, jax.numpy as jnp
        import numpy as np
        B, S, D, F, E = (4, 256, 128, 512, 4)
        n_exp = W1.shape[0]
        seq = x.shape[1]
        u = jax.nn.sigmoid(jnp.einsum('bsd,do->bso', x, Wu) + bu)[..., 0]
        k = jnp.clip(jnp.ceil(u * n_exp), 1, n_exp).astype(jnp.int32)
        h = jax.nn.relu(jnp.einsum('bsd,edf->bsef', x, W1) + b1)
        y = jnp.einsum('bsef,efd->bsed', h, W2) + b2
        s_idx = jnp.arange(seq)
        out = jnp.zeros_like(x)
        for i in range(1, n_exp + 1):
            e_idx = (s_idx + i - 1) % n_exp
            y_i = jnp.take_along_axis(y, e_idx[None, :, None, None], axis=2)[:, :, 0, :]
            w = jnp.where(k >= i, u / i, 0.0)
            out = out + w[..., None] * y_i
        return out

    def _L3_attn_ref(x, W_in, W_dt, b_dt, W_B, W_C, W_out, A_log):
        import jax, jax.numpy as jnp
        import numpy as np
        D_MODEL = 128
        D_STATE = 64
        N_HEADS = 16
        CHUNK = 64

        def segsum(x):
            T = x.shape[-1]
            xx = jnp.broadcast_to(x[..., None], x.shape + (T,))
            lower = jnp.tril(jnp.ones((T, T), dtype=bool), -1)
            xs = jnp.cumsum(jnp.where(lower, xx, 0.0), axis=-2)
            keep = jnp.tril(jnp.ones((T, T), dtype=bool), 0)
            return jnp.where(keep, xs, -jnp.inf)

        def ssd_minimal(X, A, B, C, block_len):
            b, L, h, p = X.shape
            n = B.shape[-1]
            c = L // block_len
            l = block_len
            X = X.reshape(b, c, l, h, p)
            A = A.reshape(b, c, l, h).transpose(0, 3, 1, 2)
            B = B.reshape(b, c, l, h, n)
            C = C.reshape(b, c, l, h, n)
            A_cumsum = jnp.cumsum(A, axis=-1)
            Lmat = jnp.exp(segsum(A))
            Y_diag = jnp.einsum('bclhn,bcshn,bhcls,bcshp->bclhp', C, B, Lmat, X)
            decay_states = jnp.exp(A_cumsum[:, :, :, -1:] - A_cumsum)
            states = jnp.einsum('bclhn,bhcl,bclhp->bchpn', B, decay_states, X)
            init = jnp.zeros_like(states[:, :1])
            states = jnp.concatenate([init, states], axis=1)
            A_last = A_cumsum[:, :, :, -1]
            decay_chunk = jnp.exp(segsum(jnp.pad(A_last, ((0, 0), (0, 0), (1, 0)))))
            new_states = jnp.einsum('bhzc,bchpn->bzhpn', decay_chunk, states)
            states, final_state = (new_states[:, :-1], new_states[:, -1])
            state_decay_out = jnp.exp(A_cumsum)
            Y_off = jnp.einsum('bclhn,bchpn,bhcl->bclhp', C, states, state_decay_out)
            Y = (Y_diag + Y_off).reshape(b, L, h, p)
            return (Y, final_state)

        def mamba2_forward(x, W_in, W_dt, b_dt, W_B, W_C, W_out, A_log):
            b, L, d = x.shape
            h, n = (N_HEADS, D_STATE)
            p = d // h
            xz = x @ W_in.T
            x_in, z = (xz[..., :d], xz[..., d:])
            dt = jax.nn.softplus(x @ W_dt.T + b_dt)
            A = -jnp.exp(A_log)[None, None, :] * dt
            B = (x @ W_B.T).reshape(b, L, h, n)
            C = (x @ W_C.T).reshape(b, L, h, n)
            X = x_in.reshape(b, L, h, p) * dt[..., None]
            Y, new_state = ssd_minimal(X, A, B, C, CHUNK)
            y = Y.reshape(b, L, d) * jax.nn.silu(z)
            y = y @ W_out.T
            return (y, new_state)

        def _reference_tuple_inner(x, W_in, W_dt, b_dt, W_B, W_C, W_out, A_log):
            return mamba2_forward(x, W_in, W_dt, b_dt, W_B, W_C, W_out, A_log)
        return _reference_tuple_inner(x, W_in, W_dt, b_dt, W_B, W_C, W_out, A_log)[0]

    def _L3_ffn_ref(x, W_up, A_up, B_up, scale_up, bias_up, W_down, A_down, B_down, scale_down, bias_down):
        import jax, jax.numpy as jnp
        import numpy as np
        D_MODEL = 128
        D1, D2 = (32, 32)
        F1, F2 = (64, 64)
        E = 64
        TOP_K = 2

        def kmoe(x_flat, W_router, A, B, scale, bias, d_in1, d_in2, d_out1, d_out2, top_k):
            logits = x_flat @ W_router.T
            vals, idx = jax.lax.top_k(logits, top_k)
            probs = jax.nn.softmax(vals, axis=-1)
            xs = x_flat.reshape(-1, d_in1, d_in2)
            Ag = A[idx]
            Bg = B[idx]
            Y = jnp.einsum('nkoi,nij,nkpj->nkop', Ag, xs, Bg)
            out = jnp.einsum('nkop,nk->nop', Y, probs).reshape(-1, d_out1 * d_out2)
            return out * scale + bias
        orig_shape = x.shape
        x_flat = x.reshape(-1, D1 * D2)
        h = kmoe(x_flat, W_up, A_up, B_up, scale_up, bias_up, D1, D2, F1, F2, TOP_K)
        h = jax.nn.gelu(h, approximate=False)
        y = kmoe(h, W_down, A_down, B_down, scale_down, bias_down, F1, F2, D1, D2, TOP_K)
        return y.reshape(*orig_shape[:-1], D_MODEL)
    x = L0_attn_data
    x = _layernorm(x + _L0_attn_ref(x, L0_attn_W1, L0_attn_b1, L0_attn_W2), axis=-1)
    x = _layernorm(x + _L0_ffn_ref(x, L0_ffn_w1, L0_ffn_b1, L0_ffn_w2, L0_ffn_b2), axis=-1)
    x = _layernorm(x + _L1_attn_ref(x, L1_attn_Wq, L1_attn_bq, L1_attn_Wk, L1_attn_bk, L1_attn_Wv, L1_attn_bv, L1_attn_Wo, L1_attn_bo), axis=-1)
    x = _layernorm(x + _L1_ffn_ref(x, L1_ffn_W_fc, L1_ffn_ln_w, L1_ffn_ln_b, L1_ffn_W_proj), axis=-1)
    x = _layernorm(x + _L2_attn_ref(x, L2_attn_Wq, L2_attn_Wk, L2_attn_Wv, L2_attn_Wo, L2_attn_Wf1, L2_attn_Wf2, L2_attn_Wg1, L2_attn_Wg2, L2_attn_norm_weight), axis=-1)
    x = _layernorm(x + _L2_ffn_ref(x, L2_ffn_W1, L2_ffn_b1, L2_ffn_W2, L2_ffn_b2, L2_ffn_Wu, L2_ffn_bu), axis=-1)
    x = _layernorm(x + _L3_attn_ref(x, L3_attn_W_in, L3_attn_W_dt, L3_attn_b_dt, L3_attn_W_B, L3_attn_W_C, L3_attn_W_out, L3_attn_A_log), axis=-1)
    x = _layernorm(x + _L3_ffn_ref(x, L3_ffn_W_up, L3_ffn_A_up, L3_ffn_B_up, L3_ffn_scale_up, L3_ffn_bias_up, L3_ffn_W_down, L3_ffn_A_down, L3_ffn_B_down, L3_ffn_scale_down, L3_ffn_bias_down), axis=-1)
    return x

_drawn_inputs = setup_inputs


def setup_inputs(seed=0):
    import zlib

    import numpy as np

    out = dict(_drawn_inputs(seed))
    spreads = {'L0_attn_b1': (0.0, 0.645),
     'L1_attn_bq': (0.0, 0.8),
     'L1_attn_bk': (0.0, 0.8),
     'L1_attn_bv': (0.0, 0.361),
     'L1_attn_bo': (0.0, 0.1),
     'L1_ffn_ln_w': (1.0, 0.2),
     'L1_ffn_ln_b': (0.0, 0.1),
     'L2_attn_norm_weight': (1.0, 0.6),
     'L3_attn_b_dt': (0.0, 0.8),
     'L3_ffn_bias_up': (0.0, 0.8),
     'L3_ffn_bias_down': (0.0, 0.1)}
    factors = {'L0_ffn_b1': 8.0,
     'L1_attn_Wq': 8.0,
     'L1_attn_Wk': 8.0,
     'L2_attn_Wf1': 8.0,
     'L2_attn_Wf2': 8.0,
     'L2_attn_Wg1': 8.0,
     'L2_attn_Wg2': 8.0,
     'L2_ffn_b1': 3.978,
     'L2_ffn_b2': 3.573,
     'L3_attn_A_log': 3.672,
     'L3_ffn_W_up': 8.0,
     'L3_ffn_A_up': 8.0,
     'L3_ffn_B_up': 8.0,
     'L3_ffn_W_down': 8.0,
     'L3_ffn_A_down': 8.0,
     'L3_ffn_B_down': 8.0}
    for name, (base, spread) in spreads.items():
        noise = np.random.default_rng([zlib.crc32(name.encode()), seed]).standard_normal(out[name].shape)
        drawn = base * np.exp(spread * noise) if base else spread * noise
        out[name] = jnp.asarray(drawn.astype(out[name].dtype))
    for name, factor in factors.items():
        out[name] = (out[name] * factor).astype(out[name].dtype)
    return out
```

```python
from contextlib import ExitStack

import concourse.bass as bass
from concourse import mybir
from concourse.alu_op_type import AluOpType as ALU

F32 = mybir.dt.float32
U32 = mybir.dt.uint32
ACT = mybir.ActivationFunctionType
AX = mybir.AxisListType
ds = bass.ds

P = 128
T = 4096
BATCH = 4
SEQ = T // BATCH
CH = 512
NCH = T // CH
BIG = 1.0e30
HALF = 4


def act_wait(act, sem, value):
    act.wait_ge(sem, value)
    act.nop(nofuse=True)


def pe_wait(pe, sem, value):
    pe.wait_ge(sem, value)
    pe.nop(nofuse=True)


class Core:

    def __init__(self, nc, ctx):
        self.nc, self.ctx = nc, ctx
        self.arena = ctx.enter_context(nc.sbuf_tensor("arena", [P, 53200], F32))
        self.psum = ctx.enter_context(nc.psum_tensor("psum", [P, 8 * 512], F32))
        self.bank = [self.psum[:, 512 * i:512 * i + 512] for i in range(8)]
        self.X = self.arena[:, 0:T]
        self.Y = self.arena[:, T:2 * T]
        at = 2 * T
        self.ident = self.arena[:, at:at + P]
        self.ones = self.arena[:, at + P:at + 2 * P]
        self.mean = self.arena[:, at + 2 * P:at + 3 * P]
        self.eps5 = self.arena[:, at + 3 * P:at + 3 * P + 1]
        at += 3 * P + 4
        self.norm_at = at
        self.free_at = at + 4096
        self.used = []
        self.s_meet = self.sem("s_meet")
        self.s_cleared = self.sem("s_cleared")
        self.s_const = self.sem("s_const")
        self.s_ident = self.sem("s_ident")
        self.s_ones = self.sem("s_ones")
        self.s_x = self.sem("s_x")
        self.s_xload = self.sem("s_xload")
        self.s_out = self.sem("s_out")

    def sem(self, name):
        return self.ctx.enter_context(self.nc.semaphore(name))

    def layer_sems(self, layer):
        if layer == HALF:
            self.spare = list(self.used)
        def take(name):
            if layer >= HALF and self.spare:
                return self.spare.pop()
            s = self.sem(name)
            if layer < HALF:
                self.used.append(s)
            return s
        return take

    def half_way(self, eng, clears=False):
        eng.sem_inc(self.s_meet, 1)
        eng.wait_ge(self.s_meet, 5)
        if clears:
            for s in self.used:
                eng.sem_clear(s)
            eng.sem_inc(self.s_cleared, 1)
        eng.wait_ge(self.s_cleared, 1)

    def cut(self, at, *shape):
        n = 1
        for d in shape:
            n *= d
        v = self.arena[:, at:at + n]
        if len(shape) == 2:
            v = v.rearrange("p (a b) -> p a b", a=shape[0])
        if len(shape) == 3:
            v = v.rearrange("p (a b c) -> p a b c", a=shape[0], b=shape[1])
        return v


class Places:

    def __init__(self, core, at):
        self.core, self.at = core, at

    def __call__(self, *shape):
        n = 1
        for d in shape:
            n *= d
        v = self.core.cut(self.at, *shape)
        self.at += n
        assert self.at <= 53200, self.at
        return v


def layer_norm(c, y_done):
    place = Places(c, c.norm_at)
    xc = [place(CH) for _ in range(2)]
    sq = [place(CH) for _ in range(2)]
    sd = [place(CH) for _ in range(2)]
    rs = [place(CH) for _ in range(2)]
    ps_mean, ps_var = c.bank[0:2], c.bank[2:4]
    s_mean = [c.sem(f"ln_mean{u}") for u in range(2)]
    s_xc = [c.sem(f"ln_xc{u}") for u in range(2)]
    s_sq = [c.sem(f"ln_sq{u}") for u in range(2)]
    s_var = [c.sem(f"ln_var{u}") for u in range(2)]
    s_sd = [c.sem(f"ln_sd{u}") for u in range(2)]
    s_rs = [c.sem(f"ln_rs{u}") for u in range(2)]
    ROUNDS = NCH // 2

    def col(i, u):
        return ds(i * (2 * CH) + (u * CH - 2 * CH), CH)

    def tensor(pe, layer):
        base = ROUNDS * layer
        pe.wait_ge(*y_done(layer))
        with pe.Fori(1, ROUNDS + 1) as i:
            for u in range(2):
                pe.matmul(ps_mean[u][:, :], c.mean, c.Y[:, col(i, u)], start=True, stop=True).then_inc(s_mean[u], 1)
            for u in range(2):
                pe.wait_ge(s_sq[u], i + base)
                pe.matmul(ps_var[u][:, :], c.mean, sq[u], start=True, stop=True).then_inc(s_var[u], 1)

    def vector(dve, layer):
        base = ROUNDS * layer
        dve.wait_ge(*y_done(layer))
        with dve.Fori(1, ROUNDS + 1) as i:
            for u in range(2):
                dve.wait_ge(s_mean[u], i + base)
                dve.tensor_tensor(xc[u], c.Y[:, col(i, u)], ps_mean[u][:, :], ALU.subtract).then_inc(s_xc[u], 1)
            for u in range(2):
                dve.wait_ge(s_sd[u], i + base)
                dve.reciprocal(rs[u], sd[u]).then_inc(s_rs[u], 1)
                dve.wait_ge(s_rs[u], i + base)
                dve.tensor_tensor(c.X[:, col(i, u)], xc[u], rs[u], ALU.mult).then_inc(c.s_x, 1)
            dve.wait_ge(c.s_x, i * 2 + NCH * layer)

    def scalar(act, layer):
        base = ROUNDS * layer
        with act.Fori(1, ROUNDS + 1) as i:
            for u in range(2):
                act_wait(act, s_xc[u], i + base)
                act.activation(sq[u], xc[u], ACT.Square).then_inc(s_sq[u], 1)
            for u in range(2):
                act_wait(act, s_var[u], i + base)
                act.activation(sd[u], ps_var[u][:, :], ACT.Sqrt, bias=c.eps5).then_inc(s_sd[u], 1)

    return tensor, vector, scalar


def x_ready(c, layer):
    return (c.s_x, NCH * layer) if layer else (c.s_xload, 16)


def similarity_layer(c, d, layer):
    place = Places(c, c.free_at)
    N = place(T)
    W2a, W2b = place(P), place(P)
    W1r = place(P)
    b1 = place(1)
    sq = [place(CH) for _ in range(2)]
    mx = [place(CH) for _ in range(2)]
    sd = [place(CH) for _ in range(2)]
    rs = [place(CH) for _ in range(2)]
    nt = [place(P) for _ in range(2)]
    relu = [place(SEQ) for _ in range(2)]
    cnt = [place(1) for _ in range(2)]
    dg = [place(P) for _ in range(2)]
    xs = [place(CH) for _ in range(2)]
    z = [place(CH) for _ in range(2)]
    az = [place(CH) for _ in range(2)]
    ez = [place(CH) for _ in range(2)]
    lz = [place(CH) for _ in range(2)]
    sp = [place(CH) for _ in range(2)]
    ps_sq = c.bank[0:2]
    ps_sim = [c.bank[0:2], c.bank[2:4]]
    ps_z = c.bank[4:6]
    ps_o = c.bank[6:8]
    take = c.layer_sems(layer)
    S = lambda n: take("sim_" + n)
    s_w, s_sq, s_ss, s_mx, s_sd, s_rs, s_n = S("w"), S("sq"), S("ss"), S("mx"), S("sd"), S("rs"), S("n")
    s_nt, s_sim, s_cnt, s_dg, s_z, s_zb, s_r = S("nt"), S("sim"), S("cnt"), S("dg"), S("z"), S("zb"), S("r")
    s_az, s_ez, s_lz, s_sp, s_o, s_y = S("az"), S("ez"), S("lz"), S("sp"), S("o"), S("y")
    TPB = SEQ // P
    TPC = CH // P

    def sync(sp_):
        sp_.dma_start(W2a, d["L0_attn_W2"][0:P, :]).then_inc(s_w, 16)
        sp_.dma_start(W2b, d["L0_attn_W2"][P:2 * P, :]).then_inc(s_w, 16)
        sp_.dma_start(W1r, d["W1_rows"]).then_inc(s_w, 16)
        sp_.dma_start(b1, d["L0_attn_b1"]).then_inc(s_w, 16)

    def tensor(pe):
        pe.wait_ge(s_w, 64)
        with pe.Fori(1, NCH // 2 + 1) as i:
            for u in range(2):
                pe.wait_ge(s_sq, i * 2 + (u - 1))
                pe.matmul(ps_sq[u][:, :], c.ones, sq[u], start=True, stop=True).then_inc(s_ss, 1)
        pe.wait_ge(s_n, NCH)
        with pe.Fori(1, BATCH + 1) as b:
            def project(h):
                pe.wait_ge(s_sp, b * 2 + (h - 1))
                pe.matmul(ps_o[h][:, :], W2a, xs[h], start=True, stop=False)
                pe.matmul(ps_o[h][:, :], W2b, sp[h], start=False, stop=True).then_inc(s_o, 1)
            for r in range(TPB):
                u, h, j = r % 2, r // TPC, r % TPC
                pe.wait_ge(s_nt, b * TPB + (r + 1 - TPB))
                for half in range(2):
                    mm = pe.matmul(ps_sim[u][half][:, :], nt[u], N[:, ds(b * SEQ + (half * CH - SEQ), CH)],
                                   start=True, stop=True)
                mm.then_inc(s_sim, 1)
                if r:
                    uu, hh, jj = (r - 1) % 2, (r - 1) // TPC, (r - 1) % TPC
                    pe.wait_ge(s_dg, b * TPB + (r - TPB))
                    pe.matmul(ps_z[hh][:, jj * P:jj * P + P], W1r, dg[uu], start=True, stop=True).then_inc(s_z, 1)
                if r == TPC + 1:
                    project(0)
            pe.wait_ge(s_dg, b * TPB)
            pe.matmul(ps_z[1][:, CH - P:CH], W1r, dg[1], start=True, stop=True).then_inc(s_z, 1)
            project(1)

    def vector(dve):
        dve.wait_ge(*x_ready(c, layer))
        with dve.Fori(1, NCH // 2 + 1) as i:
            for u in range(2):
                dve.tensor_tensor(sq[u], c.X[:, ds(i * (2 * CH) + (u - 2) * CH, CH)],
                                  c.X[:, ds(i * (2 * CH) + (u - 2) * CH, CH)], ALU.mult).then_inc(s_sq, 1)
            for u in range(2):
                dve.wait_ge(s_ss, i * 2 + (u - 1))
                dve.tensor_scalar(mx[u], ps_sq[u][:, :], 1e-12, None, ALU.max).then_inc(s_mx, 1)
            for u in range(2):
                dve.wait_ge(s_sd, i * 2 + (u - 1))
                dve.reciprocal(rs[u], sd[u]).then_inc(s_rs, 1)
                dve.wait_ge(s_rs, i * 2 + (u - 1))
                dve.tensor_tensor(N[:, ds(i * (2 * CH) + (u - 2) * CH, CH)], c.X[:, ds(i * (2 * CH) + (u - 2) * CH, CH)],
                                  rs[u], ALU.mult).then_inc(s_n, 1)
            dve.wait_ge(s_n, i * 2)
        dve.wait_ge(s_n, NCH)
        with dve.Fori(1, BATCH + 1) as b:
            def chunk_x(h):
                dve.tensor_copy(xs[h], c.X[:, ds(b * SEQ + (h * CH - SEQ), CH)]).then_inc(s_r, 1)

            def load_tile(r):
                dve.tensor_copy(nt[r % 2], N[:, ds(b * SEQ + (r * P - SEQ), P)]).then_inc(s_nt, 1)

            def softplus(h):
                dve.wait_ge(s_zb, b * 2 + (h - 1))
                dve.tensor_scalar(az[h], z[h], 0.0, None, ALU.max).then_inc(s_az, 1)
                dve.wait_ge(s_lz, b * 2 + (h - 1))
                dve.wait_ge(s_r, b * 2 + (h - 1))
                dve.wait_ge(s_az, b * 2 + (h - 1))
                dve.tensor_tensor(sp[h], az[h], lz[h], ALU.add).then_inc(s_sp, 1)

            def finish(h):
                dve.wait_ge(s_o, b * 2 + (h - 1))
                dve.tensor_tensor(c.Y[:, ds(b * SEQ + (h * CH - SEQ), CH)], xs[h], ps_o[h][:, :], ALU.add).then_inc(s_y, 1)
            chunk_x(0)
            chunk_x(1)
            load_tile(0)
            load_tile(1)
            for r in range(TPB):
                dve.wait_ge(s_cnt, b * TPB + (r + 1 - TPB))
                dve.tensor_scalar(dg[r % 2], c.ident, cnt[r % 2], None, ALU.mult).then_inc(s_dg, 1)
                if r + 2 < TPB:
                    load_tile(r + 2)
                if r == TPC:
                    softplus(0)
            softplus(1)
            finish(0)
            finish(1)
            dve.wait_ge(s_y, b * 2)

    def scalar(act):
        with act.Fori(1, NCH // 2 + 1) as i:
            for u in range(2):
                act_wait(act, s_mx, i * 2 + (u - 1))
                act.activation(sd[u], mx[u], ACT.Sqrt).then_inc(s_sd, 1)
        with act.Fori(1, BATCH + 1) as b:
            def softplus(h):
                act_wait(act, s_z, b * TPB + (h + 1) * TPC - TPB)
                act.activation(z[h], ps_z[h][:, :], ACT.Identity, bias=b1).then_inc(s_zb, 1)
                act_wait(act, s_zb, b * 2 + (h - 1))
                act.activation(ez[h], z[h], ACT.Abs).then_inc(s_ez, 1)
                act_wait(act, s_ez, b * 4 + (2 * h - 3))
                act.activation(ez[h], ez[h], ACT.Exp, scale=-1.0).then_inc(s_ez, 1)
                act_wait(act, s_ez, b * 4 + (2 * h - 2))
                act.activation(lz[h], ez[h], ACT.Ln, bias=1.0).then_inc(s_lz, 1)
            for r in range(TPB):
                act_wait(act, s_sim, b * TPB + (r + 1 - TPB))
                act.activation(relu[r % 2], c.psum[:, (r % 2) * SEQ:(r % 2) * SEQ + SEQ], ACT.Relu, accum_out=cnt[r % 2]).then_inc(s_cnt, 1)
                if r == TPC:
                    softplus(0)
            softplus(1)

    return dict(sync=sync, tensor=tensor, vector=vector, scalar=scalar, done=(s_y, NCH))


def binary_ffn_layer(c, d, layer):
    HC = 4
    place = Places(c, c.free_at)
    w1, w2 = place(HC, P), place(HC * P)
    s1, s2 = place(HC, P), place(HC * P)
    al1, al2 = place(HC), place(1)
    w1T, w2T = place(HC, P), place(HC, P)
    b1, b2 = place(HC), place(1)
    g = [[place(CH) for _ in range(HC)] for _ in range(2)]
    xs = [place(CH) for _ in range(2)]
    ps_t = c.bank[6:8]
    ps_h = c.bank[0:4]
    ps_o = c.bank[4:6]
    take = c.layer_sems(layer)
    S = lambda n: take("bin_" + n)
    s_w, s_sg, s_b, s_t, s_tc, s_h, s_g, s_o, s_y = [S(n) for n in ("w", "sg", "b", "t", "tc", "h", "g", "o", "y")]

    def sync(sp):
        sp.wait_ge(*x_ready(c, layer - 1 if layer else 0))
        sp.wait_ge(*x_ready(c, layer))
        sp.dma_start(w1, d["L0_ffn_w1"].rearrange("(c p) d -> p c d", p=P)).then_inc(s_w, 16)
        sp.dma_start(w2, d["L0_ffn_w2"]).then_inc(s_w, 16)
        sp.dma_start(b1, d["L0_ffn_b1"]).then_inc(s_w, 16)
        sp.dma_start(b2, d["L0_ffn_b2"]).then_inc(s_w, 16)

    def vector(dve):
        dve.wait_ge(*x_ready(c, layer))
        dve.wait_ge(s_w, 64)
        dve.tensor_reduce(al1, w1, AX.X, ALU.add, apply_absolute_value=True).then_inc(s_b, 1)
        dve.tensor_reduce(al2, w2, AX.X, ALU.add, apply_absolute_value=True).then_inc(s_b, 1)
        dve.wait_ge(s_b, 2)
        dve.tensor_scalar(al1, al1, 1.0 / P, None, ALU.mult).then_inc(s_b, 1)
        dve.tensor_scalar(al2, al2, 1.0 / (HC * P), None, ALU.mult).then_inc(s_b, 1)
        dve.wait_ge(s_b, 4)
        dve.wait_ge(s_sg, 2)
        for k in range(HC):
            dve.scalar_tensor_tensor(s1[:, k, :], s1[:, k, :], al1[:, k:k + 1], w1[:, k, :],
                                     ALU.mult, ALU.subtract).then_inc(s_b, 1)
        dve.scalar_tensor_tensor(s2, s2, al2, w2, ALU.mult, ALU.subtract).then_inc(s_b, 1)
        dve.wait_ge(s_b, 5 + HC)
        dve.tensor_tensor(s1, s1, w1, ALU.add).then_inc(s_b, 1)
        dve.tensor_tensor(s2, s2, w2, ALU.add).then_inc(s_b, 1)
        dve.wait_ge(s_t, 1)
        dve.tensor_copy(w1T.rearrange("p c n -> p (c n)"), ps_t[0]).then_inc(s_tc, 1)
        dve.wait_ge(s_t, 2)
        dve.tensor_copy(w2T.rearrange("p c n -> p (c n)"), ps_t[1]).then_inc(s_tc, 1)
        with dve.Fori(1, NCH // 2 + 1) as i:
            for u in range(2):
                dve.wait_ge(s_o, i * 2 + (u - 1))
                dve.scalar_tensor_tensor(c.Y[:, ds(i * (2 * CH) + (u - 2) * CH, CH)], ps_o[u], b2,
                                         c.X[:, ds(i * (2 * CH) + (u - 2) * CH, CH)], ALU.add, ALU.add).then_inc(s_y, 1)
            dve.wait_ge(s_y, i * 2)

    def scalar(act):
        act.wait_ge(s_w, 64)
        act.activation(s1, w1, ACT.Sign).then_inc(s_sg, 1)
        act.activation(s2, w2, ACT.Sign).then_inc(s_sg, 1)
        with act.Fori(1, NCH // 2 + 1) as i:
            for u in range(2):
                for k in range(HC):
                    act_wait(act, s_h, i * (2 * HC) + (u * HC + k + 1 - 2 * HC))
                    act.activation(g[u][k], ps_h[k], ACT.Gelu, bias=b1[:, k:k + 1]).then_inc(s_g, 1)

    def tensor(pe):
        pe.wait_ge(s_b, 7 + HC)
        pe.wait_ge(c.s_ident, 1)
        for k in range(HC):
            mm = pe.transpose(ps_t[0][:, k * P:k * P + P], s1[:, k, :], c.ident)
        mm.then_inc(s_t, 1)
        for k in range(HC):
            mm = pe.transpose(ps_t[1][:, k * P:k * P + P], s2[:, k * P:k * P + P], c.ident)
        mm.then_inc(s_t, 1)
        pe.wait_ge(s_tc, 2)

        def down(i, u):
            for k in range(HC):
                pe.wait_ge(s_g, i * (2 * HC) + (u * HC + k + 1 - 2 * HC))
                mm = pe.matmul(ps_o[u], w2T[:, k, :], g[u][k], start=(k == 0), stop=(k == HC - 1))
            mm.then_inc(s_o, 1)
        with pe.Fori(1, NCH // 2 + 1) as i:
            for u in range(2):
                for k in range(HC):
                    pe.matmul(ps_h[k], w1T[:, k, :], c.X[:, ds(i * (2 * CH) + (u - 2) * CH, CH)],
                              start=True, stop=True).then_inc(s_h, 1)
                down(i, u)
            pe.wait_ge(s_y, i * 2)

    return dict(sync=sync, tensor=tensor, vector=vector, scalar=scalar, done=(s_y, NCH))


def ternary_ffn_layer(c, d, layer):
    HC = 4
    place = Places(c, c.free_at)
    w1, w2 = place(HC, P), place(HC * P)
    q1, q2 = place(HC, P), place(HC * P)
    n1, n2 = place(HC, P), place(HC * P)
    ga = place(4)
    gm, rg = place(2), place(2)
    w1T, w2T, w2s = place(HC, P), place(HC, P), place(HC, P)
    lnw, lnb = place(HC), place(HC)
    wb = place(1)
    meanh = place(P)
    g = [place(CH) for _ in range(HC)]
    gc = [[place(CH) for _ in range(HC)] for _ in range(2)]
    sq = [place(CH) for _ in range(HC)]
    sd, rs, tmp = place(CH), place(CH), place(CH)
    ps_h = c.bank[0:4]
    ps_mu, ps_var, ps_o, ps_t = c.bank[4], c.bank[5], c.bank[6], c.bank[7]
    take = c.layer_sems(layer)
    S = lambda n: take("ter_" + n)
    s_w, s_a, s_gs, s_q, s_t, s_tc, s_h, s_g, s_mu, s_gc, s_sq, s_var, s_sd, s_o, s_rs, s_y = [S(n) for n in (
        "w", "a", "gs", "q", "t", "tc", "h", "g", "mu", "gc", "sq", "var", "sd", "o", "rs", "y")]

    def sync(sp):
        sp.wait_ge(*x_ready(c, layer))
        sp.dma_start(w1, d["L1_ffn_W_fc"].rearrange("(c p) d -> p c d", p=P)).then_inc(s_w, 16)
        sp.dma_start(w2, d["L1_ffn_W_proj"]).then_inc(s_w, 16)
        sp.dma_start(lnw, d["L1_ffn_ln_w"]).then_inc(s_w, 16)
        sp.dma_start(lnb, d["L1_ffn_ln_b"]).then_inc(s_w, 16)

    def vector(dve):
        dve.wait_ge(*x_ready(c, layer))
        dve.memset(meanh, 1.0 / (HC * P)).then_inc(s_a, 1)
        dve.wait_ge(s_w, 64)
        dve.tensor_reduce(ga[:, 0:1], w1, AX.XY, ALU.add, apply_absolute_value=True).then_inc(s_a, 1)
        dve.tensor_reduce(ga[:, 1:2], w2, AX.X, ALU.add, apply_absolute_value=True).then_inc(s_a, 1)
        dve.wait_ge(s_gs, 1)
        dve.tensor_scalar(gm, ps_t[:, 0:2], 1.0 / (HC * P * P), 1e-6, ALU.mult, ALU.add).then_inc(s_q, 1)
        dve.wait_ge(s_q, 1)
        dve.reciprocal(rg, gm).then_inc(s_q, 1)
        dve.wait_ge(s_q, 2)
        dve.tensor_scalar(n1, w1, rg[:, 0:1], -0.5, ALU.mult, ALU.is_lt).then_inc(s_q, 1)
        dve.tensor_scalar(n2, w2, rg[:, 1:2], -0.5, ALU.mult, ALU.is_lt).then_inc(s_q, 1)
        dve.tensor_scalar(q1, w1, rg[:, 0:1], 0.5, ALU.mult, ALU.is_gt).then_inc(s_q, 1)
        dve.tensor_scalar(q2, w2, rg[:, 1:2], 0.5, ALU.mult, ALU.is_gt).then_inc(s_q, 1)
        dve.wait_ge(s_q, 6)
        dve.tensor_tensor(q1, q1, n1, ALU.subtract).then_inc(s_q, 1)
        dve.tensor_tensor(q2, q2, n2, ALU.subtract).then_inc(s_q, 1)
        dve.wait_ge(s_t, 1)
        dve.tensor_copy(w1T.rearrange("p c n -> p (c n)"), ps_h[0]).then_inc(s_tc, 1)
        dve.tensor_copy(w2T.rearrange("p c n -> p (c n)"), ps_h[1]).then_inc(s_tc, 1)
        dve.wait_ge(s_tc, 2)
        for k in range(HC):
            dve.tensor_scalar(w2s[:, k, :], w2T[:, k, :], lnw[:, k:k + 1], None, ALU.mult).then_inc(s_tc, 1)
        dve.wait_ge(s_t, 2)
        dve.tensor_copy(wb, ps_t[:, 4:5]).then_inc(s_tc, 1)
        dve.wait_ge(s_tc, 3 + HC)
        with dve.Fori(1, NCH + 1) as i:
            dve.wait_ge(s_mu, i)
            for k in range(HC):
                dve.tensor_tensor(gc[0][k], g[k], ps_mu, ALU.subtract).then_inc(s_gc, 1)
            dve.wait_ge(s_sd, i)
            dve.reciprocal(rs, sd).then_inc(s_rs, 1)
            dve.wait_ge(s_rs, i)
            dve.wait_ge(s_o, i)
            dve.tensor_tensor(tmp, ps_o, rs, ALU.mult).then_inc(s_tmp, 1)
            dve.wait_ge(s_tmp, i)
            dve.scalar_tensor_tensor(c.Y[:, ds(i * CH - CH, CH)], tmp, wb, c.X[:, ds(i * CH - CH, CH)],
                                     ALU.add, ALU.add).then_inc(s_y, 1)
            dve.wait_ge(s_y, i)

    s_tmp = S("tmp")

    def scalar(act):
        with act.Fori(1, NCH + 1) as i:
            for k in range(HC):
                act_wait(act, s_h, i * HC + (k + 1 - HC))
                act.activation(g[k], ps_h[k], ACT.Gelu).then_inc(s_g, 1)
            for k in range(HC):
                act_wait(act, s_gc, i * HC + (k + 1 - HC))
                act.activation(sq[k], gc[0][k], ACT.Square).then_inc(s_sq, 1)
            act_wait(act, s_var, i)
            act.activation(sd, ps_var, ACT.Sqrt, bias=c.eps5).then_inc(s_sd, 1)

    def tensor(pe):
        pe.wait_ge(s_a, 3)
        pe.matmul(ps_t[:, 0:2], c.ones, ga[:, 0:2], start=True, stop=True).then_inc(s_gs, 1)
        pe.wait_ge(s_q, 8)
        for k in range(HC):
            pe.transpose(ps_h[0][:, k * P:k * P + P], q1[:, k, :], c.ident)
        for k in range(HC):
            mm = pe.transpose(ps_h[1][:, k * P:k * P + P], q2[:, k * P:k * P + P], c.ident)
        mm.then_inc(s_t, 1)
        pe.wait_ge(s_tc, 2)
        for k in range(HC):
            mm = pe.matmul(ps_t[:, 4:5], w2T[:, k, :], lnb[:, k:k + 1], start=(k == 0), stop=(k == HC - 1))
        mm.then_inc(s_t, 1)
        pe.wait_ge(s_tc, 3 + HC)
        with pe.Fori(1, NCH + 1) as i:
            for k in range(HC):
                pe.matmul(ps_h[k], w1T[:, k, :], c.X[:, ds(i * CH - CH, CH)], start=True, stop=True).then_inc(s_h, 1)
            for k in range(HC):
                pe.wait_ge(s_g, i * HC + (k + 1 - HC))
                mm = pe.matmul(ps_mu, meanh, g[k], start=(k == 0), stop=(k == HC - 1))
            mm.then_inc(s_mu, 1)
            for k in range(HC):
                pe.wait_ge(s_gc, i * HC + (k + 1 - HC))
                mm = pe.matmul(ps_o, w2s[:, k, :], gc[0][k], start=(k == 0), stop=(k == HC - 1))
            mm.then_inc(s_o, 1)
            for k in range(HC):
                pe.wait_ge(s_sq, i * HC + (k + 1 - HC))
                mm = pe.matmul(ps_var, meanh, sq[k], start=(k == 0), stop=(k == HC - 1))
            mm.then_inc(s_var, 1)

    return dict(sync=sync, tensor=tensor, vector=vector, scalar=scalar, done=(s_y, NCH))


def expert_ffn_layer(c, d, layer):
    E, HC = 4, 4
    place = Places(c, c.free_at)
    w1 = place(E, HC * P)
    w2 = place(E * HC, P)
    b1, b2 = place(E * HC), place(E)
    wu, bu = place(1), place(1)
    wur = place(P)
    h = [place(CH) for _ in range(8)]
    u_ = place(CH)
    ui = place(E, CH)
    we = [place(E, CH) for _ in range(2)]
    ye = [place(CH) for _ in range(2)]
    acc = place(CH)
    ps_h = c.bank[0:4]
    ps_o = c.bank[4:6]
    ps_u = c.bank[6]
    take = c.layer_sems(layer)
    S = lambda n: take("exp_" + n)
    s_w, s_wu, s_u, s_us, s_ui, s_we, s_h, s_r, s_o, s_ye, s_ac, s_y = [S(n) for n in (
        "w", "wu", "u", "us", "ui", "we", "h", "r", "o", "ye", "ac", "y")]

    def sync(sp):
        sp.wait_ge(*x_ready(c, layer))
        sp.dma_start(w1, d["L2_ffn_W1"].rearrange("e p f -> p e f")).then_inc(s_w, 16)
        sp.dma_start(w2, d["L2_ffn_W2"].rearrange("e (c p) n -> p (e c) n", p=P)).then_inc(s_w, 16)
        sp.dma_start(b1, d["L2_ffn_b1"]).then_inc(s_w, 16)
        sp.dma_start(b2, d["L2_ffn_b2"]).then_inc(s_w, 16)
        sp.dma_start(wu, d["L2_ffn_Wu"]).then_inc(s_w, 16)
        sp.dma_start(bu, d["L2_ffn_bu"]).then_inc(s_w, 16)

    def vector(dve):
        dve.wait_ge(*x_ready(c, layer))
        dve.wait_ge(s_w, 96)
        dve.tensor_scalar(wur, c.ones, wu, None, ALU.mult).then_inc(s_wu, 1)
        with dve.Fori(1, NCH + 1) as i:
            dve.wait_ge(s_us, i)
            for r in range(E):
                dve.tensor_scalar(ui[:, r, :], u_, 1.0 / (r + 1), None, ALU.mult).then_inc(s_ui, 1)
            dve.wait_ge(s_ui, i * E)
            for pos in range(E):
                for r in range(E):
                    e = (pos + r) % E
                    mm = dve.scalar_tensor_tensor(we[0][:, e, pos::E], u_[:, pos::E], r / E if r else -1.0,
                                                  ui[:, r, pos::E], ALU.is_gt, ALU.mult)
            mm.then_inc(s_we, 1)
            dve.wait_ge(s_we, i)
            for e in range(E):
                dve.wait_ge(s_o, i * E + (e + 1 - E))
                out = acc if e == 0 else ye[e % 2]
                dve.scalar_tensor_tensor(out, ps_o[e % 2], b2[:, e:e + 1], we[0][:, e, :],
                                         ALU.add, ALU.mult).then_inc(s_ye, 1)
                dve.wait_ge(s_ye, i * E + (e + 1 - E))
                if e:
                    dve.tensor_tensor(acc, acc, ye[e % 2], ALU.add).then_inc(s_ac, 1)
                    dve.wait_ge(s_ac, i * (E - 1) + (e + 1 - E))
            dve.tensor_tensor(c.Y[:, ds(i * CH - CH, CH)], acc, c.X[:, ds(i * CH - CH, CH)], ALU.add).then_inc(s_y, 1)
            dve.wait_ge(s_y, i)

    def scalar(act):
        with act.Fori(1, NCH + 1) as i:
            act_wait(act, s_u, i)
            act.activation(u_, ps_u, ACT.Sigmoid, bias=bu).then_inc(s_us, 1)
            for n in range(E * HC):
                act_wait(act, s_h, i * (E * HC) + (n + 1 - E * HC))
                act.activation(h[n % 8], ps_h[n % 4], ACT.Relu, bias=b1[:, n:n + 1]).then_inc(s_r, 1)

    def tensor(pe):
        pe.wait_ge(s_wu, 1)
        with pe.Fori(1, NCH + 1) as i:
            if True:
                pe.matmul(ps_u, wur, c.X[:, ds(i * CH - CH, CH)], start=True, stop=True).then_inc(s_u, 1)

            def up(e):
                for k in range(HC):
                    n = e * HC + k
                    pe.matmul(ps_h[n % 4], w1[:, e, k * P:k * P + P], c.X[:, ds(i * CH - CH, CH)],
                              start=True, stop=True).then_inc(s_h, 1)

            def down(e):
                for k in range(HC):
                    n = e * HC + k
                    pe.wait_ge(s_r, i * (E * HC) + (n + 1 - E * HC))
                    if k == 0 and e >= 2:
                        pe.wait_ge(s_ye, i * E + (e - 1 - E))
                    mm = pe.matmul(ps_o[e % 2], w2[:, n, :], h[n % 8], start=(k == 0), stop=(k == HC - 1))
                mm.then_inc(s_o, 1)
            for e in range(E):
                up(e)
                down(e)
            pe.wait_ge(s_ye, i * E)

    return dict(sync=sync, tensor=tensor, vector=vector, scalar=scalar, done=(s_y, NCH))


def outer_attention_layer(c, d, layer):
    H, C, Q = 16, 64, 8
    HC = H * C
    NB = C // Q
    NT = T // P
    order = list(range(NB - 1, -1, -1))
    width = [Q * (b + 1) for b in range(NB)]
    place = Places(c, c.norm_at)
    slots = [place(H * Q * width[NB - 1 - s]) for s in range(4)]
    wqkv = place(3, HC)
    wo = place(HC // P, P)
    bias = place(HC)
    kqv = [place(3, HC) for _ in range(2)]
    cmax = [place(HC) for _ in range(2)]
    cmin = place(HC)
    xt = [place(P) for _ in range(2)]
    den = place(HC)
    attT = place(HC // P, P)
    resets = place(HC)
    bo = place(1)
    rmax = resets[:, 0:HC // 2].bitcast(mybir.dt.bfloat16)
    rmin = resets[:, HC // 2:HC].bitcast(mybir.dt.bfloat16)
    ps_p = c.bank[0:2]
    ps_n = c.psum[:, 2 * 512:4 * 512]
    ps_t = c.psum[:, 4 * 512:6 * 512]
    ps_o = c.bank[6][:, 0:P]
    take = c.layer_sems(layer)
    S = lambda n: take("att_" + n)
    (s_w, s_rst, s_xt, s_pj, s_kqv, s_cm, s_m, s_s, s_sub, s_e, s_d, s_pv, s_r, s_rd, s_at, s_tr, s_trc, s_wo, s_y,
     s_mx) = [S(n) for n in ("w", "rst", "xt", "pj", "kqv", "cm", "m", "s", "sub", "e", "d", "pv", "r", "rd", "at",
                             "tr", "trc", "wo", "y", "mx")]
    K_, Q_, V_ = 0, 1, 2
    SLOTS = 4

    def scores(k):
        w = width[order[k]]
        return slots[k % SLOTS][:, 0:H * Q * w].rearrange("p (h q k) -> p h q k", h=H, q=Q)

    def heads(v):
        return v.rearrange("p (h c) -> p h c", h=H)

    def over_keys(v, k):
        b, w = order[k], width[order[k]]
        return heads(v)[:, :, b * Q:b * Q + Q].unsqueeze(3).to_broadcast([P, H, Q, w])

    def over_queries(v, k):
        return heads(v)[:, :, 0:width[order[k]]].unsqueeze(2).to_broadcast([P, H, Q, width[order[k]]])

    def tile(i, u):
        return i * 2 + (u - 2)

    def sync(sp):
        sp.wait_ge(*x_ready(c, layer))
        for n, (w, b) in enumerate((("Wk", "bk"), ("Wq", "bq"), ("Wv", "bv"))):
            sp.dma_start(wqkv[:, n, :], d["L1_attn_" + w]).then_inc(s_w, 16)
            sp.dma_start(bias[32 * n:32 * n + 1, :], d["L1_attn_" + b]).then_inc(s_w, 16)
        sp.dma_start(wo, d["L1_attn_Wo"].rearrange("(c p) n -> p c n", p=P)).then_inc(s_w, 16)
        sp.dma_start(bo, d["L1_attn_bo"]).then_inc(s_w, 16)

    def vector(dve):
        dve.wait_ge(*x_ready(c, layer))
        dve.memset(resets[:, :], 0.0).then_inc(s_rst, 1)
        dve.wait_ge(s_rst, 1)
        dve.memset(rmax.rearrange("p (h c) -> p h c", h=H)[:, :, 0:1], -BIG).then_inc(s_rst, 1)
        dve.memset(rmin.rearrange("p (h c) -> p h c", h=H)[:, :, 0:1], BIG).then_inc(s_rst, 1)
        dve.tensor_copy(xt[0], c.X[:, 0:P]).then_inc(s_xt, 1)
        dve.wait_ge(s_rst, 3)
        running(dve, 0, 0)
        with dve.Fori(1, NT // 2) as i:
            vector_pair(dve, i, False)
        vector_pair(dve, NT // 2, True)

    def running(dve, n, u):
        dve.wait_ge(s_kqv, n * 6 + 2)
        dve.tensor_tensor_scan(cmax[u], rmax, kqv[u][:, K_, :], -BIG, ALU.add, ALU.max).then_inc(s_cm, 1)
        dve.tensor_tensor_scan(cmin, rmin, kqv[u][:, K_, :], BIG, ALU.add, ALU.min).then_inc(s_cm, 1)

    def take_output(dve, i, u):
        dve.wait_ge(s_wo, tile(i, u) + 1)
        col = ds(tile(i, u) * P, P)
        dve.scalar_tensor_tensor(c.Y[:, col], ps_o, bo, c.X[:, col], ALU.add, ALU.add).then_inc(s_y, 1)

    def vector_pair(dve, i, last):
        for u in range(2):
            n = tile(i, u)
            v = kqv[u][:, V_, :]
            if not (last and u):
                dve.tensor_copy(xt[1 - u], c.X[:, ds(n * P + P, P)]).then_inc(s_xt, 1)

            def weigh(k):
                b = order[k]
                dve.wait_ge(s_e, n * NB + (k + 1))
                dve.tensor_reduce(heads(den)[:, :, b * Q:b * Q + Q], scores(k), AX.X, ALU.add).then_inc(s_d, 1)
                if k == 0:
                    dve.wait_ge(s_kqv, n * 6 + 6)
                dve.wait_ge(s_d, n * NB + (k + 1))
                dve.tensor_tensor(scores(k), scores(k), over_queries(v, k), ALU.mult).then_inc(s_pv, 1)

            for k in range(NB):
                if k == 0:
                    dve.wait_ge(s_m, n * 2 + 2)
                    dve.tensor_tensor(cmax[u], cmax[u], cmin, ALU.max).then_inc(s_mx, 1)
                    dve.wait_ge(s_mx, n + 1)
                dve.wait_ge(s_s, n * (2 * NB) + (2 * k + 2))
                dve.tensor_tensor(scores(k), scores(k), over_keys(cmax[u], k), ALU.subtract).then_inc(s_sub, 1)
                if k == 1 and u == 1:
                    take_output(dve, i, 0)
                if k:
                    weigh(k - 1)
                if k == 5 and not (last and u):
                    running(dve, n + 1, 1 - u)
            weigh(NB - 1)
            dve.wait_ge(s_d, n * NB + NB)
            dve.reciprocal(den, den).then_inc(s_rd, 1)
            dve.wait_ge(s_rd, n + 1)
            dve.wait_ge(s_r, SLOTS + n * NB + NB)
            dve.tensor_tensor(den.rearrange("p (h b q) -> p h b q", h=H, b=NB),
                              den.rearrange("p (h b q) -> p h b q", h=H, b=NB),
                              ps_n.rearrange("p (b h q) -> p h b q", b=NB, h=H), ALU.mult).then_inc(s_at, 1)
            dve.wait_ge(s_tr, n * 2 + 2)
        take_output(dve, i, 1)
        dve.wait_ge(s_y, i * 2)

    def gpsimd(pool):
        def tile_scores(i, u):
            n = tile(i, u)
            q, k_ = kqv[u][:, Q_, :], kqv[u][:, K_, :]
            pool.wait_ge(s_kqv, n * 6 + 4)
            pool.wait_ge(s_cm, n * 2 + 2)
            pool.tensor_tensor(cmax[u], q, cmax[u], ALU.mult).then_inc(s_m, 1)
            pool.tensor_tensor(cmin, q, cmin, ALU.mult).then_inc(s_m, 1)
            for k in range(NB):
                b, w = order[k], width[order[k]]
                pool.wait_ge(s_r, n * NB + (k + 1))
                pool.tensor_tensor(scores(k), over_keys(q, k), over_queries(k_, k), ALU.mult).then_inc(s_s, 1)
                diag = scores(k)[:, :, :, w - Q:w]
                pool.wait_ge(s_s, n * (2 * NB) + (2 * k + 1))
                pool.nop(nofuse=True)
                pool.affine_select(out=diag, in_=diag, compare_op=ALU.is_ge, fill=-BIG, base=0,
                                   pattern=[[0, H], [1, Q], [-1, Q]], channel_multiplier=0).then_inc(s_s, 1)
        with pool.Fori(1, NT // 2 + 1) as i:
            for u in range(2):
                tile_scores(i, u)

    def scalar(act):
        def copies(n, u):
            for piece in range(6):
                act_wait(act, s_pj, n * 6 + (piece + 1))
                part, half = piece // 2, piece % 2
                act.activation(kqv[u][:, part, half * 512:half * 512 + 512], ps_p[half], ACT.Copy,
                               scale=C ** -0.5 if part == Q_ else 1.0).then_inc(s_kqv, 1)
        for piece in range(6):
            act.wait_ge(s_pj, piece + 1)
            part, half = piece // 2, piece % 2
            act.activation(kqv[0][:, part, half * 512:half * 512 + 512], ps_p[half], ACT.Copy,
                           scale=C ** -0.5 if part == Q_ else 1.0).then_inc(s_kqv, 1)

        def pair(i, last):
            for u in range(2):
                n = tile(i, u)
                for k in range(NB):
                    act_wait(act, s_sub, n * NB + (k + 1))
                    act.activation(scores(k), scores(k), ACT.Exp).then_inc(s_e, 1)
                    if k == 3 and not (last and u):
                        copies(n + 1, 1 - u)
                for half in range(2):
                    act_wait(act, s_tr, n * 2 + (half + 1))
                    act.activation(attT.rearrange("p a b -> p (a b)")[:, half * 512:half * 512 + 512],
                                   ps_t[:, half * 512:half * 512 + 512], ACT.Copy).then_inc(s_trc, 1)
        with act.Fori(1, NT // 2) as i:
            pair(i, False)
        pair(NT // 2, True)

    def tensor(pe):
        pe.wait_ge(s_w, 128)
        pe.sem_inc(s_r, SLOTS)

        def project(n, u):
            pe.wait_ge(s_xt, n + 1)
            for piece in range(6):
                part, half = piece // 2, piece % 2
                if piece >= 2:
                    pe.wait_ge(s_kqv, n * 6 + (piece - 1))
                rows = slice(32 * part, 32 * part + 1)
                pe.matmul(ps_p[half], c.ones[rows, :], bias[rows, half * 512:half * 512 + 512], start=True, stop=False)
                pe.matmul(ps_p[half], xt[u], wqkv[:, part, half * 512:half * 512 + 512],
                          start=False, stop=True).then_inc(s_pj, 1)
        project(0, 0)

        def pair(i, last):
            for u in range(2):
                n = tile(i, u)
                for k in range(NB):
                    b, w = order[k], width[order[k]]
                    pe.wait_ge(s_pv, n * NB + (k + 1))
                    v = scores(k).rearrange("p h q k -> p (h q) k")
                    for key in range(w):
                        mm = pe.matmul(ps_n[:, b * P:b * P + P], c.ident, v[:, :, key],
                                       start=(key == 0), stop=(key == w - 1))
                    mm.then_inc(s_r, 1)
                    if k == 2 and not (last and u):
                        project(n + 1, 1 - u)
                pe.wait_ge(s_at, n + 1)
                for half in range(2):
                    for j in range(half * 4, half * 4 + 4):
                        mm = pe.transpose(ps_t[:, j * P:j * P + P], den[:, j * P:j * P + P], c.ident)
                    mm.then_inc(s_tr, 1)
                for half in range(2):
                    pe.wait_ge(s_trc, n * 2 + (half + 1))
                    for j in range(half * 4, half * 4 + 4):
                        mm = pe.matmul(ps_o, wo[:, j, :], attT[:, j, :], start=(j == 0), stop=(j == 7))
                mm.then_inc(s_wo, 1)
            pe.wait_ge(s_y, i * 2)
        with pe.Fori(1, NT // 2) as i:
            pair(i, False)
        pair(NT // 2, True)

    return dict(sync=sync, tensor=tensor, vector=vector, scalar=scalar, gpsimd=gpsimd, done=(s_y, NT))


def linear_attention_layer(c, d, layer):
    G = 8
    D = 8
    place = Places(c, c.free_at)
    w = place(3, P)
    wfg1 = place(P)
    wf2, wg2 = place(P), place(P)
    wo = place(P)
    nw = place(1)
    sel_k = place(G, P)
    sel_v = place(G, P)
    sel_o = place(G, P)
    head_mean = place(P)
    act5 = place(5, CH)
    fg1 = place(CH)
    vrow = place(CH)
    kv = place(CH)
    st0 = place(G, CH)
    st1 = [place(CH) for _ in range(2)]
    qs = [place(CH) for _ in range(2)]
    og, sq, sd, rs, on = place(CH), place(CH), place(CH), place(CH), place(CH)
    ps_p = c.bank[0:2]
    ps_v, ps_k, ps_f, ps_q, ps_o, ps_w = c.bank[2:8]
    take = c.layer_sems(layer)
    S = lambda n: take("lin_" + n)
    (s_w, s_p, s_pa, s_vr, s_vc, s_kr, s_kv, s_fr, s_st, s_qr, s_qs, s_o, s_og, s_sq, s_ms, s_sd, s_rs, s_on, s_wo,
     s_y) = [S(n) for n in ("w", "p", "pa", "vr", "vc", "kr", "kv", "fr", "st", "qr", "qs", "o", "og", "sq", "ms",
                            "sd", "rs", "on", "wo", "y")]
    HALVES = SEQ // CH
    loads = [(w[:, 0, :], "L2_attn_Wq"), (w[:, 1, :], "L2_attn_Wk"), (w[:, 2, :], "L2_attn_Wv"), (wfg1, "Wfg1"),
             (wf2[0:16, :], "Wf2_0"), (wg2[0:16, :], "Wg2_0"), (wo, "L2_attn_Wo"), (nw, "L2_attn_norm_weight"),
             (sel_k, "sel_k"), (sel_v, "sel_v"), (sel_o, "sel_o"), (head_mean, "head_mean")]

    def sync(sp):
        sp.wait_ge(*x_ready(c, layer))
        for dst, name in loads:
            sp.dma_start(dst, d[name]).then_inc(s_w, 16)

    def chunk(b, hf):
        return b * HALVES + (hf - HALVES)

    def tensor(pe):
        pe.wait_ge(*x_ready(c, layer))
        pe.wait_ge(s_w, 16 * len(loads))
        for s in (s_vc, s_kv, s_st, s_qs, s_og):
            pe.sem_inc(s, 1)
        pe.sem_inc(s_o, 2)
        with pe.Fori(1, BATCH + 1) as b:
            for hf in range(HALVES):
                n = chunk(b, hf)
                x = c.X[:, ds(n * CH, CH)]
                for piece in range(4):
                    if piece >= 2:
                        pe.wait_ge(s_pa, n * 6 + (piece - 1))
                    if piece < 3:
                        pe.matmul(ps_p[piece % 2], w[:, piece, :], x, start=True, stop=True).then_inc(s_p, 1)
                    else:
                        pe.matmul(ps_p[1], wfg1, x, start=True, stop=True).then_inc(s_p, 1)
                pe.wait_ge(s_pa, n * 6 + 4)
                pe.matmul(ps_p[0], wf2[0:16, :], fg1[0:16, :], start=True, stop=True).then_inc(s_p, 1)
                pe.matmul(ps_p[1], wg2[0:16, :], fg1[0:16, :], start=True, stop=True).then_inc(s_p, 1)
                pe.wait_ge(s_pa, n * 6 + 6)

                def out_group(j):
                    pe.wait_ge(s_qs, n * G + (j + 2))
                    if j == 0:
                        pe.wait_ge(s_og, n + 1)
                    pe.matmul(ps_o, sel_o[:, j, :], qs[j % 2], start=(j == 0), stop=(j == G - 1)).then_inc(s_o, 1)
                for j in range(G):
                    m = n * G + j
                    pe.wait_ge(s_vc, m + 1)
                    pe.matmul(ps_v, sel_v[:, j, :], act5[:, 2, :], start=True, stop=True).then_inc(s_vr, 1)
                    pe.wait_ge(s_kv, m + 1)
                    pe.matmul(ps_k, sel_k[:, j, :], act5[:, 1, :], start=True, stop=True).then_inc(s_kr, 1)
                    pe.wait_ge(s_st, m + 1)
                    pe.matmul(ps_f, sel_k[:, j, :], act5[:, 3, :], start=True, stop=True).then_inc(s_fr, 1)
                    if j:
                        out_group(j - 1)
                    pe.wait_ge(s_qs, m + 1)
                    pe.matmul(ps_q, sel_k[:, j, :], act5[:, 0, :], start=True, stop=True).then_inc(s_qr, 1)
                out_group(G - 1)
                pe.wait_ge(s_sq, n + 1)
                pe.matmul(ps_w, head_mean, sq, start=True, stop=True).then_inc(s_ms, 1)
                pe.wait_ge(s_on, n + 1)
                pe.matmul(ps_w, wo, on, start=True, stop=True).then_inc(s_wo, 1)

    def vector(dve):
        with dve.Fori(1, BATCH + 1) as b:
            for hf in range(HALVES):
                n = chunk(b, hf)
                for j in range(G):
                    m = n * G + j
                    dve.wait_ge(s_vc, m + 2)
                    dve.wait_ge(s_kr, m + 1)
                    dve.wait_ge(s_st, m + 1)
                    dve.tensor_tensor(kv, ps_k, vrow, ALU.mult).then_inc(s_kv, 1)
                    dve.wait_ge(s_kv, m + 2)
                    dve.wait_ge(s_fr, m + 1)
                    dve.wait_ge(s_qs, m + 1)
                    st = st1[j % 2] if hf else st0[:, j, :]
                    dve.tensor_tensor_scan(st, ps_f, kv, st0[:, j, CH - 1:CH] if hf else 0.0,
                                           ALU.mult, ALU.add).then_inc(s_st, 1)
                    dve.wait_ge(s_st, m + 2)
                    dve.wait_ge(s_qr, m + 1)
                    dve.wait_ge(s_o, m + 1)
                    dve.tensor_tensor(qs[j % 2], ps_q, st, ALU.mult).then_inc(s_qs, 1)
                dve.wait_ge(s_o, n * G + (G + 2))
                dve.tensor_tensor(og, ps_o, act5[:, 4, :], ALU.mult).then_inc(s_og, 1)
                dve.wait_ge(s_sd, n + 1)
                dve.reciprocal(rs, sd).then_inc(s_rs, 1)
                dve.wait_ge(s_rs, n + 1)
                dve.scalar_tensor_tensor(on, og, nw, rs, ALU.mult, ALU.mult).then_inc(s_on, 1)
                dve.wait_ge(s_wo, n + 1)
                dve.tensor_tensor(c.Y[:, ds(n * CH, CH)], ps_w, c.X[:, ds(n * CH, CH)], ALU.add).then_inc(s_y, 1)
                dve.wait_ge(s_y, n + 1)

    def scalar(act):
        with act.Fori(1, BATCH + 1) as b:
            for hf in range(HALVES):
                n = chunk(b, hf)
                for piece, (dst, func) in enumerate([
                        (act5[:, 0, :], ACT.Silu), (act5[:, 1, :], ACT.Silu), (act5[:, 2, :], ACT.Copy),
                        (fg1[0:16, :], ACT.Copy), (act5[:, 3, :], ACT.Sigmoid), (act5[:, 4, :], ACT.Sigmoid)]):
                    act_wait(act, s_p, n * 6 + (piece + 1))
                    src = ps_p[piece % 2]
                    act.activation(dst, src[0:16, :] if piece == 3 else src, func).then_inc(s_pa, 1)
                for j in range(G):
                    m = n * G + j
                    act_wait(act, s_vr, m + 1)
                    act_wait(act, s_kv, m + 1)
                    act.activation(vrow, ps_v, ACT.Copy).then_inc(s_vc, 1)
                act_wait(act, s_og, n + 2)
                act.activation(sq, og, ACT.Square).then_inc(s_sq, 1)
                act_wait(act, s_ms, n + 1)
                act.activation(sd, ps_w, ACT.Sqrt, bias=c.eps5).then_inc(s_sd, 1)

    return dict(sync=sync, tensor=tensor, vector=vector, scalar=scalar, done=(s_y, NCH))


def state_space_layer(c, d, layer):
    H, N, L, PD = 16, 64, 64, 8
    TPB = SEQ // P
    place = Places(c, c.norm_at)
    wcat = place(272)
    wB, wC = place(H * N), place(H * N)
    wout = place(P)
    bdt, nega = place(H), place(H)
    later = place(P)
    upto = place(P)
    since = place(L)
    hide = place(H * L)
    xt = place(P)
    dtb, dta, dte, dtl, dt, A = [place(H) for _ in range(6)]
    zs = place(P)
    xin = place(P)
    Xd, Xe = place(P), place(P)
    arow = place(H, L)
    BT, CT = place(H * N), place(H * N)
    Bk = place(H * N)
    eD = place(H * L)
    W = place(H * L)
    inch = place(2, P)
    tot = place(2, 8)
    sm = place(32)
    state = place(64)
    stn = place(64)
    yo, ys, yT = place(P), place(P), place(P)
    ps_c = c.bank[0][:, 0:272]
    ps_s = c.bank[0][:, 288:320]
    ps_tot = c.bank[0][:, 320:352].rearrange("p (c j o) -> p c j o", c=2, o=2)
    ps_BT = c.psum[:, 512:3 * 512]
    ps_CT = c.psum[:, 3 * 512:5 * 512]
    ps_Bk = c.psum[:, 5 * 512:7 * 512]
    ps_y = c.bank[7][:, 0:P]
    ps_off = c.psum[:, 512:3 * 512].rearrange("p (o n) -> p o n", o=2)[:, :, 0:64]
    ps_st = c.psum[:, 5 * 512:7 * 512].rearrange("p (c n) -> p c n", c=2)[:, :, 0:64]
    ps_T = c.bank[7][:, 2 * P:3 * P]
    ps_out = c.bank[7][:, 3 * P:4 * P]
    take = c.layer_sems(layer)
    S = lambda n: take("ssm_" + n)
    names = ("w", "al", "xt", "c", "dt", "A", "ar", "X", "BT", "CT", "Bk", "bc", "cc", "kc", "sm", "se", "D", "eD",
             "G", "W", "xe", "st", "S", "off", "yd", "y1", "tr", "tc", "o", "y", "z", "zero")
    (s_w, s_al, s_xt, s_c, s_dt, s_A, s_ar, s_X, s_BT, s_CT, s_Bk, s_bc, s_cc, s_kc, s_sm, s_se, s_D, s_eD,
     s_G, s_W, s_xe, s_st, s_S, s_off, s_yd, s_y1, s_tr, s_tc, s_o, s_y, s_z, s_zero) = [S(n) for n in names]
    loads = [(wcat, "W_cat"), (wB, "W_BT"), (wC, "W_CT"), (wout, "W_outT"), (bdt, "b_dt_rows"), (nega, "A_log_rows"),
             (later, "later"), (upto, "upto"), (since, "since"), (hide, "hide"), (inch, "inch")]

    def hv(v, k):
        return v.rearrange("p (h k) -> p h k", k=k)

    def sync(sp):
        sp.wait_ge(*x_ready(c, layer))
        for dst, name in loads:
            sp.dma_start(dst, d[name]).then_inc(s_w, 16)

    def tile(b, r):
        return b * TPB + (r - TPB)

    def vector(dve):
        dve.wait_ge(*x_ready(c, layer))
        dve.wait_ge(s_al, 1)
        dve.tensor_scalar(nega, nega, -1.0, None, ALU.mult).then_inc(s_al, 1)
        dve.wait_ge(s_al, 2)
        with dve.Fori(1, BATCH + 1) as b:
            for r in range(TPB):
                n = tile(b, r)
                dve.tensor_copy(xt, c.X[:, ds(n * P, P)]).then_inc(s_xt, 1)
                if r == 0:
                    dve.memset(state, 0.0).then_inc(s_zero, 1)
                dve.wait_ge(s_c, n + 1)
                dve.tensor_tensor(dtb, ps_c[:, 256:272], bdt, ALU.add).then_inc(s_dt, 1)
                dve.wait_ge(s_dt, n * 6 + 1)
                dve.tensor_scalar(dta, dtb, 0.0, None, ALU.max).then_inc(s_dt, 1)
                dve.wait_ge(s_dt, n * 6 + 5)
                dve.tensor_tensor(dt, dta, dtl, ALU.add).then_inc(s_dt, 1)
                dve.wait_ge(s_dt, n * 6 + 6)
                dve.tensor_tensor(A, dt, nega, ALU.mult).then_inc(s_A, 1)
                dve.tensor_tensor(hv(Xd, PD), hv(ps_c[:, 0:P], PD), dt.unsqueeze(2).to_broadcast([P, H, PD]),
                                  ALU.mult).then_inc(s_X, 1)
                dve.wait_ge(s_X, n + 1)
                dve.wait_ge(s_se, n * 3 + 3)
                dve.tensor_tensor(hv(Xe, PD), hv(Xd, PD), sm[:, 16:32].unsqueeze(2).to_broadcast([P, H, PD]),
                                  ALU.mult).then_inc(s_xe, 1)
                dve.wait_ge(s_G, n + 1)
                dve.wait_ge(s_eD, n * 2 + 2)
                dve.tensor_tensor(W, ps_CT, eD, ALU.mult).then_inc(s_W, 1)
                for ch in range(2):
                    dve.wait_ge(s_st, n + 1)
                    if ch == 0:
                        dve.wait_ge(s_off, n * 2 + 1)
                    else:
                        dve.wait_ge(s_off, n * 2 + 2)
                    dve.tensor_tensor(hv(stn, PD), hv(state, PD),
                                      tot[:, ch, :].unsqueeze(2).to_broadcast([P, 8, PD]),
                                      ALU.mult).then_inc(s_S, 1)
                    dve.wait_ge(s_S, n * 4 + (2 * ch + 1))
                    dve.tensor_tensor(state, stn, ps_st[:, ch, :], ALU.add).then_inc(s_S, 1)
                    dve.wait_ge(s_S, n * 4 + (2 * ch + 2))
                dve.wait_ge(s_yd, n + 1)
                dve.tensor_tensor(yo.rearrange("p (j o q) -> p o j q", o=2, q=PD),
                                  ps_off.rearrange("p o (j q) -> p o j q", q=PD),
                                  sm[:, 0:16].rearrange("p (j o) -> p o j", o=2).unsqueeze(3).to_broadcast([P, 2, 8, PD]),
                                  ALU.mult).then_inc(s_y1, 1)
                dve.wait_ge(s_y1, n * 3 + 1)
                dve.tensor_tensor(yo, yo, ps_y, ALU.add).then_inc(s_y1, 1)
                dve.wait_ge(s_y1, n * 3 + 2)
                dve.wait_ge(s_z, n + 1)
                dve.tensor_tensor(ys, yo, zs, ALU.mult).then_inc(s_y1, 1)
                dve.wait_ge(s_o, n + 1)
                dve.tensor_tensor(c.Y[:, ds(n * P, P)], ps_out, xt, ALU.add).then_inc(s_y, 1)
                dve.wait_ge(s_y, n + 1)

    def gpsimd(pool):
        with pool.Fori(1, T // P + 1) as i:
            pool.wait_ge(s_A, i)
            pool.wait_ge(s_w, 16 * len(loads))
            for odd in range(2):
                pool.tensor_tensor(arow[:, 8 * odd:8 * odd + 8, :], A[:, odd::2].unsqueeze(2).to_broadcast([P, 8, L]),
                                   since.unsqueeze(1).to_broadcast([P, 8, L]), ALU.mult).then_inc(s_ar, 1)

    def scalar(act):
        act.wait_ge(s_w, 16 * len(loads))
        act.activation(nega, nega, ACT.Exp).then_inc(s_al, 1)
        with act.Fori(1, T // P + 1) as i:
            n = i - 1
            act_wait(act, s_dt, i * 6 - 5)
            act.activation(dte, dtb, ACT.Abs).then_inc(s_dt, 1)
            act_wait(act, s_dt, i * 6 - 3)
            act.activation(dte, dte, ACT.Exp, scale=-1.0).then_inc(s_dt, 1)
            act_wait(act, s_dt, i * 6 - 2)
            act.activation(dtl, dte, ACT.Ln, bias=1.0).then_inc(s_dt, 1)
            for half in range(2):
                act_wait(act, s_BT, i * 2 + (half - 1))
                act.activation(BT[:, half * 512:half * 512 + 512], ps_BT[:, half * 512:half * 512 + 512],
                               ACT.Copy).then_inc(s_bc, 1)
            for half in range(2):
                act_wait(act, s_CT, i * 2 + (half - 1))
                act.activation(CT[:, half * 512:half * 512 + 512], ps_CT[:, half * 512:half * 512 + 512],
                               ACT.Copy).then_inc(s_cc, 1)
            act_wait(act, s_sm, i)
            act.activation(sm, ps_s, ACT.Exp).then_inc(s_se, 1)
            for odd in range(2):
                half_p = slice(64 * odd, 64 * odd + 64)
                act.activation(tot[half_p, :, :], ps_tot[half_p, :, :, odd], ACT.Exp).then_inc(s_se, 1)
            for half in range(2):
                act_wait(act, s_Bk, i * 2 + (half - 1))
                act.activation(Bk[:, half * 512:half * 512 + 512], ps_Bk[:, half * 512:half * 512 + 512],
                               ACT.Copy).then_inc(s_kc, 1)
            for half in range(2):
                act_wait(act, s_D, i * 2 + (half - 1))
                act.activation(eD[:, half * 512:half * 512 + 512], ps_BT[:, half * 512:half * 512 + 512],
                               ACT.Exp).then_inc(s_eD, 1)
            act.activation(zs, ps_c[:, P:2 * P], ACT.Silu).then_inc(s_z, 1)
            act_wait(act, s_tr, i)
            act.activation(yT, ps_T, ACT.Copy).then_inc(s_tc, 1)

    def tensor(pe):
        pe.wait_ge(s_w, 16 * len(loads))
        with pe.Fori(1, T // P + 1) as i:
            pe_wait(pe, s_xt, i)
            pe.matmul(ps_c, xt, wcat, start=True, stop=True).then_inc(s_c, 1)
            for dst, wgt, s in ((ps_BT, wB, s_BT), (ps_CT, wC, s_CT)):
                for half in range(2):
                    for j in range(half * 4, half * 4 + 4):
                        mm = pe.matmul(dst[:, j * P:j * P + P], wgt[:, j * P:j * P + P], xt, start=True, stop=True)
                    mm.then_inc(s, 1)
            for half in range(2):
                pe.matmul(ps_Bk[:, half * 512:half * 512 + 512], xt, wB[:, half * 512:half * 512 + 512],
                          start=True, stop=True).then_inc(s_Bk, 1)
            pe_wait(pe, s_A, i)
            pe_wait(pe, s_X, i)
            pe.matmul(ps_s[:, 0:16], upto, A, start=True, stop=True)
            pe.matmul(ps_s[:, 16:32], later, A, start=True, stop=True)
            for ch in range(2):
                mm = pe.matmul(c.bank[0][:, 320 + 16 * ch:336 + 16 * ch], inch[:, ch, :], A, start=True, stop=True)
            mm.then_inc(s_sm, 1)
            pe_wait(pe, s_ar, i * 2)
            pe_wait(pe, s_bc, i * 2)
            for half in range(2):
                pe.matmul(ps_BT[:, half * 512:half * 512 + 512], later,
                          arow.rearrange("p h l -> p (h l)")[:, half * 512:half * 512 + 512], start=True, stop=False)
                pe.matmul(ps_BT[:, half * 512:half * 512 + 512], c.ident, hide[:, half * 512:half * 512 + 512],
                          start=False, stop=True).then_inc(s_D, 1)
            pe_wait(pe, s_cc, i * 2)
            for h in range(H):
                rows = slice(64 * (h % 2), 64 * (h % 2) + 64)
                for ch in range(2):
                    at = (h // 2) * P + ch * L
                    g = (h % 2) * 8 + h // 2
                    mm = pe.matmul(ps_CT[64 * ch:64 * ch + 64, g * L:g * L + L], BT[rows, at:at + L],
                                   CT[rows, at:at + L], start=True, stop=True)
            mm.then_inc(s_G, 1)
            pe_wait(pe, s_xe, i)
            pe_wait(pe, s_kc, i * 2)
            for ch in range(2):
                rows = slice(64 * ch, 64 * ch + 64)
                for h in range(H):
                    mm = pe.matmul(ps_st[64 * (h % 2):64 * (h % 2) + 64, ch, (h // 2) * PD:(h // 2) * PD + PD],
                                   Bk[rows, h * N:h * N + N], Xe[rows, h * PD:h * PD + PD], start=True, stop=True)
            mm.then_inc(s_st, 1)
            pe_wait(pe, s_eD, i * 2)
            for ch in range(2):
                if ch:
                    pe_wait(pe, s_S, i * 4 - 2)
                for h in range(H):
                    rows = slice(64 * (h % 2), 64 * (h % 2) + 64)
                    at = (h // 2) * P + ch * L
                    mm = pe.matmul(ps_off[64 * ch:64 * ch + 64, h % 2, (h // 2) * PD:(h // 2) * PD + PD], CT[rows, at:at + L],
                                   state[rows, (h // 2) * PD:(h // 2) * PD + PD], start=True, stop=True)
                mm.then_inc(s_off, 1)
            pe_wait(pe, s_W, i)
            for ch in range(2):
                rows = slice(64 * ch, 64 * ch + 64)
                for h in range(H):
                    g = (h % 2) * 8 + h // 2
                    mm = pe.matmul(ps_y[64 * ch:64 * ch + 64, h * PD:h * PD + PD], W[rows, g * L:g * L + L],
                                   Xd[rows, h * PD:h * PD + PD], start=True, stop=True)
            mm.then_inc(s_yd, 1)
            pe_wait(pe, s_y1, i * 3)
            pe.transpose(ps_T, ys, c.ident).then_inc(s_tr, 1)
            pe_wait(pe, s_tc, i)
            pe.matmul(ps_out, wout, yT, start=True, stop=True).then_inc(s_o, 1)

    return dict(sync=sync, tensor=tensor, vector=vector, scalar=scalar, gpsimd=gpsimd, done=(s_y, T // P))


def kron_experts_layer(c, d, layer):
    E, R, F = 64, 32, 64
    NS = T // 8
    NT = NS // P
    GS = 4
    PAIRS = P // GS // 2
    place = Places(c, c.free_at)
    upB, upA = place(E, F), place(E, F)
    dnB, dnA = place(E, R), place(E, R)
    wup = place(8, E)
    wdn = place(F, E)
    bup, bdn = place(F), place(R)
    sup, sdn = place(1), place(1)
    xs = place(P * R + 2 * P)
    Hid = place(P + 2 * GS, F)
    yd = place(P, R)
    lg = place(E)
    top = place(8)
    topi = place(8).bitcast(U32)
    prob = place(4)
    pk = place(2)
    dgp = place(2, P)
    pb = place(2, P)
    row = place(2 * P).bitcast(U32)
    grp = [place(P) for _ in range(2)]
    hgrp = [place(GS, F) for _ in range(2)]
    tk_ = [place(2, GS, F) for _ in range(2)]
    hb = [place(GS, F) for _ in range(2)]
    tdn = [place(2, GS, R) for _ in range(2)]
    scratch = c.nc.dram_tensor("expert_numbers", (2 * NT, 2 * P), U32, kind="Internal").ap()
    ps_l = c.bank[6][:, 0:E]
    ps_b = c.bank[7][:, 0:2 * P]
    ps_1 = c.bank[0:2]
    ps_2 = c.bank[2:4]
    take = c.layer_sems(layer)
    S = lambda n: take("kron_" + n)
    names = ("w", "xs", "l", "lg", "top", "ti", "pr", "ex", "dg", "b", "pb", "out", "row", "g", "m1", "t", "m2", "h", "a",
             "hg", "d1", "td", "d2", "yd", "y", "yb", "hz")
    (s_w, s_xs, s_l, s_lg, s_top, s_ti, s_pr, s_ex, s_dg, s_b, s_pb, s_out, s_row, s_g, s_m1, s_t, s_m2, s_h, s_a,
     s_hg, s_d1, s_td, s_d2, s_yd, s_y, s_yb, s_hz) = [S(n) for n in names]
    loads = [(upB[0:R], "up_B"), (upA[0:R], "up_A"), (dnB[0:F], "dn_B"), (dnA[0:F], "dn_A"), (wup, "W_up"),
             (wdn[0:F], "W_down"), (bup[0:F, :], "bias_up"), (bdn[0:R, :], "bias_down"), (sup, "scale_up"),
             (sdn, "scale_down")]

    def group(t, i, u):
        return i * 2 + (t * 2 * PAIRS + u - 2)

    def sync(sp):
        sp.wait_ge(*x_ready(c, layer))
        for dst, name in loads:
            sp.dma_start(dst, d[name]).then_inc(s_w, 16)
        for q in range(2 * NT):
            sp.wait_ge(s_ti, q + 1)
            sp.dma_start(scratch[q:q + 1, :].rearrange("a (n k) -> (a n) k", k=2), topi[:, 0:2]).then_inc(s_out, 16)
            sp.wait_ge(s_out, 16 * (q + 1))
            sp.dma_start(row[0:1, :], scratch[q:q + 1, :]).then_inc(s_row, 16)

    def vector(dve):
        dve.wait_ge(*x_ready(c, layer))
        dve.memset(xs[0:R, P * R:P * R + 2 * P], 0.0).then_inc(s_xs, 1)
        dve.memset(Hid[0:F, P:P + 2 * GS, :], 0.0).then_inc(s_hz, 1)
        dve.wait_ge(s_w, 16 * len(loads))

        def choose(q):
            dve.wait_ge(s_l, q + 1)
            dve.tensor_copy(lg, ps_l).then_inc(s_lg, 1)
            dve.wait_ge(s_lg, q + 1)
            dve.max(top, lg).then_inc(s_top, 1)
            dve.wait_ge(s_top, q + 1)
            if q:
                dve.wait_ge(s_out, 16 * q)
            dve.max_index(topi, top, lg).then_inc(s_ti, 1)
            dve.tensor_tensor(prob[:, 0:1], top[:, 1:2], top[:, 0:1], ALU.subtract).then_inc(s_pr, 1)
            dve.wait_ge(s_ex, q + 1)
            dve.tensor_scalar(prob[:, 2:3], prob[:, 1:2], 1.0, None, ALU.add).then_inc(s_pr, 1)
            dve.wait_ge(s_pr, 4 * q + 2)
            dve.reciprocal(pk[:, 0:1], prob[:, 2:3]).then_inc(s_pr, 1)
            dve.wait_ge(s_pr, 4 * q + 3)
            dve.tensor_tensor(pk[:, 1:2], prob[:, 1:2], pk[:, 0:1], ALU.mult).then_inc(s_pr, 1)
            dve.wait_ge(s_pr, 4 * q + 4)
            for k in range(2):
                dve.tensor_scalar(dgp[:, k, :], c.ident, pk[:, k:k + 1], None, ALU.mult).then_inc(s_dg, 1)
            dve.wait_ge(s_b, q + 1)
            dve.tensor_copy(pb.rearrange("p k n -> p (k n)"), ps_b).then_inc(s_pb, 1)
            dve.wait_ge(s_pb, q + 1)

        for t in range(NT):
            for dd in range(4):
                dve.tensor_copy(xs[0:R, 0:P * R].rearrange("p (n q) -> p n q", q=4)[:, :, dd],
                                c.X[32 * dd:32 * dd + 32, t * 8 * P:(t + 1) * 8 * P]).then_inc(s_xs, 1)
            choose(2 * t)
            with dve.Fori(1, PAIRS + 1) as i:
                for u in range(2):
                    dve.wait_ge(s_m1, group(t, i, u) + 1)
                    for s in range(GS):
                        dve.tensor_tensor(
                            tk_[u][0:R, :, s, :],
                            ps_1[u][32 * s:32 * s + 32, s * 2 * F:(s + 1) * 2 * F].rearrange("p (k f) -> p k f", k=2),
                            pb[0:R, :, ds(i * (2 * GS) + ((u - 2) * GS + s), 1)].to_broadcast([R, 2, F]),
                            ALU.mult).then_inc(s_t, 1)
                for u in range(2):
                    dve.wait_ge(s_m2, group(t, i, u) + 1)
                    for s in range(GS):
                        rows = slice(64 * (s % 2), 64 * (s % 2) + 64)
                        dve.scalar_tensor_tensor(hb[u][0:F, s, :], ps_2[u][rows, s * F:(s + 1) * F], sup[rows, :],
                                                 bup[0:F, :], ALU.mult, ALU.add).then_inc(s_h, 1)
                dve.wait_ge(s_a, group(t, i, 1) + 1)
            choose(2 * t + 1)
            with dve.Fori(1, PAIRS + 1) as i:
                for u in range(2):
                    dve.wait_ge(s_d1, group(t, i, u) + 1)
                    for s in range(GS):
                        rows = slice(64 * (s % 2), 64 * (s % 2) + 64)
                        dve.tensor_tensor(
                            tdn[u][0:F, :, s, :],
                            ps_1[u][rows, s * 2 * R:(s + 1) * 2 * R].rearrange("p (k f) -> p k f", k=2),
                            pb[0:F, :, ds(i * (2 * GS) + ((u - 2) * GS + s), 1)].to_broadcast([F, 2, R]),
                            ALU.mult).then_inc(s_td, 1)
                for u in range(2):
                    dve.wait_ge(s_d2, group(t, i, u) + 1)
                    for s in range(GS):
                        dve.tensor_copy(yd[0:R, ds(i * (2 * GS) + ((u - 2) * GS + s), 1), :],
                                        ps_2[u][32 * s:32 * s + 32, s * R:(s + 1) * R].unsqueeze(1)).then_inc(s_yd, 1)
            dve.wait_ge(s_yd, P * (t + 1))
            dve.scalar_tensor_tensor(yd[0:R], yd[0:R], sdn[0:R, :], bdn[0:R, :].unsqueeze(1).to_broadcast([R, P, R]),
                                     ALU.mult, ALU.add).then_inc(s_yb, 1)
            dve.wait_ge(s_yb, t + 1)
            for dd in range(4):
                dve.tensor_copy(c.Y[32 * dd:32 * dd + 32, t * 8 * P:(t + 1) * 8 * P],
                                yd[0:R].rearrange("p n (k q) -> p (n k) q", q=4)[:, :, dd]).then_inc(s_y, 1)
            dve.wait_ge(s_y, 4 * (t + 1))
        dve.tensor_tensor(c.Y, c.Y, c.X, ALU.add).then_inc(s_y, 1)

    def scalar(act):
        act.wait_ge(s_hz, 1)

        def exp_difference(q):
            act.wait_ge(s_pr, 4 * q + 1)
            act.activation(prob[:, 1:2], prob[:, 0:1], ACT.Exp).then_inc(s_ex, 1)
        for t in range(NT):
            act.wait_ge(s_xs, 4 * t + 5)
            for u in range(2):
                act.activation(grp[u][0:R, :], xs[0:R, u * P:u * P + P], ACT.Copy).then_inc(s_g, 1)
            exp_difference(2 * t)
            with act.Fori(1, PAIRS + 1) as i:
                for u in range(2):
                    act_wait(act, s_m1, group(t, i, u) + 1)
                    act.activation(grp[u][0:R, :], xs[0:R, ds(i * (2 * P) + u * P, P)],
                                   ACT.Copy).then_inc(s_g, 1)
                for u in range(2):
                    act_wait(act, s_h, group(t, i, u) * GS + GS)
                    act.activation(Hid[0:F, ds(i * (2 * GS) + (u - 2) * GS, GS), :], hb[u][0:F], ACT.Gelu).then_inc(s_a, 1)
            act.wait_ge(s_a, 2 * PAIRS * (t + 1))
            exp_difference(2 * t + 1)
            for u in range(2):
                act.activation(hgrp[u][0:F], Hid[0:F, u * GS:u * GS + GS, :], ACT.Copy).then_inc(s_hg, 1)
            with act.Fori(1, PAIRS + 1) as i:
                for u in range(2):
                    act_wait(act, s_d1, group(t, i, u) + 1)
                    act.activation(hgrp[u][0:F], Hid[0:F, ds(i * (2 * GS) + u * GS, GS), :], ACT.Copy).then_inc(s_hg, 1)
            act.wait_ge(s_hg, (2 * PAIRS + 2) * (t + 1))

    def tensor(pe):
        pe.wait_ge(*x_ready(c, layer))
        pe.wait_ge(s_w, 16 * len(loads))

        def spread(q):
            pe.wait_ge(s_dg, 2 * q + 2)
            pe.matmul(ps_b, c.ones, dgp.rearrange("p k n -> p (k n)"), start=True, stop=True).then_inc(s_b, 1)
            pe.wait_ge(s_pb, q + 1)
            pe.wait_ge(s_row, 16 * (q + 1))

        def numbers(i):
            return [pe.value_load(row[0:1, ds(i * (4 * GS) + (n - 4 * GS), 1)], min_val=0, max_val=E - 1)
                    for n in range(4 * GS)]

        for t in range(NT):
            for k in range(8):
                mm = pe.matmul(ps_l, c.X[:, t * 8 * P + k:(t + 1) * 8 * P:8], wup[:, k, :], start=(k == 0), stop=(k == 7))
            mm.then_inc(s_l, 1)
            spread(2 * t)
            with pe.Fori(1, PAIRS + 1) as i:
                e = numbers(i)
                for u in range(2):
                    pe.wait_ge(s_g, i * 2 + (u - 1 + t * (2 * PAIRS + 2)))
                    for n in range(2 * GS):
                        mm = pe.matmul(ps_1[u][:, n * F:(n + 1) * F], grp[u][0:R, :],
                                       upB.rearrange("p e f -> p (e f)")[0:R, ds(e[2 * GS * u + n] * F, F)],
                                       start=True, stop=True)
                    mm.then_inc(s_m1, 1)
                for u in range(2):
                    pe.wait_ge(s_t, group(t, i, u) * GS + GS)
                    for n in range(2 * GS):
                        s, k = n // 2, n % 2
                        mm = pe.matmul(ps_2[u][:, s * F:(s + 1) * F], tk_[u][0:R, k, s // 2 * 2:s // 2 * 2 + 2, :],
                                       upA.rearrange("p e f -> p (e f)")[0:R, ds(e[2 * GS * u + n] * F, F)],
                                       start=(k == 0), stop=(k == 1))
                    mm.then_inc(s_m2, 1)
            pe.wait_ge(s_a, 2 * PAIRS * (t + 1))
            for o in range(F):
                mm = pe.matmul(ps_l, Hid[0:F, 0:P, o], wdn[0:F, o, :], start=(o == 0), stop=(o == F - 1))
            mm.then_inc(s_l, 1)
            spread(2 * t + 1)
            with pe.Fori(1, PAIRS + 1) as i:
                e = numbers(i)
                for u in range(2):
                    pe.wait_ge(s_hg, i * 2 + (u - 1 + t * (2 * PAIRS + 2)))
                    for n in range(2 * GS):
                        s = n // 2
                        mm = pe.matmul(ps_1[u][:, n * R:(n + 1) * R], hgrp[u][0:F, s // 2 * 2:s // 2 * 2 + 2, :],
                                       dnB.rearrange("p e f -> p (e f)")[0:F, ds(e[2 * GS * u + n] * R, R)],
                                       start=True, stop=True)
                    mm.then_inc(s_d1, 1)
                for u in range(2):
                    pe.wait_ge(s_td, group(t, i, u) * GS + GS)
                    for n in range(2 * GS):
                        s, k = n // 2, n % 2
                        mm = pe.matmul(ps_2[u][:, s * R:(s + 1) * R], tdn[u][0:F, k, :, :],
                                       dnA.rearrange("p e f -> p (e f)")[0:F, ds(e[2 * GS * u + n] * R, R)],
                                       start=(k == 0), stop=(k == 1))
                    mm.then_inc(s_d2, 1)
            pe.wait_ge(s_yd, P * (t + 1))

    return dict(sync=sync, tensor=tensor, vector=vector, scalar=scalar, done=(s_y, 4 * NT + 1))


def layouts(np, a):
    def cols(v):
        return np.asarray(v).reshape(-1, P).T
    out = {"xT": np.asarray(a["L0_attn_data"]).reshape(T, P).T}
    out["L0_attn_W2"] = np.asarray(a["L0_attn_W2"])
    out["W1_rows"] = np.repeat(np.asarray(a["L0_attn_W1"]).reshape(1, P), P, axis=0)
    out["L0_attn_b1"] = cols(a["L0_attn_b1"])
    out["L0_ffn_w1"], out["L0_ffn_w2"] = np.asarray(a["L0_ffn_w1"]), np.asarray(a["L0_ffn_w2"])
    out["L0_ffn_b1"], out["L0_ffn_b2"] = cols(a["L0_ffn_b1"]), cols(a["L0_ffn_b2"])
    out["L1_ffn_W_fc"], out["L1_ffn_W_proj"] = np.asarray(a["L1_ffn_W_fc"]), np.asarray(a["L1_ffn_W_proj"])
    out["L1_ffn_ln_w"], out["L1_ffn_ln_b"] = cols(a["L1_ffn_ln_w"]), cols(a["L1_ffn_ln_b"])
    out["L2_ffn_W1"], out["L2_ffn_W2"] = np.asarray(a["L2_ffn_W1"]), np.asarray(a["L2_ffn_W2"])
    out["L2_ffn_b1"], out["L2_ffn_b2"] = cols(a["L2_ffn_b1"]), cols(a["L2_ffn_b2"])
    out["L2_ffn_Wu"] = np.asarray(a["L2_ffn_Wu"])
    out["L2_ffn_bu"] = np.repeat(np.asarray(a["L2_ffn_bu"]).reshape(1, 1), P, axis=0)
    for n in "kqv":
        out["L1_attn_W" + n] = np.asarray(a["L1_attn_W" + n])
        out["L1_attn_b" + n] = np.asarray(a["L1_attn_b" + n]).reshape(1, -1)
    out["L1_attn_Wo"], out["L1_attn_bo"] = np.asarray(a["L1_attn_Wo"]), cols(a["L1_attn_bo"])
    for n in "qkvo":
        out["L2_attn_W" + n] = np.asarray(a["L2_attn_W" + n])
    out["Wfg1"] = np.concatenate([np.asarray(a["L2_attn_Wf1"]), np.asarray(a["L2_attn_Wg1"]),
                                   np.zeros((P, P - 16), np.float32)], axis=1)
    none = np.zeros((8, P), np.float32)
    out["Wf2_0"] = np.concatenate([np.asarray(a["L2_attn_Wf2"]), none])
    out["Wg2_0"] = np.concatenate([none, np.asarray(a["L2_attn_Wg2"])])
    out["L2_attn_norm_weight"] = cols(a["L2_attn_norm_weight"])
    feature = np.arange(P).reshape(P, 1, 1)
    group, row = np.arange(8).reshape(1, 8, 1), np.arange(P).reshape(1, 1, P)
    head = 2 * group + row // 64
    by_key = (feature == 8 * head + row // 8 % 8).astype(np.float32)
    by_value = (feature == 8 * head + row % 8).astype(np.float32)
    out["sel_k"], out["sel_v"] = by_key, by_value
    out["sel_o"] = np.transpose(by_value, (2, 1, 0)) * np.float32(8 ** -0.5)
    f = np.arange(P)
    out["head_mean"] = (f[:, None] // 8 == f[None, :] // 8).astype(np.float32) / np.float32(8)
    out["W_cat"] = np.concatenate([np.asarray(a["L3_attn_W_in"]).T, np.asarray(a["L3_attn_W_dt"]).T], axis=1)
    out["W_BT"], out["W_CT"] = np.asarray(a["L3_attn_W_B"]).T, np.asarray(a["L3_attn_W_C"]).T
    out["W_outT"] = np.asarray(a["L3_attn_W_out"]).T
    out["b_dt_rows"] = np.repeat(np.asarray(a["L3_attn_b_dt"]).reshape(1, -1), P, axis=0)
    out["A_log_rows"] = np.repeat(np.asarray(a["L3_attn_A_log"]).reshape(1, -1), P, axis=0)
    same = f[:, None] // 64 == f[None, :] // 64
    out["later"] = (same & (f[:, None] > f[None, :])).astype(np.float32)
    out["upto"] = (same & (f[:, None] <= f[None, :])).astype(np.float32)
    out["inch"] = (f[:, None, None] // 64 == np.arange(2)[None, :, None]).repeat(P, axis=2).astype(np.float32)
    l = np.arange(64)
    out["since"] = (l[None, :] >= f[:, None] % 64).astype(np.float32)
    out["hide"] = np.where(np.tile(l, 16)[None, :] < f[:, None] % 64, -BIG, 0.0).astype(np.float32)
    for which, name in (("up", "up"), ("dn", "down")):
        for m in "AB":
            out[which + "_" + m] = np.asarray(a[f"L3_ffn_{m}_{name}"]).transpose(2, 0, 1)
    out["W_up"] = np.asarray(a["L3_ffn_W_up"]).reshape(64, 8, P).transpose(2, 1, 0)
    out["W_down"] = np.asarray(a["L3_ffn_W_down"]).reshape(64, 64, 64).transpose(2, 1, 0)
    out["bias_up"] = np.asarray(a["L3_ffn_bias_up"]).reshape(64, 64).T
    out["bias_down"] = np.asarray(a["L3_ffn_bias_down"]).reshape(32, 32).T
    for name in ("scale_up", "scale_down"):
        out[name] = np.repeat(np.asarray(a["L3_ffn_" + name]).reshape(1, 1), P, axis=0)
    return out


def build(nc, d, out, layers, start=0):
    with ExitStack() as ctx:
        c = Core(nc, ctx)
        plan = [make(c, d, n) for n, make in enumerate(layers)]

        def y_done(layer):
            return plan[layer]["done"]
        ln_tensor, ln_vector, ln_scalar = layer_norm(c, y_done)
        block = ctx.enter_context(nc.Block())

        @block.sync
        def _(sp):
            sp.dma_start(c.X, d["xT"]).then_inc(c.s_xload, 16)
            for layer, part in enumerate(plan):
                if layer == HALF:
                    c.half_way(sp)
                if "sync" in part:
                    part["sync"](sp)
            sp.wait_ge(*x_ready(c, len(plan)))
            sp.dma_start(out, c.X).then_inc(c.s_out, 16)
            sp.wait_ge(c.s_out, 16)

        @block.gpsimd
        def _(pool):
            pool.memset(c.ident, 0.0).then_inc(c.s_const, 1)
            pool.wait_ge(c.s_const, 1)
            pool.affine_select(out=c.ident, in_=c.ident, compare_op=ALU.not_equal, fill=1.0, base=0,
                               pattern=[[-1, P]], channel_multiplier=1).then_inc(c.s_ident, 1)
            for layer, part in enumerate(plan):
                if layer == HALF:
                    c.half_way(pool, clears=True)
                if "gpsimd" in part:
                    part["gpsimd"](pool)

        @block.vector
        def _(dve):
            dve.memset(c.ones, 1.0).then_inc(c.s_ones, 1)
            dve.memset(c.mean, 1.0 / P).then_inc(c.s_ones, 1)
            dve.memset(c.eps5, 1e-5).then_inc(c.s_ones, 1)
            dve.wait_ge(c.s_ident, 1)
            dve.wait_ge(c.s_ones, 3)
            for layer, part in enumerate(plan):
                if layer == HALF:
                    c.half_way(dve)
                part["vector"](dve)
                ln_vector(dve, layer)

        @block.scalar
        def _(act):
            act.wait_ge(c.s_ones, 3)
            for layer, part in enumerate(plan):
                if layer == HALF:
                    c.half_way(act)
                part["scalar"](act)
                ln_scalar(act, layer)

        @block.tensor
        def _(pe):
            pe.wait_ge(c.s_ones, 3)
            pe.wait_ge(c.s_ident, 1)
            for layer, part in enumerate(plan):
                if layer == HALF:
                    c.half_way(pe)
                part["tensor"](pe)
                ln_tensor(pe, layer)


LAYERS = [similarity_layer, binary_ffn_layer, outer_attention_layer, ternary_ffn_layer,
          linear_attention_layer, expert_ffn_layer, state_space_layer, kron_experts_layer]


def kernel(**inputs):
    import numpy as np
    import concourse.bacc as _bacc
    from concourse.bass_utils import run_bass_kernel_spmd as _run

    nc = _bacc.Bacc("TRN2", target_bir_lowering=False, num_devices=1)
    lay = layouts(np, inputs)
    arrays, d = {}, {}
    for name, a in lay.items():
        a = np.ascontiguousarray(a)
        arrays[name] = a
        d[name] = nc.dram_tensor(name, a.shape, mybir.dt.from_np(a.dtype), kind="ExternalInput").ap()
    out = nc.dram_tensor("out_xT", (P, T), F32, kind="ExternalOutput").ap()
    build(nc, d, out, LAYERS)
    r = _run(nc, [arrays], core_ids=[0])
    return np.ascontiguousarray(r.results[0]["out_xT"].T).reshape(BATCH, SEQ, P)
```

```python
from contextlib import ExitStack

import concourse.bass as bass
from concourse import mybir
from concourse.alu_op_type import AluOpType as ALU

F32 = mybir.dt.float32
U32 = mybir.dt.uint32
ACT = mybir.ActivationFunctionType
AX = mybir.AxisListType
ds = bass.ds

P = 128
T = 4096
BATCH = 4
SEQ = T // BATCH
CH = 512
NCH = T // CH
BIG = 1.0e30
LN_EXP = "natural_log_exp_and_others"
HALF = 4


def act_wait(act, sem, value):
    act.wait_ge(sem, value)
    act.nop(nofuse=True)


def pe_wait(pe, sem, value):
    pe.wait_ge(sem, value)
    pe.nop(nofuse=True)


class Core:

    def __init__(self, nc, ctx):
        self.nc, self.ctx = nc, ctx
        self.arena = ctx.enter_context(nc.sbuf_tensor("arena", [P, 53200], F32))
        self.psum = ctx.enter_context(nc.psum_tensor("psum", [P, 8 * 512], F32))
        self.bank = [self.psum[:, 512 * i:512 * i + 512] for i in range(8)]
        self.X = self.arena[:, 0:T]
        self.Y = self.arena[:, T:2 * T]
        at = 2 * T
        self.ident = self.arena[:, at:at + P]
        self.ones = self.arena[:, at + P:at + 2 * P]
        self.mean = self.arena[:, at + 2 * P:at + 3 * P]
        self.eps5 = self.arena[:, at + 3 * P:at + 3 * P + 1]
        at += 3 * P + 4
        self.norm_at = at
        self.free_at = at + 4096
        self.used = []
        self.s_meet = self.sem("s_meet")
        self.s_cleared = self.sem("s_cleared")
        self.s_const = self.sem("s_const")
        self.s_ident = self.sem("s_ident")
        self.s_ones = self.sem("s_ones")
        self.s_x = self.sem("s_x")
        self.s_xload = self.sem("s_xload")
        self.s_out = self.sem("s_out")

    def sem(self, name):
        return self.ctx.enter_context(self.nc.semaphore(name))

    def layer_sems(self, layer):
        if layer == HALF:
            self.spare = list(self.used)
        def take(name):
            if layer >= HALF and self.spare:
                return self.spare.pop()
            s = self.sem(name)
            if layer < HALF:
                self.used.append(s)
            return s
        return take

    def half_way(self, eng, clears=False):
        eng.sem_inc(self.s_meet, 1)
        eng.wait_ge(self.s_meet, 5)
        if clears:
            for s in self.used:
                eng.sem_clear(s)
            eng.sem_inc(self.s_cleared, 1)
        eng.wait_ge(self.s_cleared, 1)

    def cut(self, at, *shape):
        n = 1
        for d in shape:
            n *= d
        v = self.arena[:, at:at + n]
        if len(shape) == 2:
            v = v.rearrange("p (a b) -> p a b", a=shape[0])
        if len(shape) == 3:
            v = v.rearrange("p (a b c) -> p a b c", a=shape[0], b=shape[1])
        return v


class Places:

    def __init__(self, core, at):
        self.core, self.at = core, at

    def __call__(self, *shape):
        n = 1
        for d in shape:
            n *= d
        v = self.core.cut(self.at, *shape)
        self.at += n
        assert self.at <= 53200, self.at
        return v


def layer_norm(c, y_done, y_of):
    place = Places(c, c.norm_at)
    xc = [place(CH) for _ in range(2)]
    sq = [place(CH) for _ in range(2)]
    lv = [place(CH) for _ in range(2)]
    rs = [place(CH) for _ in range(2)]
    ps_mean, ps_var = c.bank[0:2], c.bank[2:4]
    s_mean = [c.sem(f"ln_mean{u}") for u in range(2)]
    s_xc = [c.sem(f"ln_xc{u}") for u in range(2)]
    s_sq = [c.sem(f"ln_sq{u}") for u in range(2)]
    s_var = [c.sem(f"ln_var{u}") for u in range(2)]
    s_lv = [c.sem(f"ln_lv{u}") for u in range(2)]
    s_rs = [c.sem(f"ln_rs{u}") for u in range(2)]
    ROUNDS = NCH // 2

    def col(i, u):
        return ds(i * (2 * CH) + (u * CH - 2 * CH), CH)

    def tensor(pe, layer):
        base = ROUNDS * layer
        pe.wait_ge(*y_done(layer))
        with pe.Fori(1, ROUNDS + 1) as i:
            for u in range(2):
                pe.matmul(ps_mean[u][:, :], c.mean, y_of(layer)[:, col(i, u)], start=True, stop=True).then_inc(s_mean[u], 1)
            for u in range(2):
                pe.wait_ge(s_sq[u], i + base)
                pe.matmul(ps_var[u][:, :], c.mean, sq[u], start=True, stop=True).then_inc(s_var[u], 1)

    def vector(dve, layer):
        base = ROUNDS * layer
        dve.wait_ge(*y_done(layer))
        with dve.Fori(1, ROUNDS + 1) as i:
            for u in range(2):
                dve.wait_ge(s_mean[u], i + base)
                dve.tensor_tensor(xc[u], y_of(layer)[:, col(i, u)], ps_mean[u][:, :], ALU.subtract).then_inc(s_xc[u], 1)
            for u in range(2):
                dve.wait_ge(s_rs[u], i + base)
                dve.tensor_tensor(c.X[:, col(i, u)], xc[u], rs[u], ALU.mult).then_inc(c.s_x, 1)
            dve.wait_ge(c.s_x, i * 2 + NCH * layer)

    def scalar(act, layer):
        base = ROUNDS * layer
        act.preload_act_table_set(LN_EXP)
        with act.Fori(1, ROUNDS + 1) as i:
            for u in range(2):
                act_wait(act, s_xc[u], i + base)
                act.activation(sq[u], xc[u], ACT.Square).then_inc(s_sq[u], 1)
            for u in range(2):
                act_wait(act, s_var[u], i + base)
                act.activation(lv[u], ps_var[u][:, :], ACT.Ln, bias=c.eps5).then_inc(s_lv[u], 1)
            for u in range(2):
                act_wait(act, s_lv[u], i + base)
                act.activation(rs[u], lv[u], ACT.Exp, scale=-0.5).then_inc(s_rs[u], 1)

    return tensor, vector, scalar


def x_ready(c, layer):
    return (c.s_x, NCH * layer) if layer else (c.s_xload, 16)


def similarity_layer(c, d, layer):
    place = Places(c, c.free_at)
    N = place(T)
    W2a, W2b = place(P), place(P)
    W1r = place(P)
    b1 = place(1)
    sq = [place(CH) for _ in range(2)]
    mx = [place(CH) for _ in range(2)]
    sd = [place(CH) for _ in range(2)]
    rs = [place(CH) for _ in range(2)]
    nt = [place(P) for _ in range(2)]
    relu = [place(SEQ) for _ in range(2)]
    cnt = [place(1) for _ in range(2)]
    dg = [place(P) for _ in range(2)]
    xs = [place(CH) for _ in range(2)]
    z = [place(CH) for _ in range(2)]
    az = [place(CH) for _ in range(2)]
    ez = [place(CH) for _ in range(2)]
    lz = [place(CH) for _ in range(2)]
    sp = [place(CH) for _ in range(2)]
    ps_sq = c.bank[0:2]
    ps_sim = [c.bank[0:2], c.bank[2:4]]
    ps_z = c.bank[4:6]
    ps_o = c.bank[6:8]
    take = c.layer_sems(layer)
    S = lambda n: take("sim_" + n)
    s_w, s_sq, s_ss, s_mx, s_sd, s_rs, s_n = S("w"), S("sq"), S("ss"), S("mx"), S("sd"), S("rs"), S("n")
    s_nt, s_sim, s_cnt, s_dg, s_z, s_zb, s_r = S("nt"), S("sim"), S("cnt"), S("dg"), S("z"), S("zb"), S("r")
    s_az, s_ez, s_lz, s_sp, s_o, s_y = S("az"), S("ez"), S("lz"), S("sp"), S("o"), S("y")
    TPB = SEQ // P
    TPC = CH // P

    def sync(sp_):
        sp_.dma_start(W2a, d["L0_attn_W2"][0:P, :]).then_inc(s_w, 16)
        sp_.dma_start(W2b, d["L0_attn_W2"][P:2 * P, :]).then_inc(s_w, 16)
        sp_.dma_start(W1r, d["W1_rows"]).then_inc(s_w, 16)
        sp_.dma_start(b1, d["L0_attn_b1"]).then_inc(s_w, 16)

    def tensor(pe):
        pe.wait_ge(s_w, 64)
        with pe.Fori(1, NCH // 2 + 1) as i:
            for u in range(2):
                pe.wait_ge(s_sq, i * 2 + (u - 1))
                pe.matmul(ps_sq[u][:, :], c.ones, sq[u], start=True, stop=True).then_inc(s_ss, 1)
        pe.wait_ge(s_n, NCH)
        with pe.Fori(1, BATCH + 1) as b:
            def project(h):
                pe.wait_ge(s_sp, b * 2 + (h - 1))
                pe.matmul(ps_o[h][:, :], W2a, xs[h], start=True, stop=False)
                pe.matmul(ps_o[h][:, :], W2b, sp[h], start=False, stop=True).then_inc(s_o, 1)
            for r in range(TPB):
                u, h, j = r % 2, r // TPC, r % TPC
                pe.wait_ge(s_nt, b * TPB + (r + 1 - TPB))
                for half in range(2):
                    mm = pe.matmul(ps_sim[u][half][:, :], nt[u], N[:, ds(b * SEQ + (half * CH - SEQ), CH)],
                                   start=True, stop=True)
                mm.then_inc(s_sim, 1)
                if r:
                    uu, hh, jj = (r - 1) % 2, (r - 1) // TPC, (r - 1) % TPC
                    pe.wait_ge(s_dg, b * TPB + (r - TPB))
                    pe.matmul(ps_z[hh][:, jj * P:jj * P + P], W1r, dg[uu], start=True, stop=True).then_inc(s_z, 1)
                if r == TPC + 1:
                    project(0)
            pe.wait_ge(s_dg, b * TPB)
            pe.matmul(ps_z[1][:, CH - P:CH], W1r, dg[1], start=True, stop=True).then_inc(s_z, 1)
            project(1)

    def vector(dve):
        dve.wait_ge(*x_ready(c, layer))
        with dve.Fori(1, NCH // 2 + 1) as i:
            for u in range(2):
                dve.tensor_tensor(sq[u], c.X[:, ds(i * (2 * CH) + (u - 2) * CH, CH)],
                                  c.X[:, ds(i * (2 * CH) + (u - 2) * CH, CH)], ALU.mult).then_inc(s_sq, 1)
            for u in range(2):
                dve.wait_ge(s_ss, i * 2 + (u - 1))
                dve.tensor_scalar(mx[u], ps_sq[u][:, :], 1e-12, None, ALU.max).then_inc(s_mx, 1)
            for u in range(2):
                dve.wait_ge(s_rs, i * 2 + (u - 1))
                dve.tensor_tensor(N[:, ds(i * (2 * CH) + (u - 2) * CH, CH)], c.X[:, ds(i * (2 * CH) + (u - 2) * CH, CH)],
                                  rs[u], ALU.mult).then_inc(s_n, 1)
            dve.wait_ge(s_n, i * 2)
        dve.wait_ge(s_n, NCH)
        with dve.Fori(1, BATCH + 1) as b:
            def chunk_x(h):
                dve.tensor_copy(xs[h], c.X[:, ds(b * SEQ + (h * CH - SEQ), CH)]).then_inc(s_r, 1)

            def load_tile(r):
                dve.tensor_copy(nt[r % 2], N[:, ds(b * SEQ + (r * P - SEQ), P)]).then_inc(s_nt, 1)

            def softplus(h):
                dve.wait_ge(s_zb, b * 2 + (h - 1))
                dve.tensor_scalar(az[h], z[h], 0.0, None, ALU.max).then_inc(s_az, 1)
                dve.wait_ge(s_lz, b * 2 + (h - 1))
                dve.wait_ge(s_r, b * 2 + (h - 1))
                dve.wait_ge(s_az, b * 2 + (h - 1))
                dve.tensor_tensor(sp[h], az[h], lz[h], ALU.add).then_inc(s_sp, 1)

            def finish(h):
                dve.wait_ge(s_o, b * 2 + (h - 1))
                dve.tensor_tensor(c.Y[:, ds(b * SEQ + (h * CH - SEQ), CH)], xs[h], ps_o[h][:, :], ALU.add).then_inc(s_y, 1)
            chunk_x(0)
            chunk_x(1)
            load_tile(0)
            load_tile(1)
            for r in range(TPB):
                dve.wait_ge(s_cnt, b * TPB + (r + 1 - TPB))
                dve.tensor_scalar(dg[r % 2], c.ident, cnt[r % 2], None, ALU.mult).then_inc(s_dg, 1)
                if r + 2 < TPB:
                    load_tile(r + 2)
                if r == TPC:
                    softplus(0)
            softplus(1)
            finish(0)
            finish(1)
            dve.wait_ge(s_y, b * 2)

    def scalar(act):
        act.preload_act_table_set(LN_EXP)
        with act.Fori(1, NCH // 2 + 1) as i:
            for u in range(2):
                act_wait(act, s_mx, i * 2 + (u - 1))
                act.activation(sd[u], mx[u], ACT.Ln).then_inc(s_sd, 1)
            for u in range(2):
                act_wait(act, s_sd, i * 2 + (u - 1))
                act.activation(rs[u], sd[u], ACT.Exp, scale=-0.5).then_inc(s_rs, 1)
        with act.Fori(1, BATCH + 1) as b:
            def softplus(h):
                act_wait(act, s_z, b * TPB + (h + 1) * TPC - TPB)
                act.activation(z[h], ps_z[h][:, :], ACT.Identity, bias=b1).then_inc(s_zb, 1)
                act_wait(act, s_zb, b * 2 + (h - 1))
                act.activation(ez[h], z[h], ACT.Abs).then_inc(s_ez, 1)
                act_wait(act, s_ez, b * 4 + (2 * h - 3))
                act.activation(ez[h], ez[h], ACT.Exp, scale=-1.0).then_inc(s_ez, 1)
                act_wait(act, s_ez, b * 4 + (2 * h - 2))
                act.activation(lz[h], ez[h], ACT.Ln, bias=1.0).then_inc(s_lz, 1)
            for r in range(TPB):
                act_wait(act, s_sim, b * TPB + (r + 1 - TPB))
                act.activation(relu[r % 2], c.psum[:, (r % 2) * SEQ:(r % 2) * SEQ + SEQ], ACT.Relu, accum_out=cnt[r % 2]).then_inc(s_cnt, 1)
                if r == TPC:
                    softplus(0)
            softplus(1)

    return dict(sync=sync, tensor=tensor, vector=vector, scalar=scalar, done=(s_y, NCH))


def binary_ffn_layer(c, d, layer):
    HC = 4
    place = Places(c, c.free_at)
    w1, w2 = place(HC, P), place(HC * P)
    s1, s2 = place(HC, P), place(HC * P)
    al1, al2 = place(HC), place(1)
    w1T, w2T = place(HC, P), place(HC, P)
    b1, b2 = place(HC), place(1)
    g = [[place(CH) for _ in range(HC)] for _ in range(2)]
    xs = [place(CH) for _ in range(2)]
    ps_t = c.bank[6:8]
    ps_h = c.bank[0:4]
    ps_o = c.bank[4:6]
    take = c.layer_sems(layer)
    S = lambda n: take("bin_" + n)
    s_w, s_sg, s_b, s_t, s_tc, s_h, s_g, s_o, s_y = [S(n) for n in ("w", "sg", "b", "t", "tc", "h", "g", "o", "y")]

    def sync(sp):
        sp.wait_ge(*x_ready(c, layer))
        sp.dma_start(w1, d["L0_ffn_w1"].rearrange("(c p) d -> p c d", p=P)).then_inc(s_w, 16)
        sp.dma_start(w2, d["L0_ffn_w2"]).then_inc(s_w, 16)
        sp.dma_start(b1, d["L0_ffn_b1"]).then_inc(s_w, 16)
        sp.dma_start(b2, d["L0_ffn_b2"]).then_inc(s_w, 16)

    def vector(dve):
        dve.wait_ge(*x_ready(c, layer))
        dve.wait_ge(s_w, 64)
        dve.tensor_reduce(al1, w1, AX.X, ALU.add, apply_absolute_value=True).then_inc(s_b, 1)
        dve.tensor_reduce(al2, w2, AX.X, ALU.add, apply_absolute_value=True).then_inc(s_b, 1)
        dve.wait_ge(s_b, 2)
        dve.tensor_scalar(al1, al1, 1.0 / P, None, ALU.mult).then_inc(s_b, 1)
        dve.tensor_scalar(al2, al2, 1.0 / (HC * P), None, ALU.mult).then_inc(s_b, 1)
        dve.wait_ge(s_b, 4)
        dve.wait_ge(s_sg, 2)
        for k in range(HC):
            dve.scalar_tensor_tensor(s1[:, k, :], s1[:, k, :], al1[:, k:k + 1], w1[:, k, :],
                                     ALU.mult, ALU.subtract).then_inc(s_b, 1)
        dve.scalar_tensor_tensor(s2, s2, al2, w2, ALU.mult, ALU.subtract).then_inc(s_b, 1)
        dve.wait_ge(s_b, 5 + HC)
        dve.tensor_tensor(s1, s1, w1, ALU.add).then_inc(s_b, 1)
        dve.tensor_tensor(s2, s2, w2, ALU.add).then_inc(s_b, 1)
        dve.wait_ge(s_t, 1)
        dve.tensor_copy(w1T.rearrange("p c n -> p (c n)"), ps_t[0]).then_inc(s_tc, 1)
        dve.wait_ge(s_t, 2)
        dve.tensor_copy(w2T.rearrange("p c n -> p (c n)"), ps_t[1]).then_inc(s_tc, 1)
        with dve.Fori(1, NCH // 2 + 1) as i:
            for u in range(2):
                dve.wait_ge(s_o, i * 2 + (u - 1))
                dve.scalar_tensor_tensor(c.Y[:, ds(i * (2 * CH) + (u - 2) * CH, CH)], ps_o[u], b2,
                                         c.X[:, ds(i * (2 * CH) + (u - 2) * CH, CH)], ALU.add, ALU.add).then_inc(s_y, 1)
            dve.wait_ge(s_y, i * 2)

    def scalar(act):
        act.wait_ge(s_w, 64)
        act.activation(s1, w1, ACT.Sign).then_inc(s_sg, 1)
        act.activation(s2, w2, ACT.Sign).then_inc(s_sg, 1)
        with act.Fori(1, NCH // 2 + 1) as i:
            for u in range(2):
                for k in range(HC):
                    act_wait(act, s_h, i * (2 * HC) + (u * HC + k + 1 - 2 * HC))
                    act.activation(g[u][k], ps_h[k], ACT.Gelu, bias=b1[:, k:k + 1]).then_inc(s_g, 1)

    def tensor(pe):
        pe.wait_ge(s_b, 7 + HC)
        pe.wait_ge(c.s_ident, 1)
        for k in range(HC):
            mm = pe.transpose(ps_t[0][:, k * P:k * P + P], s1[:, k, :], c.ident)
        mm.then_inc(s_t, 1)
        for k in range(HC):
            mm = pe.transpose(ps_t[1][:, k * P:k * P + P], s2[:, k * P:k * P + P], c.ident)
        mm.then_inc(s_t, 1)
        pe.wait_ge(s_tc, 2)

        def down(i, u):
            for k in range(HC):
                pe.wait_ge(s_g, i * (2 * HC) + (u * HC + k + 1 - 2 * HC))
                mm = pe.matmul(ps_o[u], w2T[:, k, :], g[u][k], start=(k == 0), stop=(k == HC - 1))
            mm.then_inc(s_o, 1)
        with pe.Fori(1, NCH // 2 + 1) as i:
            for u in range(2):
                for k in range(HC):
                    pe.matmul(ps_h[k], w1T[:, k, :], c.X[:, ds(i * (2 * CH) + (u - 2) * CH, CH)],
                              start=True, stop=True).then_inc(s_h, 1)
                down(i, u)
            pe.wait_ge(s_y, i * 2)

    return dict(sync=sync, tensor=tensor, vector=vector, scalar=scalar, done=(s_y, NCH))


def ternary_ffn_layer(c, d, layer):
    HC = 4
    place = Places(c, c.free_at)
    w1, w2 = place(HC, P), place(HC * P)
    q1, q2 = place(HC, P), place(HC * P)
    n1, n2 = place(HC, P), place(HC * P)
    ga = place(4)
    gm, rg = place(2), place(2)
    w1T, w2T, w2s = place(HC, P), place(HC, P), place(HC, P)
    lnw, lnb = place(HC), place(HC)
    wb = place(1)
    meanh = place(P)
    g = [place(CH) for _ in range(HC)]
    gc = [[place(CH) for _ in range(HC)] for _ in range(2)]
    sq = [place(CH) for _ in range(HC)]
    sd, rs, tmp = place(CH), place(CH), place(CH)
    ps_h = c.bank[0:4]
    ps_mu, ps_var, ps_o, ps_t = c.bank[4], c.bank[5], c.bank[6], c.bank[7]
    take = c.layer_sems(layer)
    S = lambda n: take("ter_" + n)
    s_w, s_a, s_gs, s_q, s_t, s_tc, s_h, s_g, s_mu, s_gc, s_sq, s_var, s_sd, s_o, s_rs, s_y = [S(n) for n in (
        "w", "a", "gs", "q", "t", "tc", "h", "g", "mu", "gc", "sq", "var", "sd", "o", "rs", "y")]

    def sync(sp):
        sp.wait_ge(*x_ready(c, layer))
        sp.dma_start(w1, d["L1_ffn_W_fc"].rearrange("(c p) d -> p c d", p=P)).then_inc(s_w, 16)
        sp.dma_start(w2, d["L1_ffn_W_proj"]).then_inc(s_w, 16)
        sp.dma_start(lnw, d["L1_ffn_ln_w"]).then_inc(s_w, 16)
        sp.dma_start(lnb, d["L1_ffn_ln_b"]).then_inc(s_w, 16)

    def vector(dve):
        dve.wait_ge(*x_ready(c, layer))
        dve.memset(meanh, 1.0 / (HC * P)).then_inc(s_a, 1)
        dve.wait_ge(s_w, 64)
        dve.tensor_reduce(ga[:, 0:1], w1, AX.XY, ALU.add, apply_absolute_value=True).then_inc(s_a, 1)
        dve.tensor_reduce(ga[:, 1:2], w2, AX.X, ALU.add, apply_absolute_value=True).then_inc(s_a, 1)
        dve.wait_ge(s_gs, 1)
        dve.tensor_scalar(gm, ps_t[:, 0:2], 1.0 / (HC * P * P), 1e-6, ALU.mult, ALU.add).then_inc(s_q, 1)
        dve.wait_ge(s_q, 1)
        dve.reciprocal(rg, gm).then_inc(s_q, 1)
        dve.wait_ge(s_q, 2)
        dve.tensor_scalar(n1, w1, rg[:, 0:1], -0.5, ALU.mult, ALU.is_lt).then_inc(s_q, 1)
        dve.tensor_scalar(n2, w2, rg[:, 1:2], -0.5, ALU.mult, ALU.is_lt).then_inc(s_q, 1)
        dve.tensor_scalar(q1, w1, rg[:, 0:1], 0.5, ALU.mult, ALU.is_gt).then_inc(s_q, 1)
        dve.tensor_scalar(q2, w2, rg[:, 1:2], 0.5, ALU.mult, ALU.is_gt).then_inc(s_q, 1)
        dve.wait_ge(s_q, 6)
        dve.tensor_tensor(q1, q1, n1, ALU.subtract).then_inc(s_q, 1)
        dve.tensor_tensor(q2, q2, n2, ALU.subtract).then_inc(s_q, 1)
        dve.wait_ge(s_t, 1)
        dve.tensor_copy(w1T.rearrange("p c n -> p (c n)"), ps_h[0]).then_inc(s_tc, 1)
        dve.tensor_copy(w2T.rearrange("p c n -> p (c n)"), ps_h[1]).then_inc(s_tc, 1)
        dve.wait_ge(s_tc, 2)
        for k in range(HC):
            dve.tensor_scalar(w2s[:, k, :], w2T[:, k, :], lnw[:, k:k + 1], None, ALU.mult).then_inc(s_tc, 1)
        dve.wait_ge(s_t, 2)
        dve.tensor_copy(wb, ps_t[:, 4:5]).then_inc(s_tc, 1)
        dve.wait_ge(s_tc, 3 + HC)
        with dve.Fori(1, NCH + 1) as i:
            dve.wait_ge(s_mu, i)
            for k in range(HC):
                dve.tensor_tensor(gc[0][k], g[k], ps_mu, ALU.subtract).then_inc(s_gc, 1)
            dve.wait_ge(s_rs, i)
            dve.wait_ge(s_o, i)
            dve.tensor_tensor(tmp, ps_o, rs, ALU.mult).then_inc(s_tmp, 1)
            dve.wait_ge(s_tmp, i)
            dve.scalar_tensor_tensor(c.Y[:, ds(i * CH - CH, CH)], tmp, wb, c.X[:, ds(i * CH - CH, CH)],
                                     ALU.add, ALU.add).then_inc(s_y, 1)
            dve.wait_ge(s_y, i)

    s_tmp = S("tmp")

    def scalar(act):
        with act.Fori(1, NCH + 1) as i:
            for k in range(HC):
                act_wait(act, s_h, i * HC + (k + 1 - HC))
                act.activation(g[k], ps_h[k], ACT.Gelu).then_inc(s_g, 1)
            for k in range(HC):
                act_wait(act, s_gc, i * HC + (k + 1 - HC))
                act.activation(sq[k], gc[0][k], ACT.Square).then_inc(s_sq, 1)
            act_wait(act, s_var, i)
            act.activation(sd, ps_var, ACT.Ln, bias=c.eps5).then_inc(s_sd, 1)
            act_wait(act, s_sd, i)
            act.activation(rs, sd, ACT.Exp, scale=-0.5).then_inc(s_rs, 1)

    def tensor(pe):
        pe.wait_ge(s_a, 3)
        pe.matmul(ps_t[:, 0:2], c.ones, ga[:, 0:2], start=True, stop=True).then_inc(s_gs, 1)
        pe.wait_ge(s_q, 8)
        for k in range(HC):
            pe.transpose(ps_h[0][:, k * P:k * P + P], q1[:, k, :], c.ident)
        for k in range(HC):
            mm = pe.transpose(ps_h[1][:, k * P:k * P + P], q2[:, k * P:k * P + P], c.ident)
        mm.then_inc(s_t, 1)
        pe.wait_ge(s_tc, 2)
        for k in range(HC):
            mm = pe.matmul(ps_t[:, 4:5], w2T[:, k, :], lnb[:, k:k + 1], start=(k == 0), stop=(k == HC - 1))
        mm.then_inc(s_t, 1)
        pe.wait_ge(s_tc, 3 + HC)
        with pe.Fori(1, NCH + 1) as i:
            for k in range(HC):
                pe.matmul(ps_h[k], w1T[:, k, :], c.X[:, ds(i * CH - CH, CH)], start=True, stop=True).then_inc(s_h, 1)
            for k in range(HC):
                pe.wait_ge(s_g, i * HC + (k + 1 - HC))
                mm = pe.matmul(ps_mu, meanh, g[k], start=(k == 0), stop=(k == HC - 1))
            mm.then_inc(s_mu, 1)
            for k in range(HC):
                pe.wait_ge(s_gc, i * HC + (k + 1 - HC))
                mm = pe.matmul(ps_o, w2s[:, k, :], gc[0][k], start=(k == 0), stop=(k == HC - 1))
            mm.then_inc(s_o, 1)
            for k in range(HC):
                pe.wait_ge(s_sq, i * HC + (k + 1 - HC))
                mm = pe.matmul(ps_var, meanh, sq[k], start=(k == 0), stop=(k == HC - 1))
            mm.then_inc(s_var, 1)

    return dict(sync=sync, tensor=tensor, vector=vector, scalar=scalar, done=(s_y, NCH))


def expert_ffn_layer(c, d, layer):
    E, HC = 4, 4
    place = Places(c, c.free_at)
    w1 = place(E, HC * P)
    w2 = place(E * HC, P)
    b1, b2 = place(E * HC), place(E)
    wu, bu = place(1), place(1)
    wur = place(P)
    h = [place(CH) for _ in range(8)]
    u_ = place(CH)
    ui = place(E, CH)
    we = [place(E, CH) for _ in range(2)]
    ye = [place(CH) for _ in range(2)]
    acc = place(CH)
    ps_h = c.bank[0:4]
    ps_o = c.bank[4:6]
    ps_u = c.bank[6]
    take = c.layer_sems(layer)
    S = lambda n: take("exp_" + n)
    s_w, s_wu, s_u, s_us, s_ui, s_we, s_h, s_r, s_o, s_ye, s_ac, s_y = [S(n) for n in (
        "w", "wu", "u", "us", "ui", "we", "h", "r", "o", "ye", "ac", "y")]

    def sync(sp):
        sp.wait_ge(*x_ready(c, layer))
        sp.dma_start(w1, d["L2_ffn_W1"].rearrange("e p f -> p e f")).then_inc(s_w, 16)
        sp.dma_start(w2, d["L2_ffn_W2"].rearrange("e (c p) n -> p (e c) n", p=P)).then_inc(s_w, 16)
        sp.dma_start(b1, d["L2_ffn_b1"]).then_inc(s_w, 16)
        sp.dma_start(b2, d["L2_ffn_b2"]).then_inc(s_w, 16)
        sp.dma_start(wu, d["L2_ffn_Wu"]).then_inc(s_w, 16)
        sp.dma_start(bu, d["L2_ffn_bu"]).then_inc(s_w, 16)

    def vector(dve):
        dve.wait_ge(*x_ready(c, layer))
        dve.wait_ge(s_w, 96)
        dve.tensor_scalar(wur, c.ones, wu, None, ALU.mult).then_inc(s_wu, 1)
        with dve.Fori(1, NCH + 1) as i:
            dve.wait_ge(s_us, i)
            for r in range(E):
                dve.tensor_scalar(ui[:, r, :], u_, 1.0 / (r + 1), None, ALU.mult).then_inc(s_ui, 1)
            dve.wait_ge(s_ui, i * E)
            for pos in range(E):
                for r in range(E):
                    e = (pos + r) % E
                    mm = dve.scalar_tensor_tensor(we[0][:, e, pos::E], u_[:, pos::E], r / E if r else -1.0,
                                                  ui[:, r, pos::E], ALU.is_gt, ALU.mult)
            mm.then_inc(s_we, 1)
            dve.wait_ge(s_we, i)
            for e in range(E):
                dve.wait_ge(s_o, i * E + (e + 1 - E))
                out = acc if e == 0 else ye[e % 2]
                dve.scalar_tensor_tensor(out, ps_o[e % 2], b2[:, e:e + 1], we[0][:, e, :],
                                         ALU.add, ALU.mult).then_inc(s_ye, 1)
                dve.wait_ge(s_ye, i * E + (e + 1 - E))
                if e:
                    dve.tensor_tensor(acc, acc, ye[e % 2], ALU.add).then_inc(s_ac, 1)
                    dve.wait_ge(s_ac, i * (E - 1) + (e + 1 - E))
            dve.tensor_tensor(c.Y[:, ds(i * CH - CH, CH)], acc, c.X[:, ds(i * CH - CH, CH)], ALU.add).then_inc(s_y, 1)
            dve.wait_ge(s_y, i)

    def scalar(act):
        with act.Fori(1, NCH + 1) as i:
            act_wait(act, s_u, i)
            act.activation(u_, ps_u, ACT.Sigmoid, bias=bu).then_inc(s_us, 1)
            for n in range(E * HC):
                act_wait(act, s_h, i * (E * HC) + (n + 1 - E * HC))
                act.activation(h[n % 8], ps_h[n % 4], ACT.Relu, bias=b1[:, n:n + 1]).then_inc(s_r, 1)

    def tensor(pe):
        pe.wait_ge(s_wu, 1)
        with pe.Fori(1, NCH + 1) as i:
            pe.matmul(ps_u, wur, c.X[:, ds(i * CH - CH, CH)], start=True, stop=True).then_inc(s_u, 1)

            def up(e):
                for k in range(HC):
                    n = e * HC + k
                    pe.matmul(ps_h[n % 4], w1[:, e, k * P:k * P + P], c.X[:, ds(i * CH - CH, CH)],
                              start=True, stop=True).then_inc(s_h, 1)

            def down(e):
                for k in range(HC):
                    n = e * HC + k
                    pe.wait_ge(s_r, i * (E * HC) + (n + 1 - E * HC))
                    if k == 0 and e >= 2:
                        pe.wait_ge(s_ye, i * E + (e - 1 - E))
                    mm = pe.matmul(ps_o[e % 2], w2[:, n, :], h[n % 8], start=(k == 0), stop=(k == HC - 1))
                mm.then_inc(s_o, 1)
            for e in range(E):
                up(e)
                down(e)
            pe.wait_ge(s_ye, i * E)

    return dict(sync=sync, tensor=tensor, vector=vector, scalar=scalar, done=(s_y, NCH))


def outer_attention_layer(c, d, layer):
    H, C, Q = 16, 64, 8
    HC = H * C
    NT = T // P
    ORDER = [7, 5, 3, 1, 6, 4, 2, 0]
    NB = len(ORDER)
    LONG = (0, 4)
    BY_ROWS = 8
    width = [Q * (b + 1) for b in ORDER]
    SLOT = [0, 2, 3, 4, 1, 2, 3, 4]
    FREE = [4, 5, 6, 7, 8, 9, 10, 11]
    place = Places(c, c.norm_at)
    early = Places(c, T)
    slots = [place(H * Q * max(width[k] for k in range(NB) if SLOT[k] == s)) for s in range(5)]
    wqkv = place(3, HC)
    wo = place(HC // P, P)
    bias = place(HC)
    kqv = [place(3, HC) for _ in range(2)]
    nmax = [place(HC) for _ in range(2)]
    kmin = place(HC)
    attT = kmin.rearrange("p (a b) -> p a b", b=P)
    xt = [place(P) for _ in range(2)]
    den = [place(HC) for _ in range(2)]
    bo = place(1)
    own = {s: early(H * Q * Q) for s in (2, 3, 4)}
    resets = early(HC)
    rmax = resets[:, 0:HC // 2].bitcast(mybir.dt.bfloat16)
    rmin = resets[:, HC // 2:HC].bitcast(mybir.dt.bfloat16)
    ps_p = c.bank[0:2] + c.bank[6:8]
    ps_n = c.bank[2:4]
    ps_d = c.bank[4:6]
    ps_t = c.psum[:, 6 * 512:8 * 512]
    ps_o = c.bank[6][:, 0:P]
    take = c.layer_sems(layer)
    S = lambda n: take("att_" + n)
    (s_w, s_rst, s_xt, s_pj, s_kqv, s_cm, s_mx, s_nm, s_s, s_sub, s_e, s_d, s_pv, s_pvp, s_r, s_ds, s_ld, s_rd, s_at,
     s_tr, s_trc, s_wo, s_y, s_own) = [S(n) for n in (
         "w", "rst", "xt", "pj", "kqv", "cm", "mx", "nm", "s", "sub", "e", "d", "pv", "pvp", "r", "ds", "ld", "rd", "at",
         "tr", "trc", "wo", "y", "own")]
    K_, Q_, V_ = 0, 1, 2
    SUMS = {}
    for k in [k for k in range(NB) if k not in LONG]:
        SUMS[k] = max(SUMS.values(), default=0) + (2 if ORDER[k] else 1)
    PV = max(SUMS.values())

    def scores(k):
        w = width[k]
        return slots[SLOT[k]][:, 0:H * Q * w].rearrange("p (h q k) -> p h q k", h=H, q=Q)

    def mixed(v, k):
        return v[:, BY_ROWS:H] if k in LONG else v

    def own_keys(k):
        return own[SLOT[k]].rearrange("p (h q k) -> p h q k", h=H, q=Q)

    def heads(v):
        return v.rearrange("p (h c) -> p h c", h=H)

    def over_keys(v, k):
        b = ORDER[k]
        return heads(v)[:, :, b * Q:b * Q + Q].unsqueeze(3).to_broadcast([P, H, Q, width[k]])

    def over_queries(v, k, lo, hi):
        return heads(v)[:, :, lo:hi].unsqueeze(2).to_broadcast([P, H, Q, hi - lo])

    def half_of(v, f):
        return v.rearrange("p (h b f q) -> p h b f q", h=H, b=4, f=2)[:, :, :, 1 - f, :]

    def half_bank(bank):
        return bank.rearrange("p (b h q) -> p h b q", b=4, h=H)

    def tiles(eng, one):
        one(0, 0, True, False)
        with eng.Fori(1, NT // 2) as i:
            one(i * 2 - 1, 1, False, False)
            one(i * 2, 0, False, False)
        one(NT - 1, 1, False, True)

    def sync(sp):
        sp.wait_ge(*x_ready(c, layer))
        for n, (w, b) in enumerate((("Wk", "bk"), ("Wq", "bq"), ("Wv", "bv"))):
            sp.dma_start(wqkv[:, n, :], d["L1_attn_" + w]).then_inc(s_w, 16)
            sp.dma_start(bias[32 * n:32 * n + 1, :], d["L1_attn_" + b]).then_inc(s_w, 16)
        sp.dma_start(wo, d["L1_attn_Wo"].rearrange("(c p) n -> p c n", p=P)).then_inc(s_w, 16)
        sp.dma_start(bo, d["L1_attn_bo"]).then_inc(s_w, 16)

    def vector(dve):
        def row_maxima(n, u):
            dve.wait_ge(s_kqv, n * 6 + 4)
            dve.tensor_tensor_scan(nmax[u], rmax, kqv[u][:, K_, :], -BIG, ALU.add, ALU.max).then_inc(s_cm, 1)
            dve.tensor_tensor_scan(kmin, rmin, kqv[u][:, K_, :], BIG, ALU.add, ALU.min).then_inc(s_cm, 1)
            dve.wait_ge(s_cm, n * 2 + 2)
            for v in (nmax[u], kmin):
                dve.scalar_tensor_tensor(v, v, -1.0, kqv[u][:, Q_, :], ALU.mult, ALU.mult).then_inc(s_mx, 1)
            dve.wait_ge(s_mx, n * 2 + 2)
            dve.tensor_tensor(nmax[u], nmax[u], kmin, ALU.min).then_inc(s_nm, 1)

        def finish_sums(n, u, f):
            dve.wait_ge(s_r, n * NB + (NB + 4 * f + 4))
            at, add = half_of(den[u], f), half_bank(ps_d[f])
            if f:
                dve.tensor_copy(at[:, :, 0, :], add[:, :, 0, :]).then_inc(s_ds, 1)
            dve.tensor_tensor(at[:, :, f:4, :], at[:, :, f:4, :], add[:, :, f:4, :], ALU.add).then_inc(s_ds, 1)

        def finish_half(n, u, f):
            dve.wait_ge(s_rd, n * 2 + (f + 1))
            dve.tensor_tensor(half_of(den[u], f), half_of(den[u], f), half_bank(ps_n[f]), ALU.mult).then_inc(s_at, 1)

        def take_output(n):
            dve.wait_ge(s_wo, n + 1)
            col = ds(n * P, P)
            dve.scalar_tensor_tensor(c.X[:, col], ps_o, bo, c.X[:, col], ALU.add, ALU.add).then_inc(s_y, 1)

        def tile(n, u, first, last):
            def subtract(k):
                dve.wait_ge(s_s, n * NB + (k + 1))
                s = mixed(scores(k), k)
                dve.tensor_tensor(s, s, mixed(over_keys(nmax[u], k), k), ALU.add).then_inc(s_sub, 1)

            def add_exp(k):
                b = ORDER[k]
                dve.wait_ge(s_e, n * NB + (k + 1))
                dve.tensor_reduce(heads(den[u])[:, :, b * Q:b * Q + Q], scores(k)[:, :, :, 0:width[k] - Q], AX.X,
                                  ALU.add).then_inc(s_d, 1)

            def weigh(k):
                b, w = ORDER[k], width[k]
                v = kqv[u][:, V_, :]
                if b:
                    add_exp(k)
                else:
                    dve.wait_ge(s_e, n * NB + (k + 1))
                dve.tensor_tensor(own_keys(k), scores(k)[:, :, :, w - Q:w], over_queries(v, k, w - Q, w),
                                  ALU.mult).then_inc(s_pv, 1)
                if b:
                    dve.wait_ge(s_d, n * (NB - 1) + (k + 1))
                    before = scores(k)[:, :, :, 0:w - Q]
                    dve.tensor_tensor(before, before, over_queries(v, k, 0, w - Q), ALU.mult).then_inc(s_pv, 1)

            if not last:
                dve.tensor_copy(xt[1 - u], c.X[:, ds(n * P + P, P)]).then_inc(s_xt, 1)
            if first:
                row_maxima(0, 0)
            dve.wait_ge(s_nm, n + 1)
            subtract(0)
            subtract(1)
            subtract(2)
            add_exp(0)
            weigh(1)
            if not first:
                finish_sums(n - 1, 1 - u, 1)
            subtract(3)
            weigh(2)
            if not first:
                finish_half(n - 1, 1 - u, 1)
            weigh(3)
            if not last:
                row_maxima(n + 1, 1 - u)
            subtract(4)
            subtract(5)
            subtract(6)
            add_exp(4)
            weigh(5)
            finish_sums(n, u, 0)
            weigh(6)
            finish_half(n, u, 0)
            subtract(7)
            weigh(7)
            if not first:
                take_output(n - 1)

        dve.wait_ge(*x_ready(c, layer))
        dve.memset(resets, 0.0).then_inc(s_rst, 1)
        dve.wait_ge(s_rst, 1)
        dve.memset(heads(rmax)[:, :, 0:1], -BIG).then_inc(s_rst, 1)
        dve.memset(heads(rmin)[:, :, 0:1], BIG).then_inc(s_rst, 1)
        dve.tensor_copy(xt[0], c.X[:, 0:P]).then_inc(s_xt, 1)
        dve.wait_ge(s_rst, 3)
        tiles(dve, tile)
        finish_sums(NT - 1, 1, 1)
        finish_half(NT - 1, 1, 1)
        take_output(NT - 1)

    def gpsimd(pool):
        def tile(n, u, first, last):
            def score(k):
                pool.wait_ge(s_r, n * NB + FREE[k])
                pool.tensor_tensor(mixed(scores(k), k), mixed(over_keys(kqv[u][:, Q_, :], k), k),
                                   mixed(over_queries(kqv[u][:, K_, :], k, 0, width[k]), k), ALU.mult).then_inc(s_s, 1)

            def weigh(k):
                w, v = width[k], kqv[u][:, V_, :]
                pool.wait_ge(s_d, n * (NB - 1) + (k + 1))
                before = scores(k)[:, :, :, 0:w - Q]
                pool.tensor_tensor(before, before, over_queries(v, k, 0, w - Q), ALU.mult).then_inc(s_pvp, 1)

            def weigh_own(n, u, k):
                w, v = width[k], kqv[u][:, V_, :]
                pool.wait_ge(s_own, n * len(LONG) + (3 + k // 4))
                own_k = scores(k)[:, :, :, w - Q:w]
                pool.tensor_tensor(own_k, own_k, over_queries(v, k, w - Q, w), ALU.mult).then_inc(s_pvp, 1)
            pool.wait_ge(s_kqv, n * 6 + 4)
            score(0)
            score(1)
            score(2)
            if not first:
                weigh_own(n - 1, 1 - u, 4)
            score(3)
            score(4)
            weigh(0)
            score(5)
            score(6)
            weigh_own(n, u, 0)
            score(7)
            weigh(4)
            if last:
                weigh_own(n, u, 4)
        pool.wait_ge(*x_ready(c, layer))
        for k in LONG:
            pool.memset(scores(k)[:, 0:BY_ROWS, :, width[k] - Q:width[k]], 0.0).then_inc(s_own, 1)
        tiles(pool, tile)

    def scalar(act):
        def copies(n, u, lo=0, hi=6):
            for piece in range(lo, hi):
                act_wait(act, s_pj, n * 6 + (piece + 1))
                part, half = piece // 2, piece % 2
                act.activation(kqv[u][:, part, half * 512:half * 512 + 512], ps_p[piece % 4], ACT.Copy,
                               scale=C ** -0.5 if part == Q_ else 1.0).then_inc(s_kqv, 1)

        def invert(n, u, f):
            act_wait(act, s_ds, n * 3 + (2 * f + 1))
            act.activation(half_of(den[u], f), half_of(den[u], f), ACT.Ln).then_inc(s_ld, 1)
            act_wait(act, s_ld, n * 2 + (f + 1))
            act.activation(half_of(den[u], f), half_of(den[u], f), ACT.Exp, scale=-1.0).then_inc(s_rd, 1)

        def take_transposed(n):
            act_wait(act, s_tr, n * 2 + 2)
            act.activation(attT.rearrange("p a b -> p (a b)"), ps_t, ACT.Copy).then_inc(s_trc, 1)

        def tile(n, u, first, last):
            def rows(k):
                b = ORDER[k]
                q, k_, p = kqv[u][:, Q_, :], kqv[u][:, K_, :], scores(k)
                if k == 0:
                    act_wait(act, s_nm, n + 1)
                act_wait(act, s_r, n * NB + FREE[k])
                for h in range(BY_ROWS):
                    for j in range(Q):
                        row = h * C + b * Q + j
                        keys = b * Q + j + 1
                        act.activation(p[:, h, j, 0:keys], k_[:, h * C:h * C + keys], ACT.Exp,
                                       scale=q[:, row:row + 1], bias=nmax[u][:, row:row + 1])

            def exp(k):
                act_wait(act, s_sub, n * NB + (k + 1))
                act.activation(mixed(scores(k), k), mixed(scores(k), k), ACT.Exp).then_inc(s_e, 1)

            rows(0)
            exp(0)
            exp(1)
            if not last:
                copies(n + 1, 1 - u, 0, 4)
            exp(2)
            if not last:
                copies(n + 1, 1 - u, 4, 6)
            if not first:
                invert(n - 1, 1 - u, 1)
            exp(3)
            rows(4)
            exp(4)
            exp(5)
            if not first:
                if not last:
                    act_wait(act, s_nm, n + 2)
                take_transposed(n - 1)
            exp(6)
            invert(n, u, 0)
            exp(7)

        act.preload_act_table_set(LN_EXP)
        act.wait_ge(s_own, 2)
        copies(0, 0)
        tiles(act, tile)
        invert(NT - 1, 1, 1)
        take_transposed(NT - 1)

    def tensor(pe):
        def project(n, u, behind):
            pe.wait_ge(s_xt, n + 1)
            for piece in range(6):
                part, half = piece // 2, piece % 2
                if piece < 2 and behind >= 1:
                    pe.wait_ge(s_kqv, n * 6 + (piece - 1))
                if piece == 2 and behind >= 2:
                    pe.wait_ge(s_y, n - 1)
                if piece >= 4:
                    pe.wait_ge(s_kqv, n * 6 + (piece - 3))
                rows = slice(32 * part, 32 * part + 1)
                pe.matmul(ps_p[piece % 4], c.ones[rows, :], bias[rows, half * 512:half * 512 + 512], start=True, stop=False)
                pe.matmul(ps_p[piece % 4], xt[u], wqkv[:, part, half * 512:half * 512 + 512],
                          start=False, stop=True).then_inc(s_pj, 1)

        def transpose(n, u):
            pe.wait_ge(s_at, n * 2 + 2)
            pe.wait_ge(s_y, n + 1)
            for j in range(HC // P):
                mm = pe.transpose(ps_t[:, j * P:j * P + P], den[u][:, j * P:j * P + P], c.ident)
                if j % 4 == 3:
                    mm.then_inc(s_tr, 1)

        def output(n):
            pe.wait_ge(s_trc, n + 1)
            for j in range(HC // P):
                mm = pe.matmul(ps_o, wo[:, j, :], attT[:, j, :], start=(j == 0), stop=(j == HC // P - 1))
            mm.then_inc(s_wo, 1)

        def tile(n, u, first, last):
            def own_sums(bank, k, v, more):
                at = bank[:, (ORDER[k] // 2) * P:(ORDER[k] // 2) * P + P].rearrange("p (h q) -> p h q", h=H)
                for j in range(Q):
                    mm = pe.matmul(at[:, :, j:Q], c.ident, v[:, :, j:Q, j], start=(j == 0 and not more),
                                   stop=(j == Q - 1))
                return mm

            def sums(k):
                b, w, f = ORDER[k], width[k], k // 4
                if k in LONG:
                    pe.wait_ge(s_e, n * NB + (k + 1))
                    own_sums(ps_d[f], k, scores(k)[:, :, :, w - Q:w], False).then_inc(s_own, 1)
                    pe.wait_ge(s_pvp, n * 4 + (2 * f + 1))
                else:
                    pe.wait_ge(s_pv, n * PV + SUMS[k])
                    own_sums(ps_d[f], k, scores(k)[:, :, :, w - Q:w], False)
                v = scores(k).rearrange("p h q k -> p (h q) k")
                for key in range(w - Q):
                    pe.matmul(ps_n[f][:, (b // 2) * P:(b // 2) * P + P], c.ident, v[:, :, key],
                              start=(key == 0), stop=False)
                if k in LONG:
                    pe.wait_ge(s_pvp, n * 4 + (2 * f + 2))
                own_v = scores(k)[:, :, :, w - Q:w] if k in LONG else own_keys(k)
                own_sums(ps_n[f], k, own_v, b > 0).then_inc(s_r, 1)

            if not first:
                pe.wait_ge(s_at, n * 2 - 1)
            if not last:
                project(n + 1, 1 - u, 1 if first else 2)
            for k in (1, 2, 3, 0):
                sums(k)
            if not first:
                if not last:
                    pe.wait_ge(s_kqv, n * 6 + 10)
                transpose(n - 1, 1 - u)
            sums(5)
            if not first:
                output(n - 1)
            sums(6)
            sums(7)
            sums(4)

        pe.wait_ge(s_w, 128)
        pe.sem_inc(s_r, NB)
        pe.sem_inc(s_y, 1)
        project(0, 0, 0)
        tiles(pe, tile)
        transpose(NT - 1, 1)
        output(NT - 1)

    return dict(sync=sync, tensor=tensor, vector=vector, scalar=scalar, gpsimd=gpsimd, result=c.X, done=(s_y, NT + 1))


def linear_attention_layer(c, d, layer):
    G = 8
    place = Places(c, c.free_at)
    w = place(3, P)
    wfg1 = place(P)
    wf2, wg2 = place(P), place(P)
    wo = place(P)
    nw = place(1)
    sel_k = place(G, P)
    sel_v = place(G, P)
    sel_o = place(G, P)
    head_mean = place(P)
    act5 = place(5, CH)
    fg1 = place(CH)
    vrow = place(CH)
    kv = place(CH)
    st0 = place(G, CH)
    st1 = [place(CH) for _ in range(2)]
    qs = [place(CH) for _ in range(2)]
    og, sq, lv, rs, on = place(CH), place(CH), place(CH), place(CH), place(CH)
    ps_p = c.bank[0:2]
    ps_v, ps_k, ps_f, ps_q, ps_o, ps_w = c.bank[2:8]
    take = c.layer_sems(layer)
    S = lambda n: take("lin_" + n)
    (s_w, s_p, s_pa, s_vr, s_vc, s_kr, s_kv, s_fr, s_st, s_qr, s_qs, s_o, s_og, s_sq, s_ms, s_sd, s_rs, s_on, s_wo,
     s_y) = [S(n) for n in ("w", "p", "pa", "vr", "vc", "kr", "kv", "fr", "st", "qr", "qs", "o", "og", "sq", "ms",
                            "sd", "rs", "on", "wo", "y")]
    HALVES = SEQ // CH
    loads = [(w[:, 0, :], "L2_attn_Wq"), (w[:, 1, :], "L2_attn_Wk"), (w[:, 2, :], "L2_attn_Wv"), (wfg1, "Wfg1"),
             (wf2[0:16, :], "Wf2_0"), (wg2[0:16, :], "Wg2_0"), (wo, "L2_attn_Wo"), (nw, "L2_attn_norm_weight"),
             (sel_k, "sel_k"), (sel_v, "sel_v"), (sel_o, "sel_o"), (head_mean, "head_mean")]

    def sync(sp):
        sp.wait_ge(*x_ready(c, layer))
        for dst, name in loads:
            sp.dma_start(dst, d[name]).then_inc(s_w, 16)

    def chunk(b, hf):
        return b * HALVES + (hf - HALVES)

    def tensor(pe):
        pe.wait_ge(*x_ready(c, layer))
        pe.wait_ge(s_w, 16 * len(loads))
        for s in (s_vc, s_kv, s_st, s_qs, s_og):
            pe.sem_inc(s, 1)
        pe.sem_inc(s_o, 2)
        with pe.Fori(1, BATCH + 1) as b:
            for hf in range(HALVES):
                n = chunk(b, hf)
                x = c.X[:, ds(n * CH, CH)]
                for piece in range(4):
                    if piece >= 2:
                        pe.wait_ge(s_pa, n * 6 + (piece - 1))
                    if piece < 3:
                        pe.matmul(ps_p[piece % 2], w[:, piece, :], x, start=True, stop=True).then_inc(s_p, 1)
                    else:
                        pe.matmul(ps_p[1], wfg1, x, start=True, stop=True).then_inc(s_p, 1)
                pe.wait_ge(s_pa, n * 6 + 4)
                pe.matmul(ps_p[0], wf2[0:16, :], fg1[0:16, :], start=True, stop=True).then_inc(s_p, 1)
                pe.matmul(ps_p[1], wg2[0:16, :], fg1[0:16, :], start=True, stop=True).then_inc(s_p, 1)
                pe.wait_ge(s_pa, n * 6 + 6)

                def out_group(j):
                    pe.wait_ge(s_qs, n * G + (j + 2))
                    if j == 0:
                        pe.wait_ge(s_og, n + 1)
                    pe.matmul(ps_o, sel_o[:, j, :], qs[j % 2], start=(j == 0), stop=(j == G - 1)).then_inc(s_o, 1)
                for j in range(G):
                    m = n * G + j
                    pe.wait_ge(s_vc, m + 1)
                    pe.matmul(ps_v, sel_v[:, j, :], act5[:, 2, :], start=True, stop=True).then_inc(s_vr, 1)
                    pe.wait_ge(s_kv, m + 1)
                    pe.matmul(ps_k, sel_k[:, j, :], act5[:, 1, :], start=True, stop=True).then_inc(s_kr, 1)
                    pe.wait_ge(s_st, m + 1)
                    pe.matmul(ps_f, sel_k[:, j, :], act5[:, 3, :], start=True, stop=True).then_inc(s_fr, 1)
                    if j:
                        out_group(j - 1)
                    pe.wait_ge(s_qs, m + 1)
                    pe.matmul(ps_q, sel_k[:, j, :], act5[:, 0, :], start=True, stop=True).then_inc(s_qr, 1)
                out_group(G - 1)
                pe.wait_ge(s_sq, n + 1)
                pe.matmul(ps_w, head_mean, sq, start=True, stop=True).then_inc(s_ms, 1)
                pe.wait_ge(s_on, n + 1)
                pe.matmul(ps_w, wo, on, start=True, stop=True).then_inc(s_wo, 1)

    def vector(dve):
        with dve.Fori(1, BATCH + 1) as b:
            for hf in range(HALVES):
                n = chunk(b, hf)
                for j in range(G):
                    m = n * G + j
                    dve.wait_ge(s_vc, m + 2)
                    dve.wait_ge(s_kr, m + 1)
                    dve.wait_ge(s_st, m + 1)
                    dve.tensor_tensor(kv, ps_k, vrow, ALU.mult).then_inc(s_kv, 1)
                    dve.wait_ge(s_kv, m + 2)
                    dve.wait_ge(s_fr, m + 1)
                    dve.wait_ge(s_qs, m + 1)
                    st = st1[j % 2] if hf else st0[:, j, :]
                    dve.tensor_tensor_scan(st, ps_f, kv, st0[:, j, CH - 1:CH] if hf else 0.0,
                                           ALU.mult, ALU.add).then_inc(s_st, 1)
                    dve.wait_ge(s_st, m + 2)
                    dve.wait_ge(s_qr, m + 1)
                    dve.wait_ge(s_o, m + 1)
                    dve.tensor_tensor(qs[j % 2], ps_q, st, ALU.mult).then_inc(s_qs, 1)
                dve.wait_ge(s_o, n * G + (G + 2))
                dve.tensor_tensor(og, ps_o, act5[:, 4, :], ALU.mult).then_inc(s_og, 1)
                dve.wait_ge(s_rs, n + 1)
                dve.scalar_tensor_tensor(on, og, nw, rs, ALU.mult, ALU.mult).then_inc(s_on, 1)
                dve.wait_ge(s_wo, n + 1)
                dve.tensor_tensor(c.Y[:, ds(n * CH, CH)], ps_w, c.X[:, ds(n * CH, CH)], ALU.add).then_inc(s_y, 1)
                dve.wait_ge(s_y, n + 1)

    def scalar(act):
        with act.Fori(1, BATCH + 1) as b:
            for hf in range(HALVES):
                n = chunk(b, hf)
                for piece, (dst, func) in enumerate([
                        (act5[:, 0, :], ACT.Silu), (act5[:, 1, :], ACT.Silu), (act5[:, 2, :], ACT.Copy),
                        (fg1[0:16, :], ACT.Copy), (act5[:, 3, :], ACT.Sigmoid), (act5[:, 4, :], ACT.Sigmoid)]):
                    act_wait(act, s_p, n * 6 + (piece + 1))
                    src = ps_p[piece % 2]
                    act.activation(dst, src[0:16, :] if piece == 3 else src, func).then_inc(s_pa, 1)
                for j in range(G):
                    m = n * G + j
                    act_wait(act, s_vr, m + 1)
                    act_wait(act, s_kv, m + 1)
                    act.activation(vrow, ps_v, ACT.Copy).then_inc(s_vc, 1)
                act_wait(act, s_og, n + 2)
                act.activation(sq, og, ACT.Square).then_inc(s_sq, 1)
                act_wait(act, s_ms, n + 1)
                act.activation(lv, ps_w, ACT.Ln, bias=c.eps5).then_inc(s_sd, 1)
                act_wait(act, s_sd, n + 1)
                act.activation(rs, lv, ACT.Exp, scale=-0.5).then_inc(s_rs, 1)

    return dict(sync=sync, tensor=tensor, vector=vector, scalar=scalar, done=(s_y, NCH))


def state_space_layer(c, d, layer):
    H, N, L, PD = 16, 64, 64, 8
    TPB = SEQ // P
    place = Places(c, c.norm_at)
    wcat = place(272)
    wB, wC = place(H * N), place(H * N)
    wout = place(P)
    bdt, nega = place(H), place(H)
    later = place(P)
    upto = place(P)
    since = place(L)
    hide = place(H * L)
    xt = place(P)
    dtb, dta, dte, dtl, dt, A = [place(H) for _ in range(6)]
    ze, zs = place(P), place(P)
    Xd = place(P)
    Xe = place(2, P)
    arow = place(H, L)
    BT, CT = place(H * N), place(H * N)
    Bk = place(H * N)
    eD = place(H * L)
    W = place(H * L)
    inch = place(2, P)
    tot = place(2, 8)
    sm = place(32)
    state = place(8, 2 * PD)
    stn = place(8, 2 * PD)
    yo, ys, yT = place(P), place(P), place(P)
    ps_c = c.bank[0][:, 0:272]
    ps_s = c.bank[0][:, 288:320]
    ps_tot = c.bank[0][:, 320:352].rearrange("p (c j o) -> p c j o", c=2, o=2)
    ps_BT = c.psum[:, 512:3 * 512]
    ps_CT = c.psum[:, 3 * 512:5 * 512]
    ps_Bk = c.psum[:, 5 * 512:7 * 512]
    ps_y = c.bank[7][:, 0:P]
    ps_off = c.bank[1][:, 0:P]
    ps_st = c.bank[5][:, 0:P].rearrange("p (c n) -> p c n", c=2)
    ps_T = c.bank[7][:, 2 * P:3 * P]
    ps_out = c.bank[7][:, 3 * P:4 * P]
    take = c.layer_sems(layer)
    S = lambda n: take("ssm_" + n)
    names = ("w", "al", "xt", "c", "dt", "A", "ar", "X", "BT", "CT", "Bk", "bc", "cc", "kc", "sm", "se", "D", "eD",
             "G", "W", "xe", "st", "S", "off", "yd", "y1", "tr", "tc", "o", "y", "z", "zero")
    (s_w, s_al, s_xt, s_c, s_dt, s_A, s_ar, s_X, s_BT, s_CT, s_Bk, s_bc, s_cc, s_kc, s_sm, s_se, s_D, s_eD,
     s_G, s_W, s_xe, s_st, s_S, s_off, s_yd, s_y1, s_tr, s_tc, s_o, s_y, s_z, s_zero) = [S(n) for n in names]
    loads = [(wcat, "W_cat"), (wB, "W_BT"), (wC, "W_CT"), (wout, "W_outT"), (bdt, "b_dt_rows"), (nega, "A_log_rows"),
             (later, "later"), (upto, "upto"), (since, "since"), (hide, "hide"), (inch, "inch")]

    def hv(v, k):
        return v.rearrange("p (h k) -> p h k", k=k)

    def sync(sp):
        sp.wait_ge(*x_ready(c, layer))
        for dst, name in loads:
            sp.dma_start(dst, d[name]).then_inc(s_w, 16)

    def tile(b, r):
        return b * TPB + (r - TPB)

    def vector(dve):
        dve.wait_ge(*x_ready(c, layer))
        dve.memset(Xe, 0.0).then_inc(s_zero, 1)
        dve.wait_ge(s_zero, 1)
        dve.wait_ge(s_al, 1)
        dve.tensor_scalar(nega, nega, -1.0, None, ALU.mult).then_inc(s_al, 1)
        dve.wait_ge(s_al, 2)
        def take_output(n):
            dve.wait_ge(s_o, n + 1)
            dve.tensor_tensor(c.Y[:, ds(n * P, P)], ps_out, c.X[:, ds(n * P, P)], ALU.add).then_inc(s_y, 1)

        def sequence(b, first, last):
            for r in range(TPB):
                n = tile(b, r)
                if r == 0:
                    dve.memset(state, 0.0).then_inc(s_zero, 1)
                dve.wait_ge(s_c, n + 1)
                dve.tensor_tensor(dtb, ps_c[:, 256:272], bdt, ALU.add).then_inc(s_dt, 1)
                dve.wait_ge(s_dt, n * 6 + 1)
                dve.tensor_scalar(dta, dtb, 0.0, None, ALU.max).then_inc(s_dt, 1)
                dve.wait_ge(s_dt, n * 6 + 5)
                dve.tensor_tensor(dt, dta, dtl, ALU.add).then_inc(s_dt, 1)
                dve.wait_ge(s_dt, n * 6 + 6)
                dve.tensor_tensor(A, dt, nega, ALU.mult).then_inc(s_A, 1)
                dve.tensor_tensor(hv(Xd, PD), hv(ps_c[:, 0:P], PD), dt.unsqueeze(2).to_broadcast([P, H, PD]),
                                  ALU.mult).then_inc(s_X, 1)
                if not (first and r == 0):
                    take_output(n - 1)
                dve.wait_ge(s_X, n + 1)
                dve.wait_ge(s_se, n * 3 + 3)
                for ch in range(2):
                    rows = slice(64 * ch, 64 * ch + 64)
                    dve.tensor_tensor(hv(Xe[rows, ch, :], PD), hv(Xd[rows], PD),
                                      sm[rows, 16:32].unsqueeze(2).to_broadcast([L, H, PD]), ALU.mult).then_inc(s_xe, 1)
                dve.wait_ge(s_G, n + 1)
                dve.wait_ge(s_eD, n * 2 + 2)
                dve.tensor_tensor(W, ps_CT, eD, ALU.mult).then_inc(s_W, 1)
                for ch in range(2):
                    dve.wait_ge(s_st, n + 1)
                    if ch == 0:
                        dve.wait_ge(s_off, n * 2 + 1)
                    else:
                        dve.wait_ge(s_off, n * 2 + 2)
                    dve.tensor_tensor(stn, state, tot[:, ch, :].unsqueeze(2).to_broadcast([P, 8, 2 * PD]),
                                      ALU.mult).then_inc(s_S, 1)
                    dve.wait_ge(s_S, n * 6 + (3 * ch + 1))
                    for odd in range(2):
                        own = (slice(64 * odd, 64 * odd + 64), slice(0, 8), slice(odd * PD, odd * PD + PD))
                        dve.tensor_tensor(state[own], stn[own], hv(ps_st[64 * odd:64 * odd + 64, ch, :], PD),
                                          ALU.add).then_inc(s_S, 1)
                    dve.wait_ge(s_S, n * 6 + (3 * ch + 3))
                if not (last and r == TPB - 1):
                    dve.wait_ge(s_Bk, n * 2 + 2)
                    dve.tensor_copy(xt, c.X[:, ds(n * P + P, P)]).then_inc(s_xt, 1)
                dve.wait_ge(s_z, n * 4 + 3)
                dve.tensor_tensor(zs, ps_c[:, P:2 * P], ze, ALU.mult).then_inc(s_z, 1)
                dve.wait_ge(s_yd, n + 1)
                dve.tensor_tensor(hv(yo, PD), hv(ps_off, PD), sm[:, 0:16].unsqueeze(2).to_broadcast([P, H, PD]),
                                  ALU.mult).then_inc(s_y1, 1)
                dve.wait_ge(s_y1, n * 3 + 1)
                dve.tensor_tensor(yo, yo, ps_y, ALU.add).then_inc(s_y1, 1)
                dve.wait_ge(s_y1, n * 3 + 2)
                dve.wait_ge(s_z, n * 4 + 4)
                dve.tensor_tensor(ys, yo, zs, ALU.mult).then_inc(s_y1, 1)
        dve.tensor_copy(xt, c.X[:, 0:P]).then_inc(s_xt, 1)
        sequence(1, True, False)
        with dve.Fori(2, BATCH) as b:
            sequence(b, False, False)
        sequence(BATCH, False, True)
        take_output(T // P - 1)

    def gpsimd(pool):
        with pool.Fori(1, T // P + 1) as i:
            pool.wait_ge(s_A, i)
            pool.wait_ge(s_w, 16 * len(loads))
            for odd in range(2):
                pool.tensor_tensor(arow[:, 8 * odd:8 * odd + 8, :], A[:, odd::2].unsqueeze(2).to_broadcast([P, 8, L]),
                                   since.unsqueeze(1).to_broadcast([P, 8, L]), ALU.mult).then_inc(s_ar, 1)

    def scalar(act):
        act.wait_ge(s_w, 16 * len(loads))
        act.preload_act_table_set(LN_EXP)
        act.activation(nega, nega, ACT.Exp).then_inc(s_al, 1)
        def take_transposed(i):
            act_wait(act, s_tr, i)
            act.activation(yT, ps_T, ACT.Copy).then_inc(s_tc, 1)

        def tile_of(i, first):
            act_wait(act, s_dt, i * 6 - 5)
            act.activation(dte, dtb, ACT.Abs).then_inc(s_dt, 1)
            act_wait(act, s_dt, i * 6 - 3)
            act.activation(dte, dte, ACT.Exp, scale=-1.0).then_inc(s_dt, 1)
            act_wait(act, s_dt, i * 6 - 2)
            act.activation(dtl, dte, ACT.Ln, bias=1.0).then_inc(s_dt, 1)
            if not first:
                take_transposed(i - 1)
            for half in range(2):
                act_wait(act, s_BT, i * 2 + (half - 1))
                act.activation(BT[:, half * 512:half * 512 + 512], ps_BT[:, half * 512:half * 512 + 512],
                               ACT.Copy).then_inc(s_bc, 1)
            for half in range(2):
                act_wait(act, s_CT, i * 2 + (half - 1))
                act.activation(CT[:, half * 512:half * 512 + 512], ps_CT[:, half * 512:half * 512 + 512],
                               ACT.Copy).then_inc(s_cc, 1)
            act_wait(act, s_sm, i)
            act.activation(sm, ps_s, ACT.Exp).then_inc(s_se, 1)
            for odd in range(2):
                half_p = slice(64 * odd, 64 * odd + 64)
                act.activation(tot[half_p, :, :], ps_tot[half_p, :, :, odd], ACT.Exp).then_inc(s_se, 1)
            for half in range(2):
                act_wait(act, s_Bk, i * 2 + (half - 1))
                act.activation(Bk[:, half * 512:half * 512 + 512], ps_Bk[:, half * 512:half * 512 + 512],
                               ACT.Copy).then_inc(s_kc, 1)
            for half in range(2):
                act_wait(act, s_D, i * 2 + (half - 1))
                act.activation(eD[:, half * 512:half * 512 + 512], ps_BT[:, half * 512:half * 512 + 512],
                               ACT.Exp).then_inc(s_eD, 1)
            act.activation(ze, ps_c[:, P:2 * P], ACT.Exp, scale=-1.0).then_inc(s_z, 1)
            act_wait(act, s_z, i * 4 - 3)
            act.activation(ze, ze, ACT.Ln, bias=1.0).then_inc(s_z, 1)
            act_wait(act, s_z, i * 4 - 2)
            act.activation(ze, ze, ACT.Exp, scale=-1.0).then_inc(s_z, 1)
        tile_of(1, True)
        with act.Fori(2, T // P + 1) as i:
            tile_of(i, False)
        take_transposed(T // P)

    def tensor(pe):
        pe.wait_ge(s_w, 16 * len(loads))

        def projections(i):
            pe_wait(pe, s_xt, i)
            pe.matmul(ps_c, xt, wcat, start=True, stop=True).then_inc(s_c, 1)
            for dst, wgt, s in ((ps_BT, wB, s_BT), (ps_CT, wC, s_CT)):
                for half in range(2):
                    for j in range(half * 4, half * 4 + 4):
                        mm = pe.matmul(dst[:, j * P:j * P + P], wgt[:, j * P:j * P + P], xt, start=True, stop=True)
                    mm.then_inc(s, 1)
            for half in range(2):
                pe.matmul(ps_Bk[:, half * 512:half * 512 + 512], xt, wB[:, half * 512:half * 512 + 512],
                          start=True, stop=True).then_inc(s_Bk, 1)

        def scan(i):
            pe_wait(pe, s_A, i)
            pe_wait(pe, s_X, i)
            pe.matmul(ps_s[:, 0:16], upto, A, start=True, stop=True)
            pe.matmul(ps_s[:, 16:32], later, A, start=True, stop=True)
            for ch in range(2):
                mm = pe.matmul(c.bank[0][:, 320 + 16 * ch:336 + 16 * ch], inch[:, ch, :], A, start=True, stop=True)
            mm.then_inc(s_sm, 1)
            pe_wait(pe, s_ar, i * 2)
            pe_wait(pe, s_bc, i * 2)
            for half in range(2):
                pe.matmul(ps_BT[:, half * 512:half * 512 + 512], later,
                          arow.rearrange("p h l -> p (h l)")[:, half * 512:half * 512 + 512], start=True, stop=False)
                pe.matmul(ps_BT[:, half * 512:half * 512 + 512], c.ident, hide[:, half * 512:half * 512 + 512],
                          start=False, stop=True).then_inc(s_D, 1)
            pe_wait(pe, s_cc, i * 2)
            for h in range(H):
                rows = slice(64 * (h % 2), 64 * (h % 2) + 64)
                for ch in range(2):
                    at = (h // 2) * P + ch * L
                    g = (h % 2) * 8 + h // 2
                    mm = pe.matmul(ps_CT[64 * ch:64 * ch + 64, g * L:g * L + L], BT[rows, at:at + L],
                                   CT[rows, at:at + L], start=True, stop=True)
            mm.then_inc(s_G, 1)
            pe_wait(pe, s_xe, i * 2)
            pe_wait(pe, s_kc, i * 2)
            for h in range(H):
                mm = pe.matmul(ps_st[64 * (h % 2):64 * (h % 2) + 64, :, (h // 2) * PD:(h // 2) * PD + PD],
                               Bk[:, h * N:h * N + N], Xe[:, :, h * PD:h * PD + PD], start=True, stop=True)
            mm.then_inc(s_st, 1)
            pe_wait(pe, s_eD, i * 2)
            for ch in range(2):
                if ch:
                    pe_wait(pe, s_S, i * 6 - 3)
                for j in range(H // 2):
                    mm = pe.matmul(ps_off[64 * ch:64 * ch + 64, j * 2 * PD:(j + 1) * 2 * PD],
                                   CT[:, j * P + ch * L:j * P + ch * L + L], state[:, j, :], start=True, stop=True)
                mm.then_inc(s_off, 1)
            pe_wait(pe, s_W, i)
            for ch in range(2):
                rows = slice(64 * ch, 64 * ch + 64)
                for h in range(H):
                    g = (h % 2) * 8 + h // 2
                    mm = pe.matmul(ps_y[64 * ch:64 * ch + 64, h * PD:h * PD + PD], W[rows, g * L:g * L + L],
                                   Xd[rows, h * PD:h * PD + PD], start=True, stop=True)
            mm.then_inc(s_yd, 1)

        def output(i):
            pe_wait(pe, s_y1, i * 3)
            pe.transpose(ps_T, ys, c.ident).then_inc(s_tr, 1)
            pe_wait(pe, s_tc, i)
            pe.matmul(ps_out, wout, yT, start=True, stop=True).then_inc(s_o, 1)

        projections(1)
        with pe.Fori(1, T // P) as i:
            scan(i)
            pe_wait(pe, s_y1, i * 3 - 2)
            projections(i + 1)
            output(i)
        scan(T // P)
        output(T // P)

    return dict(sync=sync, tensor=tensor, vector=vector, scalar=scalar, gpsimd=gpsimd, done=(s_y, T // P))


def kron_experts_layer(c, d, layer):
    E, R, F = 64, 32, 64
    NS = T // 8
    NT = NS // P
    GS = 4
    PAIRS = P // GS // 2
    place = Places(c, c.free_at)
    upB, upA = place(E, F), place(E, F)
    dnB, dnA = place(E, R), place(E, R)
    wup = place(8, E)
    wdn = place(F, E)
    bup, bdn = place(F), place(R)
    sup, sdn = place(1), place(1)
    xs = place(P * R + 2 * P)
    Hid = place(P + 2 * GS, F)
    yd = place(P, R)
    lg = place(E)
    top = place(8)
    topi = place(8).bitcast(U32)
    prob = place(4)
    pk = place(2)
    dgp = place(2, P)
    pb = place(2, P)
    row = place(2 * P).bitcast(U32)
    grp = [place(P) for _ in range(2)]
    hgrp = [place(GS, F) for _ in range(2)]
    tk_ = [place(2, GS, F) for _ in range(2)]
    hb = [place(GS, F) for _ in range(2)]
    tdn = [place(2, GS, R) for _ in range(2)]
    scratch = c.nc.dram_tensor("expert_numbers", (2 * NT, 2 * P), U32, kind="Internal").ap()
    ps_l = c.bank[6][:, 0:E]
    ps_b = c.bank[7][:, 0:2 * P]
    ps_1 = c.bank[0:2]
    ps_2 = c.bank[2:4]
    take = c.layer_sems(layer)
    S = lambda n: take("kron_" + n)
    names = ("w", "xs", "l", "lg", "top", "ti", "pr", "ex", "dg", "b", "pb", "out", "row", "g", "m1", "t", "m2", "h", "a",
             "hg", "d1", "td", "d2", "yd", "y", "yb", "hz")
    (s_w, s_xs, s_l, s_lg, s_top, s_ti, s_pr, s_ex, s_dg, s_b, s_pb, s_out, s_row, s_g, s_m1, s_t, s_m2, s_h, s_a,
     s_hg, s_d1, s_td, s_d2, s_yd, s_y, s_yb, s_hz) = [S(n) for n in names]
    loads = [(upB[0:R], "up_B"), (upA[0:R], "up_A"), (dnB[0:F], "dn_B"), (dnA[0:F], "dn_A"), (wup, "W_up"),
             (wdn[0:F], "W_down"), (bup[0:F, :], "bias_up"), (bdn[0:R, :], "bias_down"), (sup, "scale_up"),
             (sdn, "scale_down")]

    def group(t, i, u):
        return i * 2 + (t * 2 * PAIRS + u - 2)

    def sync(sp):
        sp.wait_ge(*x_ready(c, layer))
        for dst, name in loads:
            sp.dma_start(dst, d[name]).then_inc(s_w, 16)
        for q in range(2 * NT):
            sp.wait_ge(s_ti, q + 1)
            sp.dma_start(scratch[q:q + 1, :].rearrange("a (n k) -> (a n) k", k=2), topi[:, 0:2]).then_inc(s_out, 16)
            sp.wait_ge(s_out, 16 * (q + 1))
            sp.dma_start(row[0:1, :], scratch[q:q + 1, :]).then_inc(s_row, 16)

    def vector(dve):
        dve.wait_ge(*x_ready(c, layer))
        dve.memset(xs[0:R, P * R:P * R + 2 * P], 0.0).then_inc(s_xs, 1)
        dve.memset(Hid[0:F, P:P + 2 * GS, :], 0.0).then_inc(s_hz, 1)
        for u in range(2):
            dve.memset(grp[u][R:2 * R, :], 0.0).then_inc(s_hz, 1)
            dve.memset(grp[u][2 * R:P, :], 0.0).then_inc(s_hz, 1)
            dve.memset(tk_[u][R:2 * R], 0.0).then_inc(s_hz, 1)
            dve.memset(tk_[u][2 * R:P], 0.0).then_inc(s_hz, 1)
            dve.memset(hgrp[u][F:P], 0.0).then_inc(s_hz, 1)
            dve.memset(tdn[u][F:P], 0.0).then_inc(s_hz, 1)
        for table, rows in ((upB, R), (upA, R), (dnB, F), (dnA, F)):
            for at in range(rows, P, 2 * R if rows == F else R):
                dve.memset(table[at:at + (2 * R if rows == F else R)], 0.0).then_inc(s_hz, 1)
        dve.wait_ge(s_w, 16 * len(loads))

        def choose(q):
            dve.wait_ge(s_l, q + 1)
            dve.tensor_copy(lg, ps_l).then_inc(s_lg, 1)
            dve.wait_ge(s_lg, q + 1)
            dve.max(top, lg).then_inc(s_top, 1)
            dve.wait_ge(s_top, q + 1)
            if q:
                dve.wait_ge(s_out, 16 * q)
            dve.max_index(topi, top, lg).then_inc(s_ti, 1)
            dve.tensor_tensor(prob[:, 0:1], top[:, 1:2], top[:, 0:1], ALU.subtract).then_inc(s_pr, 1)
            dve.wait_ge(s_ex, q + 1)
            dve.tensor_scalar(prob[:, 2:3], prob[:, 1:2], 1.0, None, ALU.add).then_inc(s_pr, 1)
            dve.wait_ge(s_pr, 4 * q + 2)
            dve.reciprocal(pk[:, 0:1], prob[:, 2:3]).then_inc(s_pr, 1)
            dve.wait_ge(s_pr, 4 * q + 3)
            dve.tensor_tensor(pk[:, 1:2], prob[:, 1:2], pk[:, 0:1], ALU.mult).then_inc(s_pr, 1)
            dve.wait_ge(s_pr, 4 * q + 4)
            for k in range(2):
                dve.tensor_scalar(dgp[:, k, :], c.ident, pk[:, k:k + 1], None, ALU.mult).then_inc(s_dg, 1)
            dve.wait_ge(s_b, q + 1)
            dve.tensor_copy(pb.rearrange("p k n -> p (k n)"), ps_b).then_inc(s_pb, 1)
            dve.wait_ge(s_pb, q + 1)

        for t in range(NT):
            for dd in range(4):
                dve.tensor_copy(xs[0:R, 0:P * R].rearrange("p (n q) -> p n q", q=4)[:, :, dd],
                                c.X[32 * dd:32 * dd + 32, t * 8 * P:(t + 1) * 8 * P]).then_inc(s_xs, 1)
            choose(2 * t)
            with dve.Fori(1, PAIRS + 1) as i:
                for u in range(2):
                    dve.wait_ge(s_m1, group(t, i, u) + 1)
                    for k in range(2):
                        dve.tensor_tensor(tk_[u][0:R, k, :, :], ps_1[u][0:R, k * GS * F:(k + 1) * GS * F].rearrange(
                            "p (s f) -> p s f", s=GS),
                            pb[0:R, k, ds(i * (2 * GS) + (u - 2) * GS, GS)].unsqueeze(2).to_broadcast([R, GS, F]),
                            ALU.mult).then_inc(s_t, 1)
                for u in range(2):
                    dve.wait_ge(s_m2, group(t, i, u) + 1)
                    dve.wait_ge(s_a, group(t, i, u) + 1)
                    dve.scalar_tensor_tensor(hb[u][0:F], ps_2[u][0:F, 0:GS * F].rearrange("p (s f) -> p s f", s=GS),
                                             sup[0:F, :], bup[0:F, :].unsqueeze(1).to_broadcast([F, GS, F]),
                                             ALU.mult, ALU.add).then_inc(s_h, 1)
            choose(2 * t + 1)
            with dve.Fori(1, PAIRS + 1) as i:
                for u in range(2):
                    dve.wait_ge(s_d1, group(t, i, u) + 1)
                    for k in range(2):
                        dve.tensor_tensor(tdn[u][0:F, k, :, :], ps_1[u][0:F, k * GS * R:(k + 1) * GS * R].rearrange(
                            "p (s f) -> p s f", s=GS),
                            pb[0:F, k, ds(i * (2 * GS) + (u - 2) * GS, GS)].unsqueeze(2).to_broadcast([F, GS, R]),
                            ALU.mult).then_inc(s_td, 1)
                for u in range(2):
                    dve.wait_ge(s_d2, group(t, i, u) + 1)
                    dve.tensor_copy(yd[0:R, ds(i * (2 * GS) + (u - 2) * GS, GS), :],
                                    ps_2[u][0:R, 0:GS * R].rearrange("p (s f) -> p s f", s=GS)).then_inc(s_yd, 1)
            dve.wait_ge(s_yd, 2 * PAIRS * (t + 1))
            dve.scalar_tensor_tensor(yd[0:R], yd[0:R], sdn[0:R, :], bdn[0:R, :].unsqueeze(1).to_broadcast([R, P, R]),
                                     ALU.mult, ALU.add).then_inc(s_yb, 1)
            dve.wait_ge(s_yb, t + 1)
            for dd in range(4):
                dve.tensor_copy(c.Y[32 * dd:32 * dd + 32, t * 8 * P:(t + 1) * 8 * P],
                                yd[0:R].rearrange("p n (k q) -> p (n k) q", q=4)[:, :, dd]).then_inc(s_y, 1)
            dve.wait_ge(s_y, 4 * (t + 1))
        dve.tensor_tensor(c.Y, c.Y, c.X, ALU.add).then_inc(s_y, 1)

    def scalar(act):
        act.wait_ge(s_hz, 21)
        act.sem_inc(s_a, 2)

        def exp_difference(q):
            act.wait_ge(s_pr, 4 * q + 1)
            act.activation(prob[:, 1:2], prob[:, 0:1], ACT.Exp).then_inc(s_ex, 1)
        for t in range(NT):
            act.wait_ge(s_xs, 4 * t + 5)
            for u in range(2):
                act.activation(grp[u][0:R, :], xs[0:R, u * P:u * P + P], ACT.Copy).then_inc(s_g, 1)
            exp_difference(2 * t)
            with act.Fori(1, PAIRS + 1) as i:
                for u in range(2):
                    act_wait(act, s_m1, group(t, i, u) + 1)
                    act.activation(grp[u][0:R, :], xs[0:R, ds(i * (2 * P) + u * P, P)],
                                   ACT.Copy).then_inc(s_g, 1)
                for u in range(2):
                    act_wait(act, s_h, group(t, i, u) + 1)
                    act.activation(Hid[0:F, ds(i * (2 * GS) + (u - 2) * GS, GS), :], hb[u][0:F], ACT.Gelu).then_inc(s_a, 1)
            act.wait_ge(s_a, 2 + 2 * PAIRS * (t + 1))
            exp_difference(2 * t + 1)
            for u in range(2):
                act.activation(hgrp[u][0:F], Hid[0:F, u * GS:u * GS + GS, :], ACT.Copy).then_inc(s_hg, 1)
            with act.Fori(1, PAIRS + 1) as i:
                for u in range(2):
                    act_wait(act, s_d1, group(t, i, u) + 1)
                    act.activation(hgrp[u][0:F], Hid[0:F, ds(i * (2 * GS) + u * GS, GS), :], ACT.Copy).then_inc(s_hg, 1)
            act.wait_ge(s_hg, (2 * PAIRS + 2) * (t + 1))

    def tensor(pe):
        pe.wait_ge(*x_ready(c, layer))
        pe.wait_ge(s_w, 16 * len(loads))
        pe.wait_ge(s_hz, 21)

        def spread(q):
            pe.wait_ge(s_dg, 2 * q + 2)
            pe.matmul(ps_b, c.ones, dgp.rearrange("p k n -> p (k n)"), start=True, stop=True).then_inc(s_b, 1)
            pe.wait_ge(s_pb, q + 1)
            pe.wait_ge(s_row, 16 * (q + 1))

        def numbers(i):
            _, values = c.nc.values_load_multi_w_load_instructions(
                row[0:1, ds(i * (4 * GS) - 4 * GS, 4 * GS)], engines=(mybir.EngineType.PE,), min_val=0, max_val=E - 1,
                skip_runtime_bounds_check_because="max_index over the experts' logits gives 0 to 63")
            return values

        for t in range(NT):
            for k in range(8):
                mm = pe.matmul(ps_l, c.X[:, t * 8 * P + k:(t + 1) * 8 * P:8], wup[:, k, :], start=(k == 0), stop=(k == 7))
            mm.then_inc(s_l, 1)
            spread(2 * t)
            with pe.Fori(1, PAIRS + 1) as i:
                e = numbers(i)
                for u in range(2):
                    pe.wait_ge(s_g, i * 2 + (u - 1 + t * (2 * PAIRS + 2)))
                    for n in range(2 * GS):
                        s, k = n // 2, n % 2
                        mm = pe.matmul(ps_1[u][0:R, (k * GS + s) * F:(k * GS + s + 1) * F], grp[u][:, s * R:(s + 1) * R],
                                       upB.rearrange("p e f -> p (e f)")[:, ds(e[2 * GS * u + n] * F, F)],
                                       start=True, stop=True)
                    mm.then_inc(s_m1, 1)
                for u in range(2):
                    pe.wait_ge(s_t, group(t, i, u) * 2 + 2)
                    for n in range(2 * GS):
                        s, k = n // 2, n % 2
                        mm = pe.matmul(ps_2[u][0:F, s * F:(s + 1) * F], tk_[u][:, k, s, :],
                                       upA.rearrange("p e f -> p (e f)")[:, ds(e[2 * GS * u + n] * F, F)],
                                       start=(k == 0), stop=(k == 1))
                    mm.then_inc(s_m2, 1)
            pe.wait_ge(s_a, 2 + 2 * PAIRS * (t + 1))
            for o in range(F):
                mm = pe.matmul(ps_l, Hid[0:F, 0:P, o], wdn[0:F, o, :], start=(o == 0), stop=(o == F - 1))
            mm.then_inc(s_l, 1)
            spread(2 * t + 1)
            with pe.Fori(1, PAIRS + 1) as i:
                e = numbers(i)
                for u in range(2):
                    pe.wait_ge(s_hg, i * 2 + (u - 1 + t * (2 * PAIRS + 2)))
                    for n in range(2 * GS):
                        s, k = n // 2, n % 2
                        mm = pe.matmul(ps_1[u][0:F, (k * GS + s) * R:(k * GS + s + 1) * R], hgrp[u][:, s, :],
                                       dnB.rearrange("p e f -> p (e f)")[:, ds(e[2 * GS * u + n] * R, R)],
                                       start=True, stop=True)
                    mm.then_inc(s_d1, 1)
                for u in range(2):
                    pe.wait_ge(s_td, group(t, i, u) * 2 + 2)
                    for n in range(2 * GS):
                        s, k = n // 2, n % 2
                        mm = pe.matmul(ps_2[u][0:R, s * R:(s + 1) * R], tdn[u][:, k, s, :],
                                       dnA.rearrange("p e f -> p (e f)")[:, ds(e[2 * GS * u + n] * R, R)],
                                       start=(k == 0), stop=(k == 1))
                    mm.then_inc(s_d2, 1)
            pe.wait_ge(s_yd, 2 * PAIRS * (t + 1))

    return dict(sync=sync, tensor=tensor, vector=vector, scalar=scalar, done=(s_y, 4 * NT + 1))


def layouts(np, a):
    def cols(v):
        return np.asarray(v).reshape(-1, P).T
    out = {"xT": np.asarray(a["L0_attn_data"]).reshape(T, P).T}
    out["L0_attn_W2"] = np.asarray(a["L0_attn_W2"])
    out["W1_rows"] = np.repeat(np.asarray(a["L0_attn_W1"]).reshape(1, P), P, axis=0)
    out["L0_attn_b1"] = cols(a["L0_attn_b1"])
    out["L0_ffn_w1"], out["L0_ffn_w2"] = np.asarray(a["L0_ffn_w1"]), np.asarray(a["L0_ffn_w2"])
    out["L0_ffn_b1"], out["L0_ffn_b2"] = cols(a["L0_ffn_b1"]), cols(a["L0_ffn_b2"])
    out["L1_ffn_W_fc"], out["L1_ffn_W_proj"] = np.asarray(a["L1_ffn_W_fc"]), np.asarray(a["L1_ffn_W_proj"])
    out["L1_ffn_ln_w"], out["L1_ffn_ln_b"] = cols(a["L1_ffn_ln_w"]), cols(a["L1_ffn_ln_b"])
    out["L2_ffn_W1"], out["L2_ffn_W2"] = np.asarray(a["L2_ffn_W1"]), np.asarray(a["L2_ffn_W2"])
    out["L2_ffn_b1"], out["L2_ffn_b2"] = cols(a["L2_ffn_b1"]), cols(a["L2_ffn_b2"])
    out["L2_ffn_Wu"] = np.asarray(a["L2_ffn_Wu"])
    out["L2_ffn_bu"] = np.repeat(np.asarray(a["L2_ffn_bu"]).reshape(1, 1), P, axis=0)
    for n in "kqv":
        out["L1_attn_W" + n] = np.asarray(a["L1_attn_W" + n])
        out["L1_attn_b" + n] = np.asarray(a["L1_attn_b" + n]).reshape(1, -1)
    out["L1_attn_Wo"], out["L1_attn_bo"] = np.asarray(a["L1_attn_Wo"]), cols(a["L1_attn_bo"])
    for n in "qkvo":
        out["L2_attn_W" + n] = np.asarray(a["L2_attn_W" + n])
    out["Wfg1"] = np.concatenate([np.asarray(a["L2_attn_Wf1"]), np.asarray(a["L2_attn_Wg1"]),
                                   np.zeros((P, P - 16), np.float32)], axis=1)
    none = np.zeros((8, P), np.float32)
    out["Wf2_0"] = np.concatenate([np.asarray(a["L2_attn_Wf2"]), none])
    out["Wg2_0"] = np.concatenate([none, np.asarray(a["L2_attn_Wg2"])])
    out["L2_attn_norm_weight"] = cols(a["L2_attn_norm_weight"])
    feature = np.arange(P).reshape(P, 1, 1)
    group, row = np.arange(8).reshape(1, 8, 1), np.arange(P).reshape(1, 1, P)
    head = 2 * group + row // 64
    by_key = (feature == 8 * head + row // 8 % 8).astype(np.float32)
    by_value = (feature == 8 * head + row % 8).astype(np.float32)
    out["sel_k"], out["sel_v"] = by_key, by_value
    out["sel_o"] = np.transpose(by_value, (2, 1, 0)) * np.float32(8 ** -0.5)
    f = np.arange(P)
    out["head_mean"] = (f[:, None] // 8 == f[None, :] // 8).astype(np.float32) / np.float32(8)
    out["W_cat"] = np.concatenate([np.asarray(a["L3_attn_W_in"]).T, np.asarray(a["L3_attn_W_dt"]).T], axis=1)
    out["W_BT"], out["W_CT"] = np.asarray(a["L3_attn_W_B"]).T, np.asarray(a["L3_attn_W_C"]).T
    out["W_outT"] = np.asarray(a["L3_attn_W_out"]).T
    out["b_dt_rows"] = np.repeat(np.asarray(a["L3_attn_b_dt"]).reshape(1, -1), P, axis=0)
    out["A_log_rows"] = np.repeat(np.asarray(a["L3_attn_A_log"]).reshape(1, -1), P, axis=0)
    same = f[:, None] // 64 == f[None, :] // 64
    out["later"] = (same & (f[:, None] > f[None, :])).astype(np.float32)
    out["upto"] = (same & (f[:, None] <= f[None, :])).astype(np.float32)
    out["inch"] = (f[:, None, None] // 64 == np.arange(2)[None, :, None]).repeat(P, axis=2).astype(np.float32)
    l = np.arange(64)
    out["since"] = (l[None, :] >= f[:, None] % 64).astype(np.float32)
    out["hide"] = np.where(np.tile(l, 16)[None, :] < f[:, None] % 64, -BIG, 0.0).astype(np.float32)
    for which, name in (("up", "up"), ("dn", "down")):
        for m in "AB":
            out[which + "_" + m] = np.asarray(a[f"L3_ffn_{m}_{name}"]).transpose(2, 0, 1)
    out["W_up"] = np.asarray(a["L3_ffn_W_up"]).reshape(64, 8, P).transpose(2, 1, 0)
    out["W_down"] = np.asarray(a["L3_ffn_W_down"]).reshape(64, 64, 64).transpose(2, 1, 0)
    out["bias_up"] = np.asarray(a["L3_ffn_bias_up"]).reshape(64, 64).T
    out["bias_down"] = np.asarray(a["L3_ffn_bias_down"]).reshape(32, 32).T
    for name in ("scale_up", "scale_down"):
        out[name] = np.repeat(np.asarray(a["L3_ffn_" + name]).reshape(1, 1), P, axis=0)
    return out


def build(nc, d, out, layers, start=0):
    with ExitStack() as ctx:
        c = Core(nc, ctx)
        plan = [make(c, d, n) for n, make in enumerate(layers)]

        def y_done(layer):
            return plan[layer]["done"]

        def y_of(layer):
            return plan[layer].get("result", c.Y)
        ln_tensor, ln_vector, ln_scalar = layer_norm(c, y_done, y_of)
        block = ctx.enter_context(nc.Block())

        @block.sync
        def _(sp):
            sp.dma_start(c.X, d["xT"]).then_inc(c.s_xload, 16)
            for layer, part in enumerate(plan):
                if layer == HALF:
                    c.half_way(sp)
                if "sync" in part:
                    part["sync"](sp)
            sp.wait_ge(*x_ready(c, len(plan)))
            sp.dma_start(out, c.X).then_inc(c.s_out, 16)
            sp.wait_ge(c.s_out, 16)

        @block.gpsimd
        def _(pool):
            pool.memset(c.ident, 0.0).then_inc(c.s_const, 1)
            pool.wait_ge(c.s_const, 1)
            pool.affine_select(out=c.ident, in_=c.ident, compare_op=ALU.not_equal, fill=1.0, base=0,
                               pattern=[[-1, P]], channel_multiplier=1).then_inc(c.s_ident, 1)
            for layer, part in enumerate(plan):
                if layer == HALF:
                    c.half_way(pool, clears=True)
                if "gpsimd" in part:
                    part["gpsimd"](pool)

        @block.vector
        def _(dve):
            dve.memset(c.ones, 1.0).then_inc(c.s_ones, 1)
            dve.memset(c.mean, 1.0 / P).then_inc(c.s_ones, 1)
            dve.memset(c.eps5, 1e-5).then_inc(c.s_ones, 1)
            dve.wait_ge(c.s_ident, 1)
            dve.wait_ge(c.s_ones, 3)
            for layer, part in enumerate(plan):
                if layer == HALF:
                    c.half_way(dve)
                part["vector"](dve)
                ln_vector(dve, layer)

        @block.scalar
        def _(act):
            act.wait_ge(c.s_ones, 3)
            for layer, part in enumerate(plan):
                if layer == HALF:
                    c.half_way(act)
                part["scalar"](act)
                ln_scalar(act, layer)

        @block.tensor
        def _(pe):
            pe.wait_ge(c.s_ones, 3)
            pe.wait_ge(c.s_ident, 1)
            for layer, part in enumerate(plan):
                if layer == HALF:
                    c.half_way(pe)
                part["tensor"](pe)
                ln_tensor(pe, layer)


LAYERS = [similarity_layer, binary_ffn_layer, outer_attention_layer, ternary_ffn_layer,
          linear_attention_layer, expert_ffn_layer, state_space_layer, kron_experts_layer]


def kernel(**inputs):
    import numpy as np
    import concourse.bacc as _bacc
    from concourse.bass_utils import run_bass_kernel_spmd as _run

    nc = _bacc.Bacc("TRN2", target_bir_lowering=False, num_devices=1)
    lay = layouts(np, inputs)
    arrays, d = {}, {}
    for name, a in lay.items():
        a = np.ascontiguousarray(a)
        arrays[name] = a
        d[name] = nc.dram_tensor(name, a.shape, mybir.dt.from_np(a.dtype), kind="ExternalInput").ap()
    out = nc.dram_tensor("out_xT", (P, T), F32, kind="ExternalOutput").ap()
    build(nc, d, out, LAYERS)
    r = _run(nc, [arrays], core_ids=[0])
    return np.ascontiguousarray(r.results[0]["out_xT"].T).reshape(BATCH, SEQ, P)
```
